# Optimizing a Trainium2 kernel written in Bass

```python
import numpy as np
import jax
import jax.numpy as jnp

def _softmax(x, axis=-1):
    return jax.nn.softmax(x, axis=axis)

def _gelu(x):
    return jax.nn.gelu(x, approximate=True)

def _silu(x):
    return jax.nn.silu(x)

def _sigmoid(x):
    return jax.nn.sigmoid(x)

def _layernorm(x, axis=-1, eps=1e-05):
    m = jnp.mean(x, axis=axis, keepdims=True)
    v = jnp.var(x, axis=axis, keepdims=True)
    return (x - m) / jnp.sqrt(v + eps)

def _scatter_add(tgt, idx, src, axis=0):
    return tgt.at[idx].add(src)

def _segment_sum(src, seg, n):
    return jax.ops.segment_sum(src, seg, n)
kernel_name = 'mk_adaln_d2_jaxref_r8_1db97b'

def setup_inputs(seed: int=0):
    np.random.seed(seed)
    _w = jnp.asarray

    def _L0_attn_setup():
        import jax, jax.numpy as jnp
        import numpy as np
        B, L, D, N = (2, 256, 128, 16)
        H = D // N
        THETA = 10000.0

        def apply_rope(x):
            l, h = (x.shape[-2], x.shape[-1])
            freqs = THETA ** (-jnp.arange(0, h, 2, dtype=jnp.float32) / h)
            ang = jnp.arange(l, dtype=jnp.float32)[:, None] * freqs
            cos, sin = (jnp.cos(ang), jnp.sin(ang))
            x_even = x[..., 0::2]
            x_odd = x[..., 1::2]
            out_even = cos * x_even - sin * x_odd
            out_odd = sin * x_even + cos * x_odd
            return jnp.stack((out_even, out_odd), axis=-1).reshape(x.shape)
        key = jax.random.key(seed)
        ks = jax.random.split(key, 9)
        s = 0.02
        return {'x': jax.random.normal(ks[0], (B, L, D), dtype=jnp.float32), 'Wq': jax.random.normal(ks[1], (D, D), dtype=jnp.float32) * s, 'bq': jax.random.normal(ks[2], (D,), dtype=jnp.float32) * s, 'Wk': jax.random.normal(ks[3], (D, D), dtype=jnp.float32) * s, 'bk': jax.random.normal(ks[4], (D,), dtype=jnp.float32) * s, 'Wv': jax.random.normal(ks[5], (D, D), dtype=jnp.float32) * s, 'bv': jax.random.normal(ks[6], (D,), dtype=jnp.float32) * s, 'Wo': jax.random.normal(ks[7], (D, D), dtype=jnp.float32) * s, 'bo': jax.random.normal(ks[8], (D,), dtype=jnp.float32) * s, 'scale': jnp.ones((1,), dtype=jnp.float32) * H ** (-0.5)}
    _L0_attn_in = _L0_attn_setup()

    def _L0_ffn_setup():
        import math
        import jax, jax.numpy as jnp
        import numpy as np
        TOP_K = 2
        _GELU_C = math.sqrt(2.0 / math.pi)

        def gelu_new(x):
            return 0.5 * x * (1.0 + jnp.tanh(_GELU_C * (x + 0.044715 * x * x * x)))
        key = jax.random.key(seed)
        ks = jax.random.split(key, 6)
        B, T, C, E, H = (2, 256, 128, 8, 512)
        s_in = 1.0 / math.sqrt(C)
        s_hid = 1.0 / math.sqrt(H)
        return {'x': jax.random.normal(ks[0], (B, T, C), dtype=jnp.float32), 'router_w': jax.random.normal(ks[1], (E, C), dtype=jnp.float32) * s_in, 'w_fc': jax.random.normal(ks[2], (E, C, H), dtype=jnp.float32) * s_in, 'b_fc': jax.random.normal(ks[3], (E, H), dtype=jnp.float32) * 0.02, 'w_proj': jax.random.normal(ks[4], (E, H, C), dtype=jnp.float32) * s_hid, 'b_proj': jax.random.normal(ks[5], (E, C), dtype=jnp.float32) * 0.02}
    _L0_ffn_in = _L0_ffn_setup()
    _L0_c = _w((lambda *s: np.random.randn(*s).astype(np.float32) * 0.05)(32, 128))
    _L0_wmod = _w((lambda *s: np.random.randn(*s).astype(np.float32) * 0.05)(128, 6 * 128) * 128 ** (-0.5))

    def _L1_attn_setup():
        import jax, jax.numpy as jnp
        import numpy as np
        EMBED_DIM = 128
        NUM_HEADS = 16
        DEPTH = 12
        HEAD_DIM = EMBED_DIM // NUM_HEADS // 2
        LAMBDA_INIT = float(0.8 - 0.6 * np.exp(-0.3 * DEPTH))
        B, T = (2, 256)
        key = jax.random.key(seed)
        ks = jax.random.split(key, 10)
        s = 0.02
        return {'query': jax.random.normal(ks[0], (B, T, EMBED_DIM), jnp.float32), 'Wq': jax.random.normal(ks[1], (EMBED_DIM, EMBED_DIM), jnp.float32) * s, 'Wk': jax.random.normal(ks[2], (EMBED_DIM, EMBED_DIM), jnp.float32) * s, 'Wv': jax.random.normal(ks[3], (EMBED_DIM, EMBED_DIM), jnp.float32) * s, 'Wo': jax.random.normal(ks[4], (EMBED_DIM, EMBED_DIM), jnp.float32) * s, 'lambda_q1': jax.random.normal(ks[5], (HEAD_DIM,), jnp.float32) * 0.1, 'lambda_k1': jax.random.normal(ks[6], (HEAD_DIM,), jnp.float32) * 0.1, 'lambda_q2': jax.random.normal(ks[7], (HEAD_DIM,), jnp.float32) * 0.1, 'lambda_k2': jax.random.normal(ks[8], (HEAD_DIM,), jnp.float32) * 0.1, 'subln_w': jnp.ones((2 * HEAD_DIM,), jnp.float32)}
    _L1_attn_in = _L1_attn_setup()

    def _L1_ffn_setup():
        import jax, jax.numpy as jnp
        import numpy as np
        key = jax.random.key(seed)
        ks = jax.random.split(key, 5)
        B, T, D, E = (4, 256, 128, 8)
        inputs = jax.random.normal(ks[0], (B, T, D), dtype=jnp.float32)
        Wr = jax.random.normal(ks[1], (D, E), dtype=jnp.float32) * 0.02
        br = jnp.zeros((E,), dtype=jnp.float32)
        W1 = jax.random.normal(ks[2], (E, D, D), dtype=jnp.float32) * 0.02
        b1 = jnp.zeros((E, D), dtype=jnp.float32)
        W2 = jax.random.normal(ks[3], (E, D, D), dtype=jnp.float32) * 0.02
        b2 = jnp.zeros((E, D), dtype=jnp.float32)
        return {'inputs': inputs, 'Wr': Wr, 'br': br, 'W1': W1, 'b1': b1, 'W2': W2, 'b2': b2}
    _L1_ffn_in = _L1_ffn_setup()
    _L1_c = _w((lambda *s: np.random.randn(*s).astype(np.float32) * 0.05)(32, 128))
    _L1_wmod = _w((lambda *s: np.random.randn(*s).astype(np.float32) * 0.05)(128, 6 * 128) * 128 ** (-0.5))
    _d = {'L0_attn_x': _L0_attn_in['x'], 'L0_attn_Wq': _L0_attn_in['Wq'], 'L0_attn_bq': _L0_attn_in['bq'], 'L0_attn_Wk': _L0_attn_in['Wk'], 'L0_attn_bk': _L0_attn_in['bk'], 'L0_attn_Wv': _L0_attn_in['Wv'], 'L0_attn_bv': _L0_attn_in['bv'], 'L0_attn_Wo': _L0_attn_in['Wo'], 'L0_attn_bo': _L0_attn_in['bo'], 'L0_attn_scale': _L0_attn_in['scale'], 'L0_ffn_router_w': _L0_ffn_in['router_w'], 'L0_ffn_w_fc': _L0_ffn_in['w_fc'], 'L0_ffn_b_fc': _L0_ffn_in['b_fc'], 'L0_ffn_w_proj': _L0_ffn_in['w_proj'], 'L0_ffn_b_proj': _L0_ffn_in['b_proj'], 'L0_c': _L0_c, 'L0_wmod': _L0_wmod, 'L1_attn_Wq': _L1_attn_in['Wq'], 'L1_attn_Wk': _L1_attn_in['Wk'], 'L1_attn_Wv': _L1_attn_in['Wv'], 'L1_attn_Wo': _L1_attn_in['Wo'], 'L1_attn_lambda_q1': _L1_attn_in['lambda_q1'], 'L1_attn_lambda_k1': _L1_attn_in['lambda_k1'], 'L1_attn_lambda_q2': _L1_attn_in['lambda_q2'], 'L1_attn_lambda_k2': _L1_attn_in['lambda_k2'], 'L1_attn_subln_w': _L1_attn_in['subln_w'], 'L1_ffn_Wr': _L1_ffn_in['Wr'], 'L1_ffn_br': _L1_ffn_in['br'], 'L1_ffn_W1': _L1_ffn_in['W1'], 'L1_ffn_b1': _L1_ffn_in['b1'], 'L1_ffn_W2': _L1_ffn_in['W2'], 'L1_ffn_b2': _L1_ffn_in['b2'], 'L1_c': _L1_c, 'L1_wmod': _L1_wmod}
    _x0 = _d['L0_attn_x']
    _d['L0_attn_x'] = jax.random.normal(jax.random.fold_in(jax.random.key(seed), 1), (32, 256, 128), dtype=_x0.dtype)
    del _x0
    return _d

def reference(L0_attn_x, L0_attn_Wq, L0_attn_bq, L0_attn_Wk, L0_attn_bk, L0_attn_Wv, L0_attn_bv, L0_attn_Wo, L0_attn_bo, L0_attn_scale, L0_ffn_router_w, L0_ffn_w_fc, L0_ffn_b_fc, L0_ffn_w_proj, L0_ffn_b_proj, L0_c, L0_wmod, L1_attn_Wq, L1_attn_Wk, L1_attn_Wv, L1_attn_Wo, L1_attn_lambda_q1, L1_attn_lambda_k1, L1_attn_lambda_q2, L1_attn_lambda_k2, L1_attn_subln_w, L1_ffn_Wr, L1_ffn_br, L1_ffn_W1, L1_ffn_b1, L1_ffn_W2, L1_ffn_b2, L1_c, L1_wmod):

    def _L0_attn_ref(x, Wq, bq, Wk, bk, Wv, bv, Wo, bo, scale):
        import jax, jax.numpy as jnp
        import numpy as np
        B, L, D, N = (2, 256, 128, 16)
        H = D // N
        THETA = 10000.0

        def apply_rope(x):
            l, h = (x.shape[-2], x.shape[-1])
            freqs = THETA ** (-jnp.arange(0, h, 2, dtype=jnp.float32) / h)
            ang = jnp.arange(l, dtype=jnp.float32)[:, None] * freqs
            cos, sin = (jnp.cos(ang), jnp.sin(ang))
            x_even = x[..., 0::2]
            x_odd = x[..., 1::2]
            out_even = cos * x_even - sin * x_odd
            out_odd = sin * x_even + cos * x_odd
            return jnp.stack((out_even, out_odd), axis=-1).reshape(x.shape)
        b, l, d = x.shape
        q = x @ Wq.T + bq
        k = x @ Wk.T + bk
        v = x @ Wv.T + bv
        q = q.reshape(b, l, N, H).transpose(0, 2, 1, 3)
        k = k.reshape(b, l, N, H).transpose(0, 2, 1, 3)
        v = v.reshape(b, l, N, H).transpose(0, 2, 1, 3)
        q = apply_rope(q) * scale
        k = apply_rope(k)
        dots = jnp.einsum('bnih,bnjh->bnij', q, k)
        i = jnp.arange(l)
        mask = i[:, None] < i[None, :]
        dots = jnp.where(mask, jnp.float32(-100000.0), dots)
        attn = jax.nn.softmax(dots, axis=-1)
        o = jnp.einsum('bnij,bnjh->bnih', attn, v)
        o = o.transpose(0, 2, 1, 3).reshape(b, l, d)
        return o @ Wo.T + bo

    def _L0_ffn_ref(x, router_w, w_fc, b_fc, w_proj, b_proj):
        import math
        import jax, jax.numpy as jnp
        import numpy as np
        TOP_K = 2
        _GELU_C = math.sqrt(2.0 / math.pi)

        def gelu_new(x):
            return 0.5 * x * (1.0 + jnp.tanh(_GELU_C * (x + 0.044715 * x * x * x)))
        B, T, C = x.shape
        E = router_w.shape[0]
        N = B * T
        xf = x.reshape(N, C)
        logits = xf @ router_w.T
        probs = jax.nn.softmax(logits, axis=-1)
        topk_probs, topk_idx = jax.lax.top_k(probs, TOP_K)
        topk_probs = topk_probs / jnp.sum(topk_probs, axis=-1, keepdims=True)
        combine = jnp.zeros((N, E), dtype=x.dtype).at[jnp.arange(N)[:, None], topk_idx].add(topk_probs)
        h = gelu_new(jnp.einsum('nc,ech->neh', xf, w_fc) + b_fc)
        out = jnp.einsum('neh,ehc->nec', h, w_proj) + b_proj
        y = jnp.einsum('nec,ne->nc', out, combine)
        return y.reshape(B, T, C)

    def _L1_attn_ref(query, Wq, Wk, Wv, Wo, lambda_q1, lambda_k1, lambda_q2, lambda_k2, subln_w):
        import jax, jax.numpy as jnp
        import numpy as np
        EMBED_DIM = 128
        NUM_HEADS = 16
        DEPTH = 12
        HEAD_DIM = EMBED_DIM // NUM_HEADS // 2
        LAMBDA_INIT = float(0.8 - 0.6 * np.exp(-0.3 * DEPTH))
        B, T = (2, 256)
        Bsz, Tt, E = query.shape
        H, hd = (NUM_HEADS, HEAD_DIM)
        scaling = hd ** (-0.5)
        q = jnp.einsum('bte,fe->btf', query, Wq).reshape(Bsz, Tt, 2 * H, hd).transpose(0, 2, 1, 3)
        k = jnp.einsum('bse,fe->bsf', query, Wk).reshape(Bsz, Tt, 2 * H, hd).transpose(0, 2, 1, 3)
        v = jnp.einsum('bse,fe->bsf', query, Wv).reshape(Bsz, Tt, H, 2 * hd).transpose(0, 2, 1, 3)
        q = q * scaling
        scores = jnp.einsum('bhtd,bhsd->bhts', q, k)
        attn_w = jax.nn.softmax(scores.astype(jnp.float32), axis=-1).astype(q.dtype)
        lam1 = jnp.exp(jnp.sum(lambda_q1 * lambda_k1))
        lam2 = jnp.exp(jnp.sum(lambda_q2 * lambda_k2))
        lam = lam1 - lam2 + LAMBDA_INIT
        aw = attn_w.reshape(Bsz, H, 2, Tt, Tt)
        aw = aw[:, :, 0] - lam * aw[:, :, 1]
        attn = jnp.einsum('bhts,bhsd->bhtd', aw, v)
        x32 = attn.astype(jnp.float32)
        normed = (x32 * jax.lax.rsqrt(jnp.mean(x32 * x32, axis=-1, keepdims=True) + 1e-05)).astype(attn.dtype)
        attn = normed * subln_w
        attn = attn * (1.0 - LAMBDA_INIT)
        out = attn.transpose(0, 2, 1, 3).reshape(Bsz, Tt, H * 2 * hd)
        return jnp.einsum('bte,fe->btf', out, Wo)

    def _L1_ffn_ref(inputs, Wr, br, W1, b1, W2, b2):
        import jax, jax.numpy as jnp
        import numpy as np
        B, T, D = inputs.shape
        E = Wr.shape[1]
        x = inputs.reshape(B * T, D)
        N = x.shape[0]
        C = N // E
        logits = x @ Wr + br
        probs = jax.nn.softmax(logits, axis=-1)
        gate = jnp.max(probs, axis=-1, keepdims=True)
        idx = jnp.argmax(probs, axis=-1)
        mask = jax.nn.one_hot(idx, E, dtype=jnp.float32)
        pos = (jnp.cumsum(mask, axis=0) * mask).astype(jnp.int32)
        mask = mask * (pos < C).astype(jnp.float32)
        mask_flat = jnp.sum(mask, axis=-1, keepdims=True)
        gate = gate * mask_flat
        combine = (gate * mask_flat * jax.nn.one_hot(idx, E, dtype=jnp.float32))[..., None] * jax.nn.one_hot(pos, C, dtype=jnp.float32)
        dispatch = combine
        expert_in = jnp.einsum('nd,nec->ecd', x, dispatch)
        h = jax.nn.relu(jnp.einsum('ecd,edf->ecf', expert_in, W1) + b1[:, None, :])
        eo = jnp.einsum('ecf,efd->ecd', h, W2) + b2[:, None, :]
        out = jnp.einsum('ecd,nec->nd', eo, combine)
        return out.reshape(B, T, D)
    x = L0_attn_x
    mod = (_silu(L0_c) @ L0_wmod).reshape(L0_c.shape[0], 6, 1, -1)
    sa, ca, ga, sb, cb, gb = (mod[:, 0], mod[:, 1], mod[:, 2], mod[:, 3], mod[:, 4], mod[:, 5])
    ga = (2 * (ga >= 0) - 1) * jnp.maximum(jnp.abs(ga), 0.25)
    gb = (2 * (gb >= 0) - 1) * jnp.maximum(jnp.abs(gb), 0.25)
    h = _layernorm(x, axis=-1) * (1 + ca) + sa
    x = x + ga * _L0_attn_ref(h, L0_attn_Wq, L0_attn_bq, L0_attn_Wk, L0_attn_bk, L0_attn_Wv, L0_attn_bv, L0_attn_Wo, L0_attn_bo, L0_attn_scale)
    h = _layernorm(x, axis=-1) * (1 + cb) + sb
    x = x + gb * _L0_ffn_ref(h, L0_ffn_router_w, L0_ffn_w_fc, L0_ffn_b_fc, L0_ffn_w_proj, L0_ffn_b_proj)
    mod = (_silu(L1_c) @ L1_wmod).reshape(L1_c.shape[0], 6, 1, -1)
    sa, ca, ga, sb, cb, gb = (mod[:, 0], mod[:, 1], mod[:, 2], mod[:, 3], mod[:, 4], mod[:, 5])
    ga = (2 * (ga >= 0) - 1) * jnp.maximum(jnp.abs(ga), 0.25)
    gb = (2 * (gb >= 0) - 1) * jnp.maximum(jnp.abs(gb), 0.25)
    h = _layernorm(x, axis=-1) * (1 + ca) + sa
    x = x + ga * _L1_attn_ref(h, L1_attn_Wq, L1_attn_Wk, L1_attn_Wv, L1_attn_Wo, L1_attn_lambda_q1, L1_attn_lambda_k1, L1_attn_lambda_q2, L1_attn_lambda_k2, L1_attn_subln_w)
    h = _layernorm(x, axis=-1) * (1 + cb) + sb
    x = x + gb * _L1_ffn_ref(h, L1_ffn_Wr, L1_ffn_br, L1_ffn_W1, L1_ffn_b1, L1_ffn_W2, L1_ffn_b2)
    return x

_drawn_inputs = setup_inputs


def setup_inputs(seed=0):
    import zlib

    import numpy as np

    out = dict(_drawn_inputs(seed))
    spreads = {'L1_attn_subln_w': (1.0, 0.6),
     'L1_ffn_br': (0.0, 0.8),
     'L1_ffn_b1': (0.0, 0.8),
     'L1_ffn_b2': (0.0, 0.8)}
    factors = {'L0_attn_Wq': 8.0,
     'L0_attn_bq': 8.0,
     'L0_attn_Wk': 8.0,
     'L0_attn_bk': 8.0,
     'L0_attn_Wv': 8.0,
     'L0_attn_bv': 8.0,
     'L0_attn_Wo': 8.0,
     'L0_attn_bo': 6.943,
     'L0_ffn_b_fc': 8.0,
     'L0_ffn_b_proj': 8.0,
     'L1_attn_Wq': 8.0,
     'L1_attn_Wk': 8.0,
     'L1_attn_Wv': 6.204,
     'L1_attn_Wo': 6.111,
     'L1_attn_lambda_q1': 8.0,
     'L1_attn_lambda_k1': 8.0,
     'L1_attn_lambda_q2': 8.0,
     'L1_attn_lambda_k2': 8.0,
     'L1_ffn_Wr': 8.0,
     'L1_ffn_W1': 8.0,
     'L1_ffn_W2': 8.0,
     'L1_c': 5.631,
     'L1_wmod': 5.582}
    for name, (base, spread) in spreads.items():
        noise = np.random.default_rng([zlib.crc32(name.encode()), seed]).standard_normal(out[name].shape)
        drawn = base * np.exp(spread * noise) if base else spread * noise
        out[name] = jnp.asarray(drawn.astype(out[name].dtype))
    for name, factor in factors.items():
        out[name] = (out[name] * factor).astype(out[name].dtype)
    return out
```

```python
from contextlib import ExitStack
import numpy as np
import concourse.bass as bass
from concourse import mybir

F32, BF16, I32 = mybir.dt.float32, mybir.dt.bfloat16, mybir.dt.int32
ALU, ACT, AX = mybir.AluOpType, mybir.ActivationFunctionType, mybir.AxisListType

P = 128
D = 128
T = 256
QB = T // P
NEXP = 8
HID = 512
EPS = 1e-5
NC8 = 8
PAIR = D // NC8
TERMS_K = [0, 1, 2, 0, 1, 0]
TERMS_Q = [0, 0, 0, 1, 1, 2]
NT = len(TERMS_K)
ROWS = NT * PAIR
BIG = -1e30
LAMBDA_INIT = float(0.8 - 0.6 * np.exp(-0.3 * 12))
HEADS = [2, 4]
HD = [8, 4]
GROUPS = [4, 8]
AUNITS = [12, 32]
SLOTS = 10
BUFS = 3
C_ID, C_LT, C_MA, C_MC, C_PERM, C_ROT, C_COS, C_SIN, C_HM = 0, 128, 256, 384, 512, 640, 768, 1024, 1280
C_TRI, C_REG, C_CAP, C_IOTA = 1286, 1350, 1358, 1366


def sizes(nb):
    tokens = nb * T
    tiles = 2 * tokens // P + NEXP - 1
    return tokens + P, tiles, tokens // NEXP, C_IOTA + tiles


def constants(nb):
    region, tiles, cap, cols = sizes(nb)
    c = np.zeros((P, cols), np.float32)
    e = np.arange(NEXP)
    c[:, C_TRI:C_TRI + 64] = (e[None, :] < e[:, None]).reshape(1, 64)
    c[:, C_REG:C_REG + NEXP] = e * region
    c[:, C_CAP:C_CAP + NEXP] = e * cap + 1
    c[:, C_IOTA:] = np.arange(tiles)
    i = np.arange(P)
    c[:, C_ID:C_ID + P] = np.eye(P)
    c[:, C_LT:C_LT + P] = i[:, None] < i[None, :]
    c[:, C_MA:C_MA + P] = np.where(i[:, None] < i[None, :], BIG, 0)
    c[:, C_MC:C_MC + P] = np.where(i[:, None] > i[None, :], BIG, 0)
    feat = 16 * (i % 8) + i // 8
    c[feat, C_PERM + i] = 1
    c[feat ^ 1, C_ROT + i] = 1
    half = np.arange(0, 8, 2, dtype=np.float32) / np.float32(8)
    freqs = (np.float32(10000.0) ** (-half)).astype(np.float32)
    ang = np.arange(T, dtype=np.float32)[:, None] * freqs
    which = (feat % 8) // 2
    c[:, C_COS:C_COS + T] = np.cos(ang).astype(np.float32)[:, which].T
    sign = np.where(feat % 2 == 0, -1, 1).astype(np.float32)
    c[:, C_SIN:C_SIN + T] = np.sin(ang).astype(np.float32)[:, which].T * sign[:, None]
    for L in range(2):
        for j in range(HEADS[L]):
            own = (i % PAIR) // HD[L] == j
            aug = (i - ROWS) % HEADS[L] == j
            c[:, C_HM + 2 * L + j] = np.where(i < ROWS, own, (i < ROWS + 2 * HEADS[L]) & aug)
    return c


class Event:

    def __init__(self, sem, nb, n, by):
        self.sem, self.nb, self.n, self.by = sem, nb, n, by

    def at(self, L, b, k=None):
        done = (self.nb * self.n[0] if L else 0) + b * self.n[L] + (self.n[L] if k is None else k)
        return done * self.by


def wait(eng, event, L, b, k=None, own=None):
    value = event.at(L, b, k)
    if not isinstance(value, int) or value > 0:
        eng.wait_ge(event.sem, value)
        if own is not None and not isinstance(value, int):
            eng.sem_inc(own, 1)


def build(nc, NB, ins, out):
    ctx = ExitStack()
    with ctx:
        def sb(name, shape, dt=F32):
            return ctx.enter_context(nc.sbuf_tensor(name, shape, dt))

        def psum(name, cols):
            return ctx.enter_context(nc.psum_tensor(name, [P, cols], F32))

        def sem(name):
            return ctx.enter_context(nc.semaphore(name))

        def event(name, n0=1, n1=None, by=1):
            return Event(sem(name), NB, [n0, n0 if n1 is None else n1], by)

        X = sb("X", [P, NB * QB, D])
        REGION, TILES0, CAP, cols = sizes(NB)
        TPB = NB * QB
        CON = sb("CON", [P, cols])
        IDB = sb("IDB", [P, P], BF16)
        MAB = sb("MAB", [P, 4, P], BF16)
        MCB = sb("MCB", [P, 4, P], BF16)
        LTB = sb("LTB", [P, P], BF16)
        COSS, SINS = sb("COSS", [P, T]), sb("SINS", [P, T])
        WQP = sb("WQP", [P, 2, D])
        WKP = sb("WKP", [P, 2, D])
        WQR, WKR = sb("WQR", [P, D]), sb("WKR", [P, D])
        WVT, WOT = sb("WVT", [P, 2, D]), sb("WOT", [P, 2, D])
        BQK = sb("BQK", [P, 4])
        BVR = sb("BVR", [P, D])
        RWT = sb("RWT", [P, 3, NEXP])
        CA1T, SAT = sb("CA1T", [P, 2, 32]), sb("SAT", [P, 2, 32])
        LAMSEL = sb("LAMSEL", [P, 64])
        WSUB = sb("WSUB", [P, 8])
        NHALF = sb("NHALF", [P, 32])
        ST6, MV = sb("ST6", [P, 2, QB, 6]), sb("MV", [P, 2, QB, 2])
        RSTD, NMR = sb("RSTD", [P, 2, QB]), sb("NMR", [P, 2, QB])
        XN = sb("XN", [P, QB, D])
        HT = sb("HT", [P, T])
        T1, QK, RES = sb("T1", [P, 2, T]), sb("QK", [P, 2 * T]), sb("RES", [P, 2 * T])
        T2 = RES[:, :].rearrange("p (k t) -> p k t", k=2)
        PARTS = sb("PARTS", [P, 3, 2 * T], BF16)
        KU = sb("KU", [P, NC8, T], BF16)
        QS = sb("QS", [P, BUFS, NC8, T], BF16)
        KM = sb("KM", [P, BUFS, 4, NC8, T], BF16)
        VB = sb("VB", [P, BUFS, QB, 16, 32])
        MX = sb("MX", [P, QB * NC8 * 4])
        NM = sb("NM", [P, QB, 64], BF16)
        MTS = sb("MTS", [P, T], BF16)
        PT = sb("PT", [P, 4, 4 * T])
        OT = sb("OT", [P, 8, T])
        TOK = sb("TOK", [P, 8, QB, 4, 9])
        RS, RSL = sb("RS", [P, 64]), sb("RSL", [P, 64])
        TN = sb("TN", [P, 8, QB, 4, 8])
        AOU, SQ, AO = sb("AOU", [P, QB, D]), sb("SQ", [P, QB, D]), sb("AO", [P, QB, D])
        SS, RMS = sb("SS", [P, 32]), sb("RMS", [P, 32])
        AOT = sb("AOT", [P, T])
        MB = sb("MB", [P, 5, D])
        YG = sb("YG", [P, QB, D])
        H2 = sb("H2", [P, QB, D])
        H2T = sb("H2T", [P, T])
        GX = sb("GX", [P, QB, D])
        LG = sb("LG", [P, QB, NEXP])
        ONB = sb("ONB", [P, P], BF16)
        BRR = sb("BRR", [P, NEXP])
        CMP, EQ = sb("CMP", [P, QB, 64]), sb("EQ", [P, QB, 64])
        RK, OHS = sb("RK", [P, QB * NEXP]), sb("OHS", [P, QB, NEXP], BF16)
        OH = sb("OH", [P, TPB, 2, NEXP])
        OH1 = sb("OH1", [P, QB, NEXP])
        M1, L2, W = sb("M1", [P, QB]), sb("L2", [P, QB]), sb("W", [P, QB])
        LE, LX = sb("LE", [P, QB, NEXP]), sb("LX", [P, QB, NEXP])
        WALL = sb("WALL", [P, TPB, 2])
        SALL = sb("SALL", [P, TPB, 2])
        GALL = sb("GALL", [P, TPB])
        RC = sb("RC", [P, 2, NEXP])
        POS = sb("POS", [P, QB, NEXP])
        PO = sb("PO", [P, QB, 2, NEXP])
        PP, EO, KEEP = sb("PP", [P, QB]), sb("EO", [P, QB]), sb("KEEP", [P, QB])
        SIDX = sb("SIDX", [P, QB, 2], I32)
        SF = sb("SF", [P, QB])
        GI0, GI1 = sb("GI0", [P, TPB, 2], I32), sb("GI1", [P, TPB], I32)
        GIS = sb("GIS", [P, QB, 2], I32)
        GY = sb("GY", [P, QB, 2, D])
        GC = sb("GC", [P, QB, D])
        GBR = sb("GBR", [P, 2, D])
        CNT, NTI, NTF = sb("CNT", [P, NEXP]), sb("NTI", [P, NEXP], I32), sb("NTF", [P, NEXP])
        BT, ADJ = sb("BT", [P, NEXP]), sb("ADJ", [P, NEXP])
        BT8 = sb("BT8", [P, 64])
        CNTI = sb("CNTI", [1, NEXP], I32)
        TE, ROW = sb("TE", [1, TILES0], I32), sb("ROW", [1, TILES0], I32)
        LIM = sb("LIM", [1, 1])
        WFC = sb("WFC", [P, NEXP * HID])
        ONE3 = sb("ONE3", [3, P], BF16)
        B1T = RWT[:, 1, :]

        KMF = [KM[:, k, :, :, :].rearrange("p a b c -> p (a b c)").bitcast(F32) for k in range(3)]
        XIN = [KMF[0][:, D * k:D * k + D] for k in range(4)]
        XTT = [KMF[0][:, 512 + D * k:640 + D * k] for k in range(2)]
        HS = [KMF[0][:, 1024 + HID * k:1024 + HID * (k + 1)] for k in range(2)]
        WPR = [KMF[k][:, 2048:4096] for k in range(2)]
        OTF = OT[:, :, :].rearrange("p a t -> p (a t)")
        HTT = [OTF[:, HID * k:HID * (k + 1)] for k in range(2)]
        YO = [OTF[:, 1024 + D * k:1152 + D * k] for k in range(4)]
        BFP = QS[0:3, :, :, :].rearrange("p b c t -> p (b c t)")[:, 0:NEXP * (HID + D)]
        BP3, BP3B = KMF[2][0:3, 0:NEXP * HID], PT[0:3, 3, :]
        W1S, W2S = KMF[1][:, 0:1024], KMF[1][:, 1024:2048]
        B2R = KMF[1][:, 2048:3072]
        CW = min(512, CAP)
        KC = CW // P
        XC = [KMF[2][:, 512 * k:512 * k + CW] for k in range(2)]
        XCT = [KMF[2][:, 1024 + 512 * k:1024 + 512 * k + CW] for k in range(2)]
        HC = [KMF[2][:, 2048 + 512 * k:2048 + 512 * k + CW] for k in range(2)]
        YC = [KMF[2][:, 3072 + 512 * k:3072 + 512 * k + CW] for k in range(2)]
        CHUNKS = NEXP * CAP // CW
        WORK = PT[:, :, :].rearrange("p a t -> p (a t)")
        ZERO = OT[:, 0:4, :].rearrange("p a t -> p (a t)")

        AB = [psum(f"AB{i}", 512) for i in range(2)]
        CS = [psum(f"CS{i}", 1024) for i in range(2)]
        OB, MI = psum("OB", 512), psum("MI", 512)
        MIB = MI[:, :].bitcast(BF16)

        parts_dram = nc.dram_tensor("parts_dram", [BUFS, 2, 3, P, T], BF16, kind="Internal").ap()
        max_dram = nc.dram_tensor("max_dram", [BUFS, 64, T], BF16, kind="Internal").ap()
        xs0 = nc.dram_tensor("xs0", [NEXP * REGION, D], F32, kind="Internal").ap()
        ys0 = nc.dram_tensor("ys0", [TILES0 * P, D], F32, kind="Internal").ap()
        xs1 = nc.dram_tensor("xs1", [NEXP * CAP, D], F32, kind="Internal").ap()
        ys1 = nc.dram_tensor("ys1", [NEXP * CAP, D], F32, kind="Internal").ap()
        mod_dram = nc.dram_tensor("mod_dram", [2, 32, 5, D], F32, kind="Internal").ap()

        e_stats, e_aggr, e_veps, e_rstd = event("e_stats", 2), event("e_aggr", 2), event("e_veps"), event("e_rstd", 3)
        e_xn, e_xnT, e_hT = event("e_xn", 2), event("e_xnT"), event("e_hT")
        e_qkps, e_cos, e_qkrot, e_sin, e_qk = (event("e_qkps"), event("e_cos", 2, 0), event("e_qkrot", 1, 0),
                                               event("e_sin", 2, 0), event("e_qk"))
        e_split = event("e_split", 4)
        e_pout, e_qs, e_ku = event("e_pout", 3, by=16), event("e_qs", 6, by=16), event("e_ku", 3, by=16)
        e_km = event("e_km", 2, 4)
        e_vps, e_v = event("e_vps"), event("e_v")
        e_amm, e_amax = event("e_amm", *AUNITS), event("e_amax", *AUNITS)
        e_nm, e_nmT, e_mts = event("e_nm", 3), event("e_nmT"), event("e_mts")
        e_mout, e_min = event("e_mout", by=16), event("e_min", by=16)
        e_cmm, e_exp = event("e_cmm", 8, 16), event("e_exp", 8, 16)
        e_pv, e_ot = event("e_pv", *GROUPS), event("e_ot", 2, 4)
        e_otT, e_tok = event("e_otT", 2, 4), event("e_tok", 2, 4)
        e_rs, e_rsl, e_tn, e_aou, e_sq, e_ss = (event("e_rs"), event("e_rsl", 0, 1), event("e_tn", 0, 1),
                                                event("e_aou", 0, 2), event("e_sq", 0, 1), event("e_ss", 0, 1))
        e_ms, e_rms, e_nrm, e_ao = event("e_ms", 0, 1), event("e_rms", 0, 1), event("e_nrm", 0, 1), event("e_ao", 2, 1)
        e_aoT, e_aot, e_y, e_mb, e_yg = (event("e_aoT"), event("e_aot"), event("e_y"), event("e_mb", by=16),
                                         event("e_yg"))
        e_xa, e_x1 = event("e_xa", 1, 0), event("e_x1")
        e_st2, e_ag2, e_ve2, e_rs2 = event("e_st2", 2), event("e_ag2", 2), event("e_ve2"), event("e_rs2", 3)
        e_h1, e_h1c, e_h2 = event("e_h1", 2), event("e_h1c"), event("e_h2")
        e_rank = event("e_rank", 5)
        e_oh, e_ohs, e_wt = event("e_oh", 2, 1), event("e_ohs"), event("e_wt", 4, 1)
        e_wexp, e_gate, e_gate2 = event("e_wexp"), event("e_gate", 3, 2), event("e_gate2", 0, 2)
        e_posps, e_pos, e_slot = event("e_posps"), event("e_pos", 3, 2), event("e_slot", 3, 9)
        e_sc, e_gx = event("e_sc", 4, 2, 16), event("e_gx", 0, 1)
        e_gis, e_gat, e_gbr = event("e_gis", 0, 1), event("e_gat", 0, 4, 16), event("e_gbr", 0, 1, 16)
        e_cmb, e_x2 = event("e_cmb", 0, 5), event("e_x2", 0, 1)
        e_h2T, e_h2t, e_lgps, e_lg = event("e_h2T"), event("e_h2t"), event("e_lgps"), event("e_lg")
        w_pool, w_pe, w_dve, w_sp = sem("w_pool"), sem("w_pe"), sem("w_dve"), sem("w_sp")
        s_ld, s_w, s_ones = sem("s_ld"), sem("s_w"), sem("s_ones")
        s_cb, s_mm, s_ev, s_sv, s_sa = sem("s_cb"), sem("s_mm"), sem("s_ev"), sem("s_sv"), sem("s_sa")
        s_fill, s_wp = sem("s_fill"), sem("s_wp")
        s_rc = sem("s_rc")
        s_tab, s_b3, s_bld, s_tail = sem("s_tab"), sem("s_b3"), sem("s_bld"), sem("s_tail")
        f_x, f_st = [sem(f"f_x{r}") for r in range(4)], [sem(f"f_st{r}") for r in range(4)]
        c_x, c_st = [sem(f"c_x{r}") for r in range(2)], [sem(f"c_st{r}") for r in range(2)]
        o_g, o_gb = [sem(f"o_g{r}") for r in range(2)], [sem(f"o_gb{r}") for r in range(2)]
        f_xT, f_xt, f_h, f_g, f_hT, f_ht, f_y, f_yo = (sem("f_xT"), sem("f_xt"), sem("f_h"),
                                                                  sem("f_g"), sem("f_hT"), sem("f_ht"), sem("f_y"),
                                                                  sem("f_yo"))
        c_w, c_xT, c_xt, c_h, c_r, c_y, c_yo = (sem("c_w"), sem("c_xT"), sem("c_xt"),
                                                           sem("c_h"), sem("c_r"), sem("c_y"), sem("c_yo"))
        o_m, o_a, o_st = sem("o_m"), sem("o_a"), sem("o_st")

        IDF = CON[:, C_ID:C_ID + P]
        PERM, ROT = CON[:, C_PERM:C_PERM + P], CON[:, C_ROT:C_ROT + P]

        WRAW = KM[:, 0, :, :, :].rearrange("p a b c -> p (a b c)").bitcast(F32)
        wraw = [WRAW[:, k * D:(k + 1) * D] for k in range(8)]
        WMOD = [WRAW[:, 1024 + 768 * L:1024 + 768 * (L + 1)] for L in range(2)]
        S = KM[:, 1, :, :, :].rearrange("p a b c -> p (a b c)").bitcast(F32)
        CC = [S[0:32, 128 * L:128 * L + 128] for L in range(2)]
        CE = [S[0:32, 256 + 128 * L:384 + 128 * L] for L in range(2)]
        MODR = [S[0:32, 512 + 768 * L:512 + 768 * (L + 1)] for L in range(2)]
        ROWS_OUT = [S[0:32, 2048 + 640 * L:2048 + 640 * (L + 1)].rearrange("p (k d) -> p k d", d=D) for L in range(2)]
        S2 = KM[:, 2, :, :, :].rearrange("p a b c -> p (a b c)").bitcast(F32)
        SIGN = [S2[0:32, 256 * L:256 * (L + 1)].rearrange("p (k d) -> p k d", d=D) for L in range(2)]
        MAG = [S2[0:32, 512 + 256 * L:512 + 256 * (L + 1)].rearrange("p (k d) -> p k d", d=D) for L in range(2)]
        CT = [S2[:, 1024 + 32 * L:1056 + 32 * L] for L in range(2)]
        BRAW = S2[:, 1100:1102]
        BO32 = S2[0:32, 1152:1280]
        LMB = S2[:, 1300:1316]
        LMP = S2[:, 1320:1328]
        LMS = S2[:, 1330:1332]
        LMX = S2[:, 1334:1337]
        RWS = S2[0:8, 1344:1472]
        SCL = S2[:, 1480:1481]
        B1S = S2[0:8, 1500:1628]
        SV_SILU, SV_LAM, SV_MOD = 6, 8, 24

        block = ctx.enter_context(nc.Block())
        loop_first, loop_steps = 2, (NB - 4) // 3 * 3
        attn_w = ["Wq", "Wk", "Wv", "Wo"]

        def steps(eng, step):
            for i in range(-2, loop_first):
                step(i, i % 3)
            with eng.Fori(loop_first, loop_first + loop_steps - 2, 3) as i:
                for r in range(3):
                    step(i + r, (loop_first + r) % 3)
            for i in range(loop_first + loop_steps, NB + 2):
                step(i, i % 3)

        def stages(i):
            if not isinstance(i, int):
                return True, True, True, True, True
            return i + 2 < NB, 0 <= i + 1 < NB, 0 <= i < NB, 0 <= i - 1 < NB, 0 <= i - 2 < NB

        def chunk(L, s):
            per = [[0, 2, 4, 6, 8, 9, 10, 11, 12, 12], [0, 4, 8, 12, 16, 20, 23, 26, 29, 32]][L]
            return range(per[s], per[s + 1]) if s < 9 else range(0)

        def group_of(L, s):
            if L == 0:
                return s // 2 if s < 8 and s % 2 == 1 else None
            return s - 1 if 1 <= s < 9 else None

        def heads(L, G):
            return [(G, g) if L else (2 * G + g // 2, g % 2) for g in range(4)]

        loads = []
        TAB_CNT, TAB_ALL = 2, 26

        def tile_loop(eng, behind, ahead):
            for t in range(2):
                ahead(t, t)
            n = (TILES0 - 4) // 4 * 4
            for t in range(2, 4):
                behind(t - 2, t - 2)
                ahead(t, t)
            with eng.Fori(4, 4 + n - 3, 4) as i:
                for r in range(4):
                    behind(i + r - 2, (r + 2) % 4)
                    ahead(i + r, r)
            for t in range(4 + n, TILES0 + 2):
                behind(t - 2, (t - 2) % 4)
                if t < TILES0:
                    ahead(t, t % 4)

        @block.sync
        def _(sp):
            def load(dst, src):
                sp.dma_start(dst, src).then_inc(s_ld, 16)
                loads.append(1)

            load(CON[:, :], ins["const"])
            for L in range(2):
                for k, w in enumerate(attn_w):
                    load(wraw[4 * L + k], ins[f"L{L}_attn_{w}"])
                load(WMOD[L], ins[f"L{L}_wmod"])
                load(CC[L], ins[f"L{L}_c"])
            load(BRAW[:, 0:1], ins["L0_attn_bq"].rearrange("(p a) -> p a", a=1))
            load(BRAW[:, 1:2], ins["L0_attn_bk"].rearrange("(p a) -> p a", a=1))
            load(BVR[:, :], ins["L0_attn_bv"].partition_broadcast(P))
            load(BO32, ins["L0_attn_bo"].partition_broadcast(32))
            load(SCL, ins["L0_attn_scale"].partition_broadcast(P))
            load(RWS, ins["L0_ffn_router_w"])
            load(RWT[:, 2, :], ins["L1_ffn_Wr"])
            for k, n in enumerate(["q1", "k1", "q2", "k2"]):
                load(LMB[:, 4 * k:4 * k + 4], ins[f"L1_attn_lambda_{n}"].partition_broadcast(P))
            load(WSUB[:, :], ins["L1_attn_subln_w"].partition_broadcast(P))
            load(BRR[:, :], ins["L1_ffn_br"].partition_broadcast(P))
            load(B1S, ins["L1_ffn_b1"])
            load(WFC[:, :].rearrange("p (e h) -> p e h", e=NEXP), ins["L0_ffn_w_fc"].rearrange("e c h -> c e h"))
            xin = ins["L0_attn_x"].rearrange("b (q p) d -> p (b q) d", p=P)
            step_b = 4
            for b in range(0, NB, step_b):
                load(X[:, QB * b:QB * (b + step_b), :], xin[:, QB * b:QB * (b + step_b), :])
            sp.wait_ge(s_sv, SV_MOD)
            for L in range(2):
                sp.dma_start(mod_dram[L], ROWS_OUT[L]).then_inc(s_w, 16)
            sp.wait_ge(s_w, 32)
            sp.wait_ge(s_ev, 22)
            for k in range(2):
                for h in range(2):
                    c = NEXP * D * h
                    sp.dma_start(WPR[k][:, c:c + NEXP * D].rearrange("p (e d) -> p e d", e=NEXP),
                                 ins["L0_ffn_w_proj"][:, P * (2 * k + h):P * (2 * k + h + 1), :].rearrange(
                                     "e p d -> p e d")).then_inc(s_wp, 16)
            sp.wait_ge(s_rc, 3)
            rows = NEXP * CAP // P
            for r in range(0, rows, 8):
                sp.dma_start(xs1[r * P:(r + 8) * P, :].rearrange("(p a) d -> p (a d)", a=8), ZERO
                             ).then_inc(s_fill, 16)
            sp.wait_ge(s_fill, 16 * (rows // 8))

            def layer(L):
                J = HEADS[L]

                def step(i, ph):
                    s1, s2, s3, s4, s5 = stages(i)
                    if s3:
                        n = 2 * J * NC8
                        wait(sp, e_mts, L, i, own=w_sp)
                        wait(sp, e_min, L, i - 3)
                        sp.dma_start(max_dram[ph, 0:n, :], MTS[0:n, :]).then_inc(e_mout.sem, 16)
                        wait(sp, e_mout, L, i, own=w_sp)
                        wait(sp, e_cmm, L, i - 3, own=w_sp)
                        sp.dma_start(QS[ROWS:ROWS + 2 * J, ph, :, :].rearrange("p c t -> p (c t)"),
                                     max_dram[ph, 0:n, :].rearrange("(r c) t -> r (c t)", c=NC8)
                                     ).then_inc(e_min.sem, 16)
                    if s4:
                        b = i - 1
                        wait(sp, e_h2, L, b - 1, own=w_sp)
                        sp.dma_start(MB[:, :, :].rearrange("p k d -> p (k d)"),
                                     bcast_rows(mod_dram, L, b)).then_inc(e_mb.sem, 16)
                    if s1 and L:
                        load_gb(i + 3)
                    if s1:
                        b, o = i + 2, (ph + 2) % 3
                        wait(sp, e_split, L, b)
                        wait(sp, e_qs, L, b - 3)
                        wait(sp, e_ku, L, b - 3, own=w_sp)
                        for part in range(3):
                            sp.dma_start(parts_dram[o, :, part].rearrange("q p t -> p q t"),
                                         PARTS[:, part, :].rearrange("p (q t) -> p q t", q=2)
                                         ).then_inc(e_pout.sem, 16)
                        wait(sp, e_pout, L, b, own=w_sp)
                        wait(sp, e_km, L, b - 1, own=w_sp)
                        for t0, n in ((0, 3), (3, 2), (5, 1)):
                            src = parts_dram[o, 1, TERMS_K[t0]:TERMS_K[t0] + n]
                            sp.dma_start(KU[PAIR * t0:PAIR * (t0 + n), :, :].rearrange("p c t -> p (c t)"),
                                         src.rearrange("a (r c) t -> (a r) (c t)", c=NC8)).then_inc(e_ku.sem, 16)
                        wait(sp, e_cmm, L, b - 3)
                        wait(sp, e_amm, L, b - 3, own=w_sp)
                        for t in range(NT):
                            sp.dma_start(QS[PAIR * t:PAIR * (t + 1), o, :, :].rearrange("p c t -> p (c t)"),
                                         parts_dram[o, 0, TERMS_Q[t]].rearrange("(r c) t -> r (c t)", c=NC8)
                                         ).then_inc(e_qs.sem, 16)

                def load_gb(b):
                    if isinstance(b, int) and b >= NB:
                        return
                    wait(sp, e_x2, L, b - 1, own=w_sp)
                    sp.dma_start(GBR[:, 0, :], bcast_rows(mod_dram, 0, b, 4)).then_inc(e_gbr.sem, 16)

                if L:
                    load_gb(0)
                steps(sp, step)

            def bcast_rows(dram, L, b, k=None):
                row = dram[L, bass.ds(b, 1)] if not isinstance(b, int) else dram[L, b:b + 1]
                if k is not None:
                    row = row[:, k:k + 1, :]
                return row.rearrange("b k d -> b (k d)").to_broadcast([P, (5 if k is None else 1) * D])

            layer(0)
            for k, n in enumerate(("L0_ffn_b_fc", "L0_ffn_b_proj")):
                sp.wait_ge(e_pv.sem, e_pv.at(0, NB - 1))
                sp.dma_start((BP3, BP3B)[k], ins[n].rearrange("e h -> (e h)").partition_broadcast(3)
                             ).then_inc(s_bld, 16)
            sp.wait_ge(s_tab, TAB_CNT)
            for e in range(NEXP):
                n = sp.value_load(CNTI[0:1, e:e + 1], min_val=0, max_val=NB * T)
                sp.dma_start(xs0[bass.ds(n + e * REGION, P), :], ZERO[:, 0:D]).then_inc(s_tail, 16)
            sp.wait_ge(s_tab, TAB_ALL)
            sp.wait_ge(s_tail, 16 * NEXP)
            sp.wait_ge(e_sc.sem, e_sc.at(0, NB - 1))

            def tile_load(t, r):
                if not isinstance(t, int) or t >= 4:
                    sp.wait_ge(f_xT, t - 3)
                row = sp.value_load(ROW[0:1, bass.ds(t, 1)], min_val=0, max_val=(NEXP - 1) * REGION + NB * T)
                sp.dma_start(XIN[r], xs0[bass.ds(row, P), :]).then_inc(f_x[r], 16)

            def tile_store(t, r):
                sp.wait_ge(f_yo, t + 1)
                sp.dma_start(ys0[bass.ds(t * P, P), :], YO[r]).then_inc(f_st[r], 16)

            for t in range(4):
                tile_load(t, t)
            n = (TILES0 - 4) // 4 * 4
            with sp.Fori(4, 4 + n - 3, 4) as i:
                for r in range(4):
                    tile_load(i + r, r)
                    tile_store(i + r - 4, r)
            for t in range(4 + n, TILES0 + 4):
                if t < TILES0:
                    tile_load(t, t % 4)
                tile_store(t - 4, t % 4)
            layer(1)
            for k in range(CHUNKS + 2):
                if k < CHUNKS:
                    if k == 0:
                        sp.wait_ge(e_sc.sem, e_sc.at(1, NB - 1))
                        sp.wait_ge(e_cmm.sem, e_cmm.at(1, NB - 1))
                        sp.dma_start(W1S.rearrange("p (e f) -> p e f", e=NEXP),
                                     ins["L1_ffn_W1"].rearrange("e c f -> c e f")).then_inc(c_w, 16)
                        sp.dma_start(W2S.rearrange("p (e f) -> p e f", e=NEXP),
                                     ins["L1_ffn_W2"].rearrange("e c f -> c e f")).then_inc(c_w, 16)
                        sp.dma_start(B2R, ins["L1_ffn_b2"].rearrange("e f -> (e f)").partition_broadcast(P)
                                     ).then_inc(c_w, 16)
                    if k >= 2:
                        sp.wait_ge(c_xT, k - 1)
                    sp.dma_start(XC[k % 2].rearrange("p (a d) -> p a d", d=D),
                                 xs1[k * CW:(k + 1) * CW, :].rearrange("(a p) d -> p a d", p=P)
                                 ).then_inc(c_x[k % 2], 16)
                if k >= 2:
                    sp.wait_ge(c_yo, k - 1)
                    sp.dma_start(ys1[(k - 2) * CW:(k - 1) * CW, :].rearrange("(a p) d -> p a d", p=P),
                                 YC[k % 2].rearrange("p (a d) -> p a d", d=D)).then_inc(c_st[k % 2], 16)
            for b in range(NB + 1):
                if b < NB:
                    if b >= 2:
                        sp.wait_ge(o_m, 2 * (b - 1))
                    sp.dma_start(GBR[:, b % 2, :], bcast_rows(mod_dram, 1, b, 4)).then_inc(o_gb[b % 2], 16)
                if b >= 1:
                    sp.wait_ge(o_a, b)
                    sp.dma_start(out[b - 1].rearrange("(q p) d -> p q d", p=P),
                                 X[:, QB * (b - 1):QB * b, :]).then_inc(o_st, 16)
            sp.wait_ge(o_st, 16 * NB)

        N_LD = 16 * len(loads)

        @block.scalar
        def _(act):
            act.wait_ge(s_ld, N_LD)
            for L in range(2):
                nc.scalar.activation(CE[L], CC[L], ACT.Exp, scale=-1.0).then_inc(s_sa, 1)
            n = 0
            outs = [(WQP[:, 0, :], D), (WKP[:, 0, :], D), (WVT[:, 0, :], D), (WOT[:, 0, :], D),
                    (WQP[:, 1, :], D), (WKP[:, 1, :], D), (WVT[:, 1, :], D), (WOT[:, 1, :], D),
                    (WQR[:, :], D), (WKR[:, :], D), (BQK[:, :], 4), (RWT[:, 0:2, :].rearrange("p a e -> p (a e)"), 2 * NEXP)]
            for k, (dst, w) in enumerate(outs):
                act.wait_ge(s_mm, k + 1)
                if k == 4:
                    nc.scalar.activation(dst, MI[:, 0:w], ACT.Copy, scale=float(HD[1]) ** -0.5).then_inc(s_ev, 1)
                else:
                    nc.scalar.activation(dst, MI[:, 0:w], ACT.Copy).then_inc(s_ev, 1)
            for L in range(2):
                act.wait_ge(s_mm, 13 + 3 * L)
                nc.scalar.activation(CT[L], MI[:, 0:32], ACT.Copy).then_inc(s_ev, 1)
                for h in range(2):
                    act.wait_ge(s_mm, 14 + 3 * L + h)
                    nc.scalar.activation(MODR[L][:, 384 * h:384 * h + 384], MI[0:32, 0:384], ACT.Copy
                                         ).then_inc(s_ev, 1)
            for k in range(4):
                act.wait_ge(s_mm, 19 + k)
                dst = (SAT if k % 2 == 0 else CA1T)[:, k // 2, :]
                nc.scalar.activation(dst, MI[:, 0:32], ACT.Copy, bias=0.0).then_inc(s_ev, 1)
            act.wait_ge(s_sv, SV_LAM)
            nc.scalar.activation(LMX[:, 0:2], LMS, ACT.Exp).then_inc(s_sa, 1)

            def layer(L):
                def step(i, ph):
                    s1, s2, s3, s4, s5 = stages(i)
                    for s in range(SLOTS):
                        if s4 and s < GROUPS[L] // 4:
                            tok(i - 1, 2 * s)
                            if s == 0:
                                tok(i - 1, 1)
                        if s1 and s == 1 + L:
                            b = i + 2
                            wait(act, e_rstd, L, b)
                            wait(act, e_xnT, L, b - 1)
                            for q in range(QB):
                                normed(XN[:, q, :], b, q, 0).then_inc(e_xn.sem, 1)
                        if s5 and s == 3:
                            b = i - 2
                            wait(act, e_rs2, L, b)
                            wait(act, e_h2T, L, b - 1)
                            wait(act, e_gx if L else e_sc, L, b - 1)
                            for q in range(QB):
                                normed(H2[:, q, :], b, q, 1).then_inc(e_h1.sem, 1)
                        if s1 and s == 1 + L:
                            b = i + 2
                            col = bass.ds(b, 1)
                            wait(act, e_xnT, L, b)
                            wait(act, e_vps, L, b - 1)
                            nc.scalar.activation(HT[:, :], MI[:, 0:T], ACT.Identity, scale=CA1T[:, L, col],
                                                 bias=SAT[:, L, col]).then_inc(e_hT.sem, 1)
                        if s1 and s == 3 and L == 1:
                            wait(act, e_qkps, L, i + 2)
                            wait(act, e_split, L, i + 1)
                            nc.scalar.activation(QK[:, :], MI[:, :], ACT.Copy).then_inc(e_qk.sem, 1)
                        if s4 and s == 7:
                            wait(act, e_aoT, L, i - 1)
                            wait(act, e_y, L, i - 2)
                            nc.scalar.activation(AOT[:, :], MI[:, 0:T], ACT.Copy).then_inc(e_aot.sem, 1)
                        if s1 and s == 5 and L == 1:
                            b = i + 2
                            wait(act, e_vps, L, b)
                            wait(act, e_pv, L, b - 3)
                            nc.scalar.activation(VB[:, (ph + 2) % 3, :, :, 0:8],
                                                 MI[:, 0:T].rearrange("p (q h d) -> p q h d", q=QB, d=8),
                                                 ACT.Copy).then_inc(e_v.sem, 1)
                        if s5 and s == 4:
                            wait(act, e_h2T, L, i - 2)
                            wait(act, e_lgps, L, i - 3)
                            nc.scalar.activation(H2T[:, :], MI[:, 0:T], ACT.Copy).then_inc(e_h2t.sem, 1)
                        if s1 and s == 4 - L:
                            wait(act, e_qk, L, i + 2)
                            wait(act, e_pout, L, i + 1)
                            nc.scalar.activation(PARTS[:, 0, :], QK[:, :], ACT.Copy).then_inc(e_split.sem, 1)
                        if s5 and s == 8:
                            b = i - 2
                            wait(act, e_wt, L, b)
                            wait(act, e_gate, L, b - 1)
                            src, dst = (L2[:, :], W[:, :]) if L == 0 else (LE[:, :, :], LX[:, :, :])
                            nc.scalar.activation(dst, src, ACT.Exp).then_inc(e_wexp.sem, 1)
                        if s1 and s == 5 - L:
                            wait(act, e_split, L, i + 2, 2)
                            nc.scalar.activation(PARTS[:, 1, :], RES[:, :], ACT.Copy).then_inc(e_split.sem, 1)
                        if s2 and s == 9:
                            wait(act, e_nmT, L, i + 1)
                            wait(act, e_mout, L, i)
                            n = 2 * HEADS[L] * NC8
                            nc.scalar.activation(MTS[0:n, :], MIB[0:n, 0:T], ACT.Copy).then_inc(e_mts.sem, 1)
                        G = group_of(L, s)
                        if s3 and G is not None:
                            for kb in range(2):
                                n = 2 * G + kb
                                w = 4 * (T if L or kb == 0 else P)
                                wait(act, e_cmm, L, i, n + 1)
                                if G < 2:
                                    wait(act, e_pv, L, i - 1, GROUPS[L] - 1 + G)
                                else:
                                    wait(act, e_pv, L, i, G - 1)
                                nc.scalar.activation(PT[:, n % 4, 0:w], CS[n % 2][:, 0:w], ACT.Exp
                                                     ).then_inc(e_exp.sem, 1)
                                if s4 and s == 1 and kb == 0 and L == 1:
                                    tok(i - 1, 3)
                            if G >= 2 and G % 2 == 0:
                                evac(i, G // 2 - 1)
                        if s4 and not s3 and s == 1 and L == 1:
                            tok(i - 1, 3)
                    if s3:
                        evac(i, GROUPS[L] // 2 - 1)
                def tok(b, r):
                    wait(act, e_otT, L, b, r + 1)
                    wait(act, e_tn if L else e_ao, L, b - 1)
                    nc.scalar.activation(TOK[:, 2 * r:2 * r + 2, :, :, :].rearrange("p a q g d -> p (a q g) d"),
                                         MI[:, :].rearrange("p (x d) -> p x d", d=32)[:, :, 0:9], ACT.Copy
                                         ).then_inc(e_tok.sem, 1)

                def normed(dst, b, q, which):
                    return nc.scalar.activation(dst, X[:, bass.ds(b * QB + q, 1), :].rearrange("p a d -> p (a d)"),
                                                ACT.Identity, scale=RSTD[:, which, q:q + 1],
                                                bias=NMR[:, which, q:q + 1])

                def evac(i, r):
                    wait(act, e_pv, L, i, 2 * r + 2)
                    wait(act, e_otT, L, i - 1)
                    nc.scalar.activation(OT[:, 2 * r:2 * r + 2, :].rearrange("p g t -> p (g t)"), OB[:, :], ACT.Copy
                                         ).then_inc(e_ot.sem, 1)
                steps(act, step)

            layer(0)

            def gelu(t, r):
                act.wait_ge(f_h, t + 1)
                if not isinstance(t, int) or t >= 2:
                    act.wait_ge(f_hT, t - 1)
                nc.scalar.activation(HS[r % 2], AB[r % 2][:, :], ACT.Gelu_apprx_tanh).then_inc(f_g, 1)

            tile_loop(act, gelu, lambda t, r: None)
            layer(1)
            for k in range(CHUNKS):
                e = k * CW // CAP
                act.wait_ge(c_xT, k + 1)
                if k >= 2:
                    act.wait_ge(c_h, k - 1)
                nc.scalar.activation(XCT[k % 2], AB[k % 2][:, 0:CW], ACT.Copy).then_inc(c_xt, 1)
                act.wait_ge(c_h, k + 1)
                if k >= 2:
                    act.wait_ge(c_y, k - 1)
                nc.scalar.activation(HC[k % 2], CS[k % 2][:, 0:CW], ACT.Relu, bias=B1T[:, e:e + 1]).then_inc(c_r, 1)

        @block.tensor
        def _(pe):
            mm = nc.tensor.matmul
            pe.wait_ge(s_ld, N_LD)
            n = [0]

            def turn(out, lhsT, rhs):
                if n[0]:
                    pe.wait_ge(s_ev, n[0])
                n[0] += 1
                return mm(out, lhsT, rhs, start=True, stop=True)

            for k, m in enumerate([PERM, PERM, IDF, IDF, PERM, PERM, IDF, IDF]):
                turn(MI[:, 0:D], wraw[k], m).then_inc(s_mm, 1)
            turn(MI[:, 0:D], wraw[0], ROT).then_inc(s_mm, 1)
            turn(MI[:, 0:D], wraw[1], ROT).then_inc(s_mm, 1)
            turn(MI[:, 0:2], PERM, BRAW)
            mm(MI[:, 2:4], ROT, BRAW, start=True, stop=True).then_inc(s_mm, 1)
            turn(MI[:, 0:NEXP], RWS, CON[0:8, 0:8])
            mm(MI[:, NEXP:2 * NEXP], B1S, CON[0:8, 0:8], start=True, stop=True).then_inc(s_mm, 1)
            pe.wait_ge(s_sv, SV_SILU)
            for L in range(2):
                turn(MI[:, 0:32], CE[L], CON[0:32, 0:32]).then_inc(s_mm, 1)
                pe.wait_ge(s_ev, 13 + 3 * L)
                for h in range(2):
                    turn(MI[0:32, 0:384], CT[L], WMOD[L][:, 384 * h:384 * h + 384]).then_inc(s_mm, 1)
            pe.wait_ge(s_sv, SV_MOD)
            for L in range(2):
                for k in range(2):
                    turn(MI[:, 0:32], MODR[L][:, D * k:D * k + D], CON[0:32, 0:32]).then_inc(s_mm, 1)
            pe.wait_ge(s_ev, 22)
            pe.wait_ge(s_cb, 8)
            pe.wait_ge(s_ones, 4)

            def layer(L):
                J = HEADS[L]

                def max_unit(b, o, u):
                    bank = AB[u % 2]
                    wait(pe, e_amax, L, b, u - 1)
                    if L == 1:
                        q, c, j = u // 16, u // 2 % 8, 2 * (u % 2)
                        mm(bank[:, :].rearrange("p (j t) -> p j t", j=2), QS[0:ROWS, o, c, q * P:q * P + P],
                           KM[0:ROWS, o, j:j + 2, c, :], start=True, stop=True).then_inc(e_amm.sem, 1)
                    elif u < 4:
                        for h in range(2):
                            mm(bank[:, 256 * h:256 * h + 256].rearrange("p (j t) -> p j t", j=2),
                               QS[0:ROWS, o, 2 * u + h, 0:P], KM[0:ROWS, o, 0:2, 2 * u + h, 0:P],
                               start=(h == 0), stop=False, skip_group_check=True)
                        mm(bank[:, :].rearrange("p (j t) -> p j t", j=4), IDB[:, :], MAB[:, :, :],
                           start=False, stop=True, skip_group_check=True).then_inc(e_amm.sem, 1)
                    else:
                        v = bank[:, :].rearrange("p (j t) -> p j t", j=2)
                        mm(v, QS[0:ROWS, o, u - 4, P:T], KM[0:ROWS, o, 0:2, u - 4, :],
                           start=True, stop=False, skip_group_check=True)
                        mm(v[:, :, P:T], IDB[:, :], MAB[:, 0:2, :],
                           start=False, stop=True, skip_group_check=True).then_inc(e_amm.sem, 1)

                def scores(b, o, G, kb):
                    n = 2 * G + kb
                    wait(pe, e_exp, L, b, n - 1)
                    w = T if L or kb == 0 else P
                    per_bank = 512 // w
                    for g, (c, j) in enumerate(heads(L, G)):
                        first = g % per_bank == 0
                        last = L == 1 and g == 3
                        m = mm(CS[n % 2][:, g * w:g * w + w], KM[:, o, j, c, kb * P:kb * P + P],
                               QS[:, o, c, T - w:T], start=first, stop=bool(L), skip_group_check=True)
                    if L == 0:
                        for bank in range(4 // per_bank):
                            v = CS[n % 2][:, 512 * bank:512 * bank + 512].rearrange("p (g t) -> p g t", t=w)
                            m = mm(v[:, :, 0:P], IDB[:, :], MCB[:, 0:per_bank, :],
                                   start=False, stop=True, skip_group_check=True)
                    m.then_inc(e_cmm.sem, 1)

                def values(b, o, G):
                    wait(pe, e_exp, L, b, 2 * G + 2)
                    if G % 2 == 0:
                        wait(pe, e_ot, L, b, G // 2)
                    for kb in range(2):
                        w = T if L or kb == 0 else P
                        for g, (c, j) in enumerate(heads(L, G)):
                            head = 2 * c + (j // 2 if L else j)
                            m = mm(OB[32 * g:32 * g + 32, (G % 2) * T + T - w:(G % 2) * T + T],
                                   VB[:, o, kb, head, :], PT[:, (2 * G + kb) % 4, g * w:g * w + w],
                                   start=(kb == 0), stop=(kb == 1), skip_group_check=True)
                    m.then_inc(e_pv.sem, 1)

                def step(i, ph):
                    s1, s2, s3, s4, s5 = stages(i)
                    free = [(e_mts, i, None) if not isinstance(i, int) or 0 <= i < NB else
                            (e_yg, i - 2, None) if i >= NB else (e_v, i + 1, None) if i > -2 else None]

                    def bank_free():
                        if free[0]:
                            wait(pe, free[0][0], L, free[0][1], free[0][2])

                    def uses(event, b, k=None):
                        free[0] = (event, b, k)

                    def turn_out(r):
                        bank_free()
                        wait(pe, e_ot, L, i - 1, r + 1)
                        for x in range(4):
                            m = nc.tensor.transpose(MI[:, P * x:P * x + P],
                                                    OT[:, 2 * r + x // 2, P * (x % 2):P * (x % 2) + P], IDF)
                        m.then_inc(e_otT.sem, 1)
                        uses(e_tok, i - 1, r + 1)

                    pending = None
                    for s in range(SLOTS):
                        if s4 and s < GROUPS[L] // 4:
                            turn_out(2 * s)
                        G = group_of(L, s) if s3 else None
                        units = list(chunk(L, s)) if s2 else []
                        if s == 0 and s2:
                            wait(pe, e_qs, L, i + 1)
                            wait(pe, e_km, L, i + 1)
                        if G == 0:
                            wait(pe, e_min, L, i)
                            wait(pe, e_v, L, i)
                        if units:
                            max_unit(i + 1, (ph + 1) % 3, units.pop(0))
                        if G is not None:
                            scores(i, ph, G, 0)
                        for u in units[0:2]:
                            max_unit(i + 1, (ph + 1) % 3, u)
                        if G is not None:
                            scores(i, ph, G, 1)
                        if s4 and s < GROUPS[L] // 4:
                            turn_out(2 * s + 1)
                        if s1 and s == 1 + L:
                            bank_free()
                            wait(pe, e_xn, L, i + 2)
                            for q in range(QB):
                                m = nc.tensor.transpose(MI[:, P * q:P * q + P], XN[:, q, :], IDF)
                            m.then_inc(e_xnT.sem, 1)
                            uses(e_hT, i + 2)
                        if s1 and s == 2 + L:
                            bank_free()
                            for k, w in enumerate((WQP, WKP)):
                                m = mm(MI[:, T * k:T * k + T], w[:, L, :], HT[:, :], start=True, stop=True)
                            m.then_inc(e_qkps.sem, 1)
                            uses(e_qk if L else e_cos, i + 2)
                        if s1 and s == 3 and L == 0:
                            bank_free()
                            for k, w in enumerate((WQR, WKR)):
                                m = mm(MI[:, T * k:T * k + T], w[:, :], HT[:, :], start=True, stop=True)
                            m.then_inc(e_qkrot.sem, 1)
                            uses(e_sin, i + 2)
                        if s5 and s == 4:
                            bank_free()
                            wait(pe, e_h2, L, i - 2)
                            for q in range(QB):
                                m = nc.tensor.transpose(MI[:, P * q:P * q + P], H2[:, q, :], IDF)
                            m.then_inc(e_h2T.sem, 1)
                            uses(e_h2t, i - 2)
                        if s1 and s == 4 + L:
                            bank_free()
                            for q in range(QB):
                                m = mm(MI[:, P * q:P * q + P], HT[:, P * q:P * q + P], WVT[:, L, :],
                                       start=True, stop=True)
                            m.then_inc(e_vps.sem, 1)
                            uses(e_v, i + 2)
                        if s5 and s == 5:
                            bank_free()
                            for q in range(QB):
                                m = mm(MI[:, NEXP * q:NEXP * q + NEXP], H2T[:, P * q:P * q + P], RWT[:, 2 * L, :],
                                       start=True, stop=True)
                            m.then_inc(e_lgps.sem, 1)
                            uses(e_lg, i - 2)
                        if s4 and s == 7:
                            bank_free()
                            wait(pe, e_ao, L, i - 1)
                            for q in range(QB):
                                m = nc.tensor.transpose(MI[:, P * q:P * q + P], AO[:, q, :], IDF)
                            m.then_inc(e_aoT.sem, 1)
                            uses(e_aot, i - 1)
                        if s5 and s == 7:
                            bank_free()
                            wait(pe, e_ohs, L, i - 2)
                            acc = [(0, LTB, 0), (1, LTB, 1), (1, ONB, 0), (2, ONB, 0), (2, ONB, 1)]
                            for k, (col, lhsT, q) in enumerate(acc):
                                m = mm(MI[:, NEXP * col:NEXP * (col + 1)], lhsT[:, :], OHS[:, q, :],
                                       start=k in (0, 1, 3), stop=k in (0, 2, 4), skip_group_check=True)
                            m.then_inc(e_posps.sem, 1)
                            uses(e_pos, i - 2, 2)
                        if s4 and s == 8:
                            bank_free()
                            wait(pe, e_aot, L, i - 1)
                            for q in range(QB):
                                m = mm(MI[:, P * q:P * q + P], AOT[:, P * q:P * q + P], WOT[:, L, :],
                                       start=True, stop=True)
                            m.then_inc(e_y.sem, 1)
                            uses(e_yg, i - 1)
                        if s2 and s == 9:
                            bank_free()
                            wait(pe, e_nm, L, i + 1, own=w_pe)
                            n = 2 * J * NC8
                            for q in range(QB):
                                m = nc.tensor.transpose(MIB[0:n, P * q:P * q + P], NM[:, q, 0:n], IDB[:, :])
                            m.then_inc(e_nmT.sem, 1)
                            uses(e_mts, i + 1)
                        for u in units[2:]:
                            max_unit(i + 1, (ph + 1) % 3, u)
                        if G is not None:
                            if pending is not None:
                                values(i, ph, pending)
                            pending = G
                    if pending is not None:
                        values(i, ph, pending)
                steps(pe, step)

            layer(0)
            pe.wait_ge(s_b3, 14)
            pe.wait_ge(s_wp, 64)

            def ahead(t, r):
                pe.wait_ge(f_x[r], 4 * (t - r) + 16)
                if not isinstance(t, int) or t >= 1:
                    pe.wait_ge(f_xt, t)
                nc.tensor.transpose(MI[:, 0:P], XIN[r], IDF).then_inc(f_xT, 1)

            def hidden(t, r, e):
                pe.wait_ge(f_xt, t + 1)
                if not isinstance(t, int) or t >= 2:
                    pe.wait_ge(f_g, t - 1)
                mm(AB[r % 2][:, :], XTT[r % 2], WFC[:, bass.ds(e * HID, HID)], start=True, stop=False)
                mm(AB[r % 2][:, :], ONE3[:, :], BFP[:, bass.ds(e * HID, HID)], start=False, stop=True
                   ).then_inc(f_h, 1)

            def turned(t, r):
                pe.wait_ge(f_g, t + 1)
                if not isinstance(t, int) or t >= 1:
                    pe.wait_ge(f_ht, t)
                for k in range(4):
                    m = nc.tensor.transpose(CS[0][:, P * k:P * k + P], HS[r % 2][:, P * k:P * k + P], IDF)
                m.then_inc(f_hT, 1)

            def project(t, r, e):
                pe.wait_ge(f_ht, t + 1)
                if not isinstance(t, int) or t >= 1:
                    pe.wait_ge(f_yo, t)
                for k in range(4):
                    mm(OB[:, 0:D], HTT[r % 2][:, P * k:P * k + P], WPR[k // 2][:, bass.ds((e + k % 2 * NEXP) * D, D)],
                       start=(k == 0), stop=False)
                mm(OB[:, 0:D], ONE3[:, :], BFP[:, bass.ds(e * D + NEXP * HID, D)], start=False, stop=True
                   ).then_inc(f_y, 1)

            def expert(t):
                return pe.value_load(TE[0:1, bass.ds(t, 1)], min_val=0, max_val=NEXP - 1)

            ahead(0, 0)
            hidden(0, 0, expert(0))
            ahead(1, 1)

            def tile(t, r):
                turned(t - 1, (r + 3) % 4)
                hidden(t, r, expert(t))
                project(t - 1, (r + 3) % 4, expert(t - 1))
                ahead(t + 1, (r + 1) % 4)

            loops = (TILES0 - 2) // 4
            with pe.Fori(1, 1 + 4 * loops - 3, 4) as i:
                for r in range(4):
                    tile(i + r, (1 + r) % 4)
            for t in range(1 + 4 * loops, TILES0 - 1):
                tile(t, t % 4)
            t = TILES0 - 1
            turned(t - 1, (t - 1) % 4)
            hidden(t, t % 4, expert(t))
            project(t - 1, (t - 1) % 4, expert(t - 1))
            turned(t, t % 4)
            project(t, t % 4, expert(t))

            layer(1)
            pe.wait_ge(c_w, 48)
            for k in range(CHUNKS):
                e = k * CW // CAP
                pe.wait_ge(c_x[k % 2], 16 * (k // 2 + 1))
                if k >= 2:
                    pe.wait_ge(c_xt, k - 1)
                for a in range(KC):
                    m = nc.tensor.transpose(AB[k % 2][:, P * a:P * a + P], XC[k % 2][:, P * a:P * a + P], IDF)
                m.then_inc(c_xT, 1)
                pe.wait_ge(c_xt, k + 1)
                if k >= 2:
                    pe.wait_ge(c_r, k - 1)
                mm(CS[k % 2][:, 0:CW], W1S[:, D * e:D * e + D], XCT[k % 2], start=True, stop=True).then_inc(c_h, 1)
                pe.wait_ge(c_r, k + 1)
                if k >= 2:
                    pe.wait_ge(c_yo, k - 1)
                dst = (OB, MI)[k % 2]
                for a in range(KC):
                    m = mm(dst[:, P * a:P * a + P], HC[k % 2][:, P * a:P * a + P], W2S[:, D * e:D * e + D],
                           start=True, stop=True)
                m.then_inc(c_y, 1)

        @block.vector
        def _(dve):
            v = nc.vector
            dve.wait_ge(s_ld, N_LD)
            v.tensor_copy(IDB[:, :], IDF).then_inc(s_cb, 1)
            v.memset(KU[ROWS:P, :, :], 1.0).then_inc(s_cb, 1)
            v.memset(QS[ROWS:P, :, :, :], 0.0).then_inc(s_cb, 1)
            v.tensor_copy(LTB[:, :], CON[:, C_LT:C_LT + P]).then_inc(s_cb, 1)
            for dst, c in ((MAB, C_MA), (MCB, C_MC)):
                v.tensor_copy(dst[:, :, :], CON[:, c:c + P].unsqueeze(1).to_broadcast([P, 4, P])).then_inc(s_cb, 1)
            v.tensor_scalar(COSS[:, :], CON[:, C_COS:C_COS + T], SCL, None, ALU.mult).then_inc(s_cb, 1)
            v.tensor_scalar(SINS[:, :], CON[:, C_SIN:C_SIN + T], SCL, None, ALU.mult).then_inc(s_cb, 1)
            c = [0]

            def link(ins):
                ins.then_inc(s_sv, 1)
                c[0] += 1
                dve.wait_ge(s_sv, c[0])

            dve.wait_ge(s_sa, 2)
            for L in range(2):
                link(v.tensor_scalar(CE[L], CE[L], 1.0, None, ALU.add))
                link(v.reciprocal(CE[L], CE[L]))
                link(v.tensor_tensor(CE[L], CE[L], CC[L], ALU.mult))
            link(v.tensor_tensor(LMP.rearrange("p (a d) -> p a d", a=2),
                                 LMB.rearrange("p (a k d) -> p a k d", a=2, k=2)[:, :, 0, :],
                                 LMB.rearrange("p (a k d) -> p a k d", a=2, k=2)[:, :, 1, :], ALU.mult))
            link(v.tensor_reduce(LMS, LMP.rearrange("p (a d) -> p a d", a=2), AX.X, ALU.add))
            for L in range(2):
                dve.wait_ge(s_ev, 15 + 3 * L)
                m = MODR[L].rearrange("p (k d) -> p k d", d=D)
                link(v.tensor_scalar(SIGN[L], m[:, 2:6:3, :], 0.0, 2.0, ALU.is_ge, ALU.mult))
                link(v.scalar_tensor_tensor(MAG[L], m[:, 2:6:3, :], -1.0, m[:, 2:6:3, :], ALU.mult, ALU.max))
                link(v.tensor_scalar(MAG[L], MAG[L], 0.25, None, ALU.max))
                R = ROWS_OUT[L]
                link(v.scalar_tensor_tensor(R[:, 0:5:4, :], SIGN[L], -1.0, MAG[L], ALU.add, ALU.mult))
                if L == 0:
                    link(v.tensor_tensor(R[:, 1, :], R[:, 0, :], BO32, ALU.mult))
                else:
                    link(v.memset(R[:, 1, :], 0.0))
                link(v.tensor_scalar(R[:, 2, :], m[:, 4, :], 1.0, None, ALU.add))
                link(v.tensor_copy(R[:, 3, :], m[:, 3, :]))
            for L in range(2):
                link(v.tensor_scalar(MODR[L][:, D:2 * D], MODR[L][:, D:2 * D], 1.0, None, ALU.add))
            dve.wait_ge(s_sa, 3)
            link(v.tensor_tensor(LMX[:, 2:3], LMX[:, 1:2], LMX[:, 0:1], ALU.subtract))
            dve.wait_ge(s_ones, 4)
            link(v.tensor_scalar(LAMSEL[:, :].rearrange("p (a b) -> p a b", b=2)[:, :, 1],
                                 NHALF[:, :], 0.5, LMX[:, 2:3], ALU.add, ALU.add))
            link(v.tensor_scalar(LAMSEL[:, :].rearrange("p (a b) -> p a b", b=2)[:, :, 1],
                                 LAMSEL[:, :].rearrange("p (a b) -> p a b", b=2)[:, :, 1],
                                 -LAMBDA_INIT, None, ALU.add))
            link(v.tensor_scalar(WSUB[:, :], WSUB[:, :], 1.0 - LAMBDA_INIT, None, ALU.mult))
            dve.wait_ge(s_ev, 22)
            dve.wait_ge(s_cb, 8)

            v.memset(RC[:, :, :], 0.0).then_inc(s_rc, 1)
            v.memset(ONB[:, :], 1.0).then_inc(s_rc, 1)
            v.memset(ZERO, 0.0).then_inc(s_rc, 1)
            v.memset(ONE3[:, :], 1.0).then_inc(s_rc, 1)
            dve.wait_ge(s_rc, 4)
            dve.wait_ge(s_fill, 16 * (NEXP * CAP // P // 8))

            def tables():
                n = [0]

                def table(ins):
                    ins.then_inc(s_tab, 1)
                    n[0] += 1
                    dve.wait_ge(s_tab, n[0])

                wait(dve, e_pos, 0, NB - 1)
                table(v.memset(ZERO[:, 0:D], 0.0))
                table(v.tensor_copy(CNTI[:, :], RC[0:1, 0, :]))
                table(v.tensor_scalar(CNT[:, :], RC[:, 0, :], float(P - 1), None, ALU.add))
                table(v.tensor_copy(NTI[:, :], CNT[:, :]))
                table(v.tensor_single_scalar(NTI[:, :], NTI[:, :], 7, op=ALU.arith_shift_right))
                table(v.tensor_copy(NTF[:, :], NTI[:, :]))
                table(v.tensor_tensor(BT8[:, :].rearrange("p (e j) -> p e j", e=NEXP),
                                      CON[:, C_TRI:C_TRI + 64].rearrange("p (e j) -> p e j", e=NEXP),
                                      NTF[:, :].unsqueeze(1).to_broadcast([P, NEXP, NEXP]), ALU.mult))
                table(v.tensor_reduce(BT[:, :], BT8[:, :].rearrange("p (e j) -> p e j", e=NEXP), AX.X, ALU.add))
                table(v.scalar_tensor_tensor(ADJ[:, :], BT[:, :], float(P), CON[:, C_REG:C_REG + NEXP],
                                             ALU.mult, ALU.subtract))
                A = KMF[0][0:1, 0:TILES0 * NEXP].rearrange("p (t e) -> p t e", e=NEXP)
                A2 = KMF[1][0:1, 0:TILES0 * NEXP].rearrange("p (t e) -> p t e", e=NEXP)
                io = CON[0:1, C_IOTA:C_IOTA + TILES0]
                bt = BT[0:1, :].unsqueeze(1).to_broadcast([1, TILES0, NEXP])
                table(v.tensor_tensor(A, io.unsqueeze(2).to_broadcast([1, TILES0, NEXP]), bt, ALU.is_ge))
                table(v.tensor_tensor(A2, A, bt, ALU.mult))
                TEF, TBF = OT[0:1, 4, 0:TILES0], OT[0:1, 5, 0:TILES0]
                table(v.tensor_reduce(TEF, A, AX.X, ALU.add))
                table(v.tensor_reduce(TBF, A2, AX.X, ALU.max))
                table(v.tensor_scalar(TEF, TEF, -1.0, None, ALU.add))
                table(v.tensor_copy(TE[:, :], TEF))
                table(v.tensor_tensor(TBF, io, TBF, ALU.subtract))
                table(v.tensor_scalar(LIM[:, :], NTF[0:1, NEXP - 1:NEXP], -1.0, 0.0, ALU.add, ALU.max))
                table(v.tensor_scalar(LIM[:, :], LIM[:, :], float(P), float((NEXP - 1) * REGION), ALU.mult, ALU.add))
                table(v.tensor_scalar(TBF, TBF, float(P), None, ALU.mult))
                table(v.scalar_tensor_tensor(TBF, TEF, float(REGION), TBF, ALU.mult, ALU.add))
                table(v.tensor_scalar(TBF, TBF, LIM[:, :], None, ALU.min))
                table(v.tensor_copy(ROW[:, :], TBF))
                OHT = WORK[:, 0:TPB * 2 * NEXP].rearrange("p (t e) -> p t e", e=NEXP)
                table(v.tensor_tensor(OHT, OH[:, :, :, :].rearrange("p t k e -> p (t k) e"),
                                      ADJ[:, :].unsqueeze(1).to_broadcast([P, TPB * 2, NEXP]), ALU.mult))
                SH = WORK[:, TPB * 16:TPB * 18]
                table(v.tensor_reduce(SH, OHT, AX.X, ALU.add))
                table(v.tensor_tensor(SH, SH, SALL[:, :, :].rearrange("p t k -> p (t k)"), ALU.add))
                table(v.tensor_copy(GI0[:, :, :].rearrange("p t k -> p (t k)"), SH))
                assert n[0] == TAB_ALL, n[0]
                m = [0]

                def part(ins):
                    ins.then_inc(s_b3, 1)
                    m[0] += 1
                    dve.wait_ge(s_b3, m[0])

                dve.wait_ge(s_bld, 32)
                dve.wait_ge(s_tail, 16 * NEXP)
                for src, lo, w in ((BP3, 0, NEXP * HID), (BP3B, NEXP * HID, NEXP * D)):
                    dst = BFP[0:3, lo:lo + w]
                    hi = PT[0:3, 0:4, :].rearrange("p a t -> p (a t)").bitcast(BF16)[:, 0:w]
                    part(v.tensor_copy(hi, src))
                    part(v.tensor_tensor(src, src, hi, ALU.subtract))
                    mid = PT[0:3, 0:4, :].rearrange("p a t -> p (a t)").bitcast(BF16)[:, w:2 * w] if w < 4096 else \
                        OT[0:3, :, :].rearrange("p a t -> p (a t)").bitcast(BF16)[:, 0:w]
                    part(v.tensor_copy(mid, src))
                    part(v.tensor_tensor(src, src, mid, ALU.subtract))
                    part(v.tensor_scalar(hi, hi, CON[0:3, 0:1], None, ALU.mult))
                    part(v.scalar_tensor_tensor(mid, mid, CON[0:3, 1:2], hi, ALU.mult, ALU.add))
                    part(v.scalar_tensor_tensor(dst, src, CON[0:3, 2:3], mid, ALU.mult, ALU.add))

            def layer(L):
                J = HEADS[L]
                MXv = MX[:, 0:QB * NC8 * J].rearrange("p (q c j) -> p q c j", q=QB, c=NC8)

                def stats(b, which, e_in, e_a, e_b, free, part):
                    if part == 0:
                        if e_in is not None:
                            wait(dve, e_in, L, b)
                        wait(dve, free, L, b - 1, own=w_dve)
                        for q in range(QB):
                            v.bn_stats(ST6[:, which, q, :], X[:, bass.ds(b * QB + q, 1), :].rearrange(
                                "p a d -> p (a d)")).then_inc(e_a.sem, 1)
                        return
                    wait(dve, e_a, L, b, own=w_dve)
                    for q in range(QB):
                        v.bn_aggr(MV[:, which, q, :], ST6[:, which, q, :]).then_inc(e_b.sem, 1)

                def step(i, ph):
                    s1, s2, s3, s4, s5 = stages(i)
                    for s in range(SLOTS):
                        units = list(chunk(L, s)) if s2 else []
                        for k in range(4):
                            for u in units[k:k + 1]:
                                maxima(i + 1, u)
                            between(i, ph, s, k)
                        if s2 and s == 8:
                            b = i + 1
                            wait(dve, e_amax, L, b)
                            wait(dve, e_nmT, L, b - 1)
                            NMv = NM[:, :, 0:2 * J * NC8].rearrange("p q (a j c) -> p q a j c", a=2, j=J)
                            v.tensor_scalar(NMv[:, :, 0].rearrange("p q j c -> p q c j"), MXv, -1.0, None, ALU.mult
                                            ).then_inc(e_nm.sem, 1)
                            wait(dve, e_nm, L, b, 1)
                            for q in range(QB):
                                v.scalar_tensor_tensor(NMv[:, q, 1].rearrange("p j c -> p c j"), MXv[:, q], -1.0,
                                                       NMv[:, q, 0].rearrange("p j c -> p c j"), ALU.mult,
                                                       ALU.subtract).then_inc(e_nm.sem, 1)

                def between(i, ph, s, k):
                    s1, s2, s3, s4, s5 = stages(i)
                    if s1 and L and s == 0:
                        combine(i + 2, k)
                    if s1 and s == L and k < 2:
                        stats(i + 2, 0, e_x2 if L else None, e_stats, e_aggr, e_xn, k)
                    if s5 and (s, k) in ((1, 2), (2, 0)):
                        stats(i - 2, 1, e_x1, e_st2, e_ag2, e_h2, s - 1)
                    if s4 and (s, k) == (1, 3):
                        wait(dve, e_tok, L, i - 1)
                        wait(dve, e_rsl if L else e_ao, L, i - 2)
                        n = GROUPS[L] * QB * 4
                        v.reciprocal(RS[:, 0:n], TOK[:, 0:GROUPS[L], :, :, :].rearrange(
                            "p a q g d -> p (a q g) d")[:, :, 8]).then_inc(e_rs.sem, 1)
                    if s4 and L == 1 and (s, k) == (3, 2):
                        b = i - 1
                        wait(dve, e_sq, L, b)
                        wait(dve, e_ms, L, b - 1)
                        v.tensor_reduce(SS[:, :], SQ[:, :, :].rearrange("p q (h d) -> p (q h) d", d=8), AX.X,
                                        ALU.add).then_inc(e_ss.sem, 1)
                    if s1 and L == 0 and s in (2, 3) and k == 1:
                        b = i + 2
                        wait(dve, e_qkps if s == 2 else e_qkrot, L, b)
                        wait(dve, e_qk, L, b - 1)
                        if s == 3:
                            wait(dve, e_split, L, b - 1)
                        dst = T1 if s == 2 else T2
                        tab = (COSS[:, :], CON[:, C_COS:C_COS + T]) if s == 2 else (SINS[:, :],
                                                                                   CON[:, C_SIN:C_SIN + T])
                        for k in range(2):
                            v.scalar_tensor_tensor(dst[:, k, :], MI[:, T * k:T * k + T],
                                                   BQK[:, 2 * (s - 2) + k:2 * (s - 2) + k + 1], tab[k],
                                                   ALU.add, ALU.mult).then_inc((e_cos if s == 2 else e_sin).sem, 1)
                    if s1 and L == 0 and (s, k) == (4, 1):
                        b = i + 2
                        wait(dve, e_vps, L, b)
                        wait(dve, e_pv, L, b - 3)
                        v.tensor_tensor(VB[:, (ph + 2) % 3, :, :, 0:8],
                                        MI[:, 0:T].rearrange("p (q h d) -> p q h d", q=QB, d=8),
                                        BVR[:, :].rearrange("p (h d) -> p h d", d=8).unsqueeze(1).to_broadcast(
                                            [P, QB, 16, 8]), ALU.add).then_inc(e_v.sem, 1)
                    if s1 and (s, k) == (5, 0 if L else 3):
                        wait(dve, e_split, L, i + 2, 3)
                        v.tensor_tensor(PARTS[:, 2, :], RES[:, :], PARTS[:, 1, :], ALU.subtract
                                        ).then_inc(e_split.sem, 1)
                    if s5 and (5, 2) <= (s, k) <= (8, 0):
                        route(i - 2, s, k)
                    if s5 and (s, k) == (8, 0):
                        place(i - 2, 0)
                    if s4 and (s, k) == (8, 2):
                        b = i - 1
                        wait(dve, e_y, L, b)
                        wait(dve, e_mb, L, b)
                        wait(dve, e_x1, L, b - 1)
                        v.tensor_tensor(YG[:, :, :], MI[:, 0:T].rearrange("p (q d) -> p q d", q=QB),
                                        MB[:, 0, :].unsqueeze(1).to_broadcast([P, QB, D]), ALU.mult
                                        ).then_inc(e_yg.sem, 1)
                    if s5 and (s, k) == (9, 1):
                        place(i - 2, 1)
                    if s1 and (s, k) in (((9, 2), (9, 3)) if L == 0 else ((7, 1), (7, 3), (8, 1), (8, 3))):
                        b, o = i + 2, (ph + 2) % 3
                        j = (s - 7) * 2 + k // 2 if L else k - 2
                        if j == 0:
                            wait(dve, e_ku, L, b)
                            wait(dve, e_cmm, L, b - 3)
                            wait(dve, e_amm, L, b - 3)
                        v.tensor_scalar(KM[:, o, j, :, :], KU[:, :, :],
                                        CON[:, C_HM + 2 * L + j:C_HM + 2 * L + j + 1], None, ALU.mult
                                        ).then_inc(e_km.sem, 1)

                def maxima(b, u):
                    wait(dve, e_amm, L, b, u + 1)
                    if u == 0:
                        wait(dve, e_nm, L, b - 1)
                    if L:
                        dst = MXv[:, u // 16, u // 2 % 8, 2 * (u % 2):2 * (u % 2) + 2]
                        src = AB[u % 2][:, :].rearrange("p (j t) -> p j t", j=2)
                    elif u < 4:
                        dst = MXv[:, 0, 2 * u:2 * u + 2, :].rearrange("p c j -> p (c j)")
                        src = AB[u % 2][:, :].rearrange("p (j t) -> p j t", j=4)
                    else:
                        dst = MXv[:, 1, u - 4, :]
                        src = AB[u % 2][:, :].rearrange("p (j t) -> p j t", j=2)
                    v.tensor_reduce(dst, src, AX.X, ALU.max).then_inc(e_amax.sem, 1)

                def route(b, s, k):
                    tiles = bass.ds(b * QB, QB)
                    cmp = CMP[:, :, :].rearrange("p q (e j) -> p q e j", e=NEXP)
                    eq = EQ[:, :, :].rearrange("p q (e j) -> p q e j", e=NEXP)
                    rk = RK[:, :].rearrange("p (q e) -> p q e", q=QB)
                    if (s, k) == (5, 2):
                        wait(dve, e_lgps, L, b)
                        wait(dve, e_wexp, L, b - 1)
                        lg = MI[:, 0:QB * NEXP].rearrange("p (q e) -> p q e", q=QB)
                        if L:
                            v.tensor_tensor(LG[:, :, :], lg, BRR[:, :].unsqueeze(1).to_broadcast([P, QB, NEXP]),
                                            ALU.add).then_inc(e_lg.sem, 1)
                        else:
                            v.tensor_copy(LG[:, :, :], lg).then_inc(e_lg.sem, 1)
                    if (s, k) == (5, 3):
                        wait(dve, e_lg, L, b)
                        lj = LG[:, :, :].unsqueeze(2).to_broadcast([P, QB, NEXP, NEXP])
                        le = LG[:, :, :].unsqueeze(3).to_broadcast([P, QB, NEXP, NEXP])
                        v.tensor_tensor(cmp, lj, le, ALU.is_gt).then_inc(e_rank.sem, 1)
                        v.tensor_tensor(eq, lj, le, ALU.is_equal).then_inc(e_rank.sem, 1)
                    if (s, k) == (6, 0):
                        wait(dve, e_rank, L, b, 2)
                        v.tensor_tensor(EQ[:, :, :], EQ[:, :, :], CON[:, C_TRI:C_TRI + 64].unsqueeze(1).to_broadcast(
                            [P, QB, 64]), ALU.mult).then_inc(e_rank.sem, 1)
                    if (s, k) == (6, 1):
                        wait(dve, e_rank, L, b, 3)
                        v.tensor_tensor(CMP[:, :, :], CMP[:, :, :], EQ[:, :, :], ALU.add).then_inc(e_rank.sem, 1)
                    if (s, k) == (6, 2):
                        wait(dve, e_rank, L, b, 4)
                        v.tensor_reduce(RK[:, :], CMP[:, :, :].rearrange("p q (e j) -> p (q e) j", e=NEXP), AX.X,
                                        ALU.add).then_inc(e_rank.sem, 1)
                    if (s, k) == (6, 3):
                        wait(dve, e_rank, L, b, 5)
                        wait(dve, e_posps, L, b - 1)
                        v.tensor_scalar(OHS[:, :, :], rk, 1.0 if L == 0 else 0.0, None, ALU.is_le
                                        ).then_inc(e_ohs.sem, 1)
                        if L == 0:
                            for n in range(2):
                                v.tensor_scalar(OH[:, tiles, n, :], rk, float(n), None, ALU.is_equal
                                                ).then_inc(e_oh.sem, 1)
                            v.tensor_reduce(M1[:, :], LG[:, :, :], AX.X, ALU.max).then_inc(e_wt.sem, 1)
                        else:
                            v.tensor_scalar(OH1[:, :, :], rk, 0.0, None, ALU.is_equal).then_inc(e_oh.sem, 1)
                            v.tensor_reduce(M1[:, :], LG[:, :, :], AX.X, ALU.max).then_inc(e_gate.sem, 1)
                    if (s, k) == (7, 0):
                        if L == 0:
                            wait(dve, e_oh, L, b)
                            v.tensor_tensor(LE[:, :, :], LG[:, :, :], OH[:, tiles, 1, :], ALU.mult
                                            ).then_inc(e_wt.sem, 1)
                        else:
                            wait(dve, e_gate, L, b, 1)
                            v.tensor_tensor(LE[:, :, :], LG[:, :, :], M1[:, :].unsqueeze(2).to_broadcast(
                                [P, QB, NEXP]), ALU.subtract).then_inc(e_wt.sem, 1)
                    if L == 0 and (s, k) == (7, 2):
                        wait(dve, e_wt, L, b, 2)
                        v.tensor_reduce(L2[:, :], LE[:, :, :], AX.X, ALU.add).then_inc(e_wt.sem, 1)
                    if L == 0 and (s, k) == (8, 0):
                        wait(dve, e_wt, L, b, 3)
                        v.tensor_tensor(L2[:, :], L2[:, :], M1[:, :], ALU.subtract).then_inc(e_wt.sem, 1)

                def place(b, part):
                    tiles = bass.ds(b * QB, QB)
                    if part:
                        place_rows(b, tiles)
                        return
                    wait(dve, e_posps, L, b)
                    wait(dve, e_pos, L, b - 1)
                    v.tensor_tensor(POS[:, :, :], MI[:, 0:QB * NEXP].rearrange("p (q e) -> p q e", q=QB),
                                    RC[:, L, :].unsqueeze(1).to_broadcast([P, QB, NEXP]), ALU.add
                                    ).then_inc(e_pos.sem, 1)
                    wait(dve, e_pos, L, b, 1)
                    v.tensor_tensor(RC[:, L, :], RC[:, L, :], MI[:, QB * NEXP:(QB + 1) * NEXP], ALU.add
                                    ).then_inc(e_pos.sem, 1)

                def place_rows(b, tiles):
                    wait(dve, e_sc, L, b - 1)
                    if L == 0:
                        v.tensor_tensor(POS[:, :, :], POS[:, :, :], CON[:, C_REG:C_REG + NEXP].unsqueeze(1
                                        ).to_broadcast([P, QB, NEXP]), ALU.add).then_inc(e_pos.sem, 1)
                        wait(dve, e_pos, L, b)
                        v.tensor_tensor(PO[:, :, :, :], OH[:, tiles, :, :],
                                        POS[:, :, :].unsqueeze(2).to_broadcast([P, QB, 2, NEXP]), ALU.mult
                                        ).then_inc(e_slot.sem, 1)
                        wait(dve, e_slot, L, b, 1)
                        v.tensor_reduce(SALL[:, tiles, :].rearrange("p q k -> p (q k)"),
                                        PO[:, :, :, :].rearrange("p q k e -> p (q k) e"), AX.X, ALU.add
                                        ).then_inc(e_slot.sem, 1)
                        wait(dve, e_slot, L, b, 2, own=w_dve)
                        v.tensor_copy(SIDX[:, :, :], SALL[:, tiles, :]).then_inc(e_slot.sem, 1)
                        wait(dve, e_wexp, L, b)
                        v.tensor_scalar(M1[:, :], W[:, :], 1.0, None, ALU.add).then_inc(e_gate.sem, 1)
                        wait(dve, e_gate, L, b, 1)
                        v.reciprocal(WALL[:, tiles, 0], M1[:, :]).then_inc(e_gate.sem, 1)
                        wait(dve, e_gate, L, b, 2)
                        v.tensor_tensor(WALL[:, tiles, 1], WALL[:, tiles, 0], W[:, :], ALU.mult
                                        ).then_inc(e_gate.sem, 1)
                        return
                    v.tensor_tensor(PO[:, :, 0, :], OH1[:, :, :], POS[:, :, :], ALU.mult).then_inc(e_slot.sem, 1)
                    v.tensor_tensor(PO[:, :, 1, :], OH1[:, :, :], CON[:, C_CAP:C_CAP + NEXP].unsqueeze(1
                                    ).to_broadcast([P, QB, NEXP]), ALU.mult).then_inc(e_slot.sem, 1)
                    wait(dve, e_wexp, L, b)
                    v.tensor_reduce(SF[:, :], LX[:, :, :], AX.X, ALU.add).then_inc(e_gate.sem, 1)
                    wait(dve, e_slot, L, b, 2)
                    v.tensor_reduce(PP[:, :], PO[:, :, 0, :], AX.X, ALU.add).then_inc(e_slot.sem, 1)
                    v.tensor_reduce(EO[:, :], PO[:, :, 1, :], AX.X, ALU.add).then_inc(e_slot.sem, 1)
                    wait(dve, e_slot, L, b, 4)
                    v.tensor_scalar(KEEP[:, :], PP[:, :], float(CAP - 1), None, ALU.is_lt).then_inc(e_slot.sem, 1)
                    v.tensor_tensor(EO[:, :], PP[:, :], EO[:, :], ALU.add).then_inc(e_slot.sem, 1)
                    wait(dve, e_slot, L, b, 6)
                    wait(dve, e_gate, L, b)
                    v.tensor_tensor(GI1[:, tiles], EO[:, :], KEEP[:, :], ALU.mult).then_inc(e_slot.sem, 1)
                    v.scalar_tensor_tensor(PP[:, :], EO[:, :], float(-NEXP * CAP), KEEP[:, :], ALU.add, ALU.mult
                                           ).then_inc(e_slot.sem, 1)
                    v.reciprocal(M1[:, :], SF[:, :]).then_inc(e_gate2.sem, 1)
                    wait(dve, e_slot, L, b, 8)
                    wait(dve, e_gate2, L, b, 1)
                    v.tensor_scalar(SIDX[:, :, 0], PP[:, :], float(NEXP * CAP), None, ALU.add).then_inc(e_slot.sem, 1)
                    wait(dve, e_gx, L, b - 1)
                    v.tensor_tensor(GALL[:, tiles], M1[:, :], KEEP[:, :], ALU.mult).then_inc(e_gate2.sem, 1)

                def combine(b, part):
                    if part == 0:
                        wait(dve, e_gat, L, b)
                        for q in range(QB):
                            v.tensor_scalar(GC[:, q, :], GY[:, q, 0, :],
                                            WALL[:, bass.ds(b * QB + q, 1), 0], None, ALU.mult).then_inc(e_cmb.sem, 1)
                    elif part == 1:
                        for q in range(QB):
                            wait(dve, e_cmb, L, b, q + 1)
                            v.scalar_tensor_tensor(GC[:, q, :], GY[:, q, 1, :], WALL[:, bass.ds(b * QB + q, 1), 1],
                                                   GC[:, q, :], ALU.mult, ALU.add).then_inc(e_cmb.sem, 1)
                    elif part == 2:
                        wait(dve, e_gbr, L, b)
                        wait(dve, e_cmb, L, b, 4)
                        v.tensor_tensor(GC[:, :, :], GC[:, :, :], GBR[:, 0, :].unsqueeze(1).to_broadcast([P, QB, D]),
                                        ALU.mult).then_inc(e_cmb.sem, 1)
                    else:
                        wait(dve, e_cmb, L, b)
                        v.tensor_tensor(X[:, bass.ds(b * QB, QB), :], X[:, bass.ds(b * QB, QB), :], GC[:, :, :],
                                        ALU.add).then_inc(e_x2.sem, 1)

                steps(dve, step)

            layer(0)
            tables()
            def tile_out(t, r):
                dve.wait_ge(f_hT, t + 1)
                if not isinstance(t, int) or t >= 2:
                    dve.wait_ge(f_y, t - 1)
                v.tensor_copy(HTT[r % 2], CS[0][:, 0:HID]).then_inc(f_ht, 1)
                dve.wait_ge(f_y, t + 1)
                if not isinstance(t, int) or t >= 4:
                    dve.wait_ge(f_st[r], 4 * (t - r))
                v.tensor_copy(YO[r], OB[:, 0:D]).then_inc(f_yo, 1)

            def tile_in(t, r):
                dve.wait_ge(f_xT, t + 1)
                if not isinstance(t, int) or t >= 2:
                    dve.wait_ge(f_h, t - 1)
                v.tensor_copy(XTT[r % 2], MI[:, 0:P]).then_inc(f_xt, 1)

            tile_loop(dve, tile_out, tile_in)
            layer(1)
            for k in range(CHUNKS):
                e = k * CW // CAP
                dve.wait_ge(c_y, k + 1)
                if k >= 2:
                    dve.wait_ge(c_st[k % 2], 16 * (k // 2))
                v.tensor_tensor(YC[k % 2].rearrange("p (a d) -> p a d", d=D),
                                (OB, MI)[k % 2][:, 0:CW].rearrange("p (a d) -> p a d", d=D),
                                B2R[:, D * e:D * e + D].unsqueeze(1).to_broadcast([P, KC, D]), ALU.add
                                ).then_inc(c_yo, 1)
            for b in range(NB):
                dve.wait_ge(o_g[b % 2], 32 * (b // 2 + 1))
                dve.wait_ge(o_gb[b % 2], 16 * (b // 2 + 1))
                for q in range(QB):
                    v.scalar_tensor_tensor(GC[:, q, :] if b % 2 else YG[:, q, :], GY[:, q, b % 2, :],
                                           GALL[:, QB * b + q:QB * b + q + 1], GBR[:, b % 2, :], ALU.mult, ALU.mult
                                           ).then_inc(o_m, 1)
                dve.wait_ge(o_m, 2 * (b + 1))
                v.tensor_tensor(X[:, QB * b:QB * b + QB, :], X[:, QB * b:QB * b + QB, :],
                                GC[:, :, :] if b % 2 else YG[:, :, :], ALU.add).then_inc(o_a, 1)

        @block.gpsimd
        def _(pool):
            g = nc.gpsimd
            g.memset(VB[:, :, :, :, :], 0.0).then_inc(s_ones, 1)
            g.memset(LAMSEL[:, :], 1.0).then_inc(s_ones, 1)
            g.memset(NHALF[:, :], -0.5).then_inc(s_ones, 1)
            pool.wait_ge(s_ones, 3)
            g.memset(VB[:, :, :, :, 8:9], 1.0).then_inc(s_ones, 1)
            pool.wait_ge(s_ones, 4)
            pool.wait_ge(s_ev, 22)
            pool.wait_ge(s_w, 32)
            pool.wait_ge(s_cb, 8)

            def layer(L):
                J, NG = HEADS[L], GROUPS[L]

                def rstd(b, which, e_ag, e_a, e_b):
                    wait(pool, e_ag, L, b, own=w_pool)
                    g.tensor_scalar(RSTD[:, which, :], MV[:, which, :, 1], EPS, None, ALU.add).then_inc(e_a.sem, 1)
                    wait(pool, e_a, L, b, own=w_pool)
                    g.tensor_tensor(RSTD[:, which, :], RSTD[:, which, :], NHALF[:, 0:QB], ALU.pow
                                    ).then_inc(e_b.sem, 1)
                    wait(pool, e_b, L, b, 1, own=w_pool)
                    g.tensor_tensor(NMR[:, which, :], MV[:, which, :, 0], RSTD[:, which, :], ALU.mult
                                    ).then_inc(e_b.sem, 1)
                    wait(pool, e_b, L, b, 2, own=w_pool)
                    g.tensor_scalar(NMR[:, which, :], NMR[:, which, :], -1.0, None, ALU.mult).then_inc(e_b.sem, 1)

                def step(i, ph):
                    s1, s2, s3, s4, s5 = stages(i)
                    if s1:
                        b = i + 2
                        wait(pool, e_xn, L, b - 1, own=w_pool)
                        rstd(b, 0, e_aggr, e_veps, e_rstd)
                    if s5:
                        b = i - 2
                        wait(pool, e_h1, L, b - 1, own=w_pool)
                        rstd(b, 1, e_ag2, e_ve2, e_rs2)
                    if s4 and L == 0:
                        b = i - 1
                        wait(pool, e_rs, L, b, own=w_pool)
                        wait(pool, e_aoT, L, b - 1, own=w_pool)
                        for q in range(QB):
                            g.tensor_tensor(AO[:, q, :].rearrange("p (a g d) -> p a g d", a=NG, d=8),
                                            TOK[:, 0:NG, q, :, 0:8],
                                            RS[:, 0:32].rearrange("p (a q g) -> p a q g", a=NG, q=QB)[
                                                :, :, q, :].unsqueeze(3).to_broadcast([P, NG, 4, 8]),
                                            ALU.mult).then_inc(e_ao.sem, 1)
                    if s4 and L == 1:
                        b = i - 1
                        wait(pool, e_rs, L, b, own=w_pool)
                        wait(pool, e_tn, L, b - 1, own=w_pool)
                        g.tensor_tensor(RSL[:, :], RS[:, :], LAMSEL[:, :], ALU.mult).then_inc(e_rsl.sem, 1)
                        wait(pool, e_rsl, L, b, own=w_pool)
                        wait(pool, e_aou, L, b - 1, own=w_pool)
                        g.tensor_tensor(TN[:, :, :, :, :].rearrange("p a q g d -> p (a q g) d"),
                                        TOK[:, :, :, :, :].rearrange("p a q g d -> p (a q g) d")[:, :, 0:8],
                                        RSL[:, :].unsqueeze(2).to_broadcast([P, 64, 8]), ALU.mult
                                        ).then_inc(e_tn.sem, 1)
                        wait(pool, e_tn, L, b, own=w_pool)
                        wait(pool, e_nrm, L, b - 1, own=w_pool)
                        for q in range(QB):
                            g.tensor_tensor(AOU[:, q, :].rearrange("p (a g d) -> p a g d", a=8, d=8),
                                            TN[:, :, q, 0:4:2, :], TN[:, :, q, 1:4:2, :], ALU.add
                                            ).then_inc(e_aou.sem, 1)
                        wait(pool, e_aou, L, b, own=w_pool)
                        wait(pool, e_ss, L, b - 1, own=w_pool)
                        g.tensor_tensor(SQ[:, :, :], AOU[:, :, :], AOU[:, :, :], ALU.mult).then_inc(e_sq.sem, 1)
                    if s5:
                        b = i - 2
                        wait(pool, e_h1, L, b, own=w_pool)
                        wait(pool, e_mb, L, b, own=w_pool)
                        g.tensor_tensor(H2[:, :, :], H2[:, :, :],
                                        MB[:, 2, :].unsqueeze(1).to_broadcast([P, QB, D]), ALU.mult
                                        ).then_inc(e_h1c.sem, 1)
                        wait(pool, e_h1c, L, b, own=w_pool)
                        g.tensor_tensor(H2[:, :, :], H2[:, :, :],
                                        MB[:, 3, :].unsqueeze(1).to_broadcast([P, QB, D]), ALU.add
                                        ).then_inc(e_h2.sem, 1)
                    if s1:
                        b = i + 2
                        if L == 0:
                            wait(pool, e_cos, L, b, own=w_pool)
                            wait(pool, e_sin, L, b, own=w_pool)
                            wait(pool, e_split, L, b - 1, own=w_pool)
                            g.tensor_tensor(QK[:, :], T1[:, :, :].rearrange("p k t -> p (k t)"),
                                            RES[:, :], ALU.add).then_inc(e_qk.sem, 1)
                        wait(pool, e_split, L, b, 1, own=w_pool)
                        g.tensor_tensor(RES[:, :], QK[:, :], PARTS[:, 0, :], ALU.subtract).then_inc(e_split.sem, 1)
                    if s4 and L == 1:
                        b = i - 1
                        wait(pool, e_ss, L, b, own=w_pool)
                        wait(pool, e_nrm, L, b - 1, own=w_pool)
                        g.tensor_scalar(RMS[:, :], SS[:, :], 1.0 / 8, EPS, ALU.mult, ALU.add).then_inc(e_ms.sem, 1)
                        wait(pool, e_ms, L, b, own=w_pool)
                        g.tensor_tensor(RMS[:, :], RMS[:, :], NHALF[:, :], ALU.pow).then_inc(e_rms.sem, 1)
                        wait(pool, e_rms, L, b, own=w_pool)
                        g.tensor_tensor(AOU[:, :, :].rearrange("p q (h d) -> p (q h) d", d=8),
                                        AOU[:, :, :].rearrange("p q (h d) -> p (q h) d", d=8),
                                        RMS[:, :].unsqueeze(2).to_broadcast([P, 32, 8]), ALU.mult
                                        ).then_inc(e_nrm.sem, 1)
                        wait(pool, e_nrm, L, b, own=w_pool)
                        wait(pool, e_aoT, L, b - 1, own=w_pool)
                        g.tensor_tensor(AO[:, :, :].rearrange("p q (h d) -> p (q h) d", d=8),
                                        AOU[:, :, :].rearrange("p q (h d) -> p (q h) d", d=8),
                                        WSUB[:, :].unsqueeze(1).to_broadcast([P, 32, 8]), ALU.mult
                                        ).then_inc(e_ao.sem, 1)
                    if s1 and L:
                        gather(i + 3)
                    if s4:
                        b = i - 1
                        xb = X[:, bass.ds(b * QB, QB), :]
                        wait(pool, e_yg, L, b, own=w_pool)
                        g.tensor_tensor(xb, xb, YG[:, :, :], ALU.add).then_inc(e_xa.sem if L == 0 else e_x1.sem, 1)
                        if L == 0:
                            wait(pool, e_xa, L, b, own=w_pool)
                            g.tensor_tensor(xb, xb, MB[:, 1, :].unsqueeze(1).to_broadcast([P, QB, D]), ALU.add
                                            ).then_inc(e_x1.sem, 1)
                    if s5:
                        b = i - 2
                        if L:
                            wait(pool, e_gate2, L, b, own=w_pool)
                            wait(pool, e_sc, L, b - 1, own=w_pool)
                            g.tensor_tensor(GX[:, :, :], H2[:, :, :], GALL[:, bass.ds(b * QB, QB)].unsqueeze(2
                                            ).to_broadcast([P, QB, D]), ALU.mult).then_inc(e_gx.sem, 1)
                            wait(pool, e_gx, L, b, own=w_pool)
                        wait(pool, e_slot, L, b, own=w_pool)
                        for q in range(QB):
                            for k in range(1 if L else 2):
                                dst = xs1 if L else xs0
                                g.indirect_dma_start(dst[:, :], bass.IndirectOffsetOnAxis(SIDX[:, q, k:k + 1], 0),
                                                     GX[:, q, :] if L else H2[:, q, :], None,
                                                     bounds_check=(NEXP * (CAP if L else REGION)) - 1,
                                                     oob_is_err=False).then_inc(e_sc.sem, 16)

                def gather(b):
                    if isinstance(b, int) and b >= NB:
                        return
                    wait(pool, e_x2, L, b - 1, own=w_pool)
                    g.tensor_copy(GIS[:, :, :], GI0[:, bass.ds(b * QB, QB), :]).then_inc(e_gis.sem, 1)
                    wait(pool, e_gis, L, b, own=w_pool)
                    for q in range(QB):
                        for k in range(2):
                            g.indirect_dma_start(GY[:, q, k, :], None, ys0[:, :],
                                                 bass.IndirectOffsetOnAxis(GIS[:, q, k:k + 1], 0),
                                                 bounds_check=TILES0 * P - 1, oob_is_err=False
                                                 ).then_inc(e_gat.sem, 16)

                if L:
                    gather(0)
                steps(pool, step)

            layer(0)
            pool.wait_ge(s_tab, TAB_ALL)
            for r in range(4):
                pool.wait_ge(f_st[r], 16 * len(range(r, TILES0, 4)))
            layer(1)
            for r in range(2):
                pool.wait_ge(c_st[r], 16 * len(range(r, CHUNKS, 2)))
            for b in range(NB):
                if b >= 2:
                    pool.wait_ge(o_m, 2 * (b - 1))
                for q in range(QB):
                    g.indirect_dma_start(GY[:, q, b % 2, :], None, ys1[:, :],
                                         bass.IndirectOffsetOnAxis(GI1[:, QB * b + q:QB * b + q + 1], 0),
                                         bounds_check=NEXP * CAP - 1, oob_is_err=False).then_inc(o_g[b % 2], 16)


_INS = (["L0_attn_x", "L0_c", "L0_wmod", "L1_c", "L1_wmod", "L0_attn_scale", "L1_attn_subln_w"]
        + ["L0_attn_" + n for n in ("Wq", "bq", "Wk", "bk", "Wv", "bv", "Wo", "bo")]
        + ["L0_ffn_" + n for n in ("router_w", "w_fc", "b_fc", "w_proj", "b_proj")]
        + ["L1_attn_" + n for n in ("Wq", "Wk", "Wv", "Wo", "lambda_q1", "lambda_k1", "lambda_q2", "lambda_k2")]
        + ["L1_ffn_" + n for n in ("Wr", "br", "W1", "b1", "W2", "b2")])


def kernel(**inputs):
    import numpy as _np
    import concourse.bacc as _bacc
    from concourse import mybir as _mybir
    from concourse.bass_utils import run_bass_kernel_spmd as _run

    nc = _bacc.Bacc("TRN2", target_bir_lowering=False, num_devices=1)
    nb = inputs["L0_attn_x"].shape[0]
    arrays, ins = {}, {}
    for name in _INS + ["const"]:
        a = constants(nb) if name == "const" else _np.ascontiguousarray(inputs[name])
        arrays[f"in_{name}"] = a
        ins[name] = nc.dram_tensor(f"in_{name}", a.shape, _mybir.dt.from_np(a.dtype), kind="ExternalInput").ap()
    out = nc.dram_tensor("out_x", (nb, T, D), F32, kind="ExternalOutput").ap()
    build(nc, nb, ins, out)
    r = _run(nc, [arrays], core_ids=[0])
    return r.results[0]["out_x"]
```

```python
from contextlib import ExitStack
import numpy as np
import concourse.bass as bass
from concourse import mybir

F32, BF16, I32 = mybir.dt.float32, mybir.dt.bfloat16, mybir.dt.int32
ALU, ACT, AX = mybir.AluOpType, mybir.ActivationFunctionType, mybir.AxisListType

P = 128
D = 128
T = 256
QB = T // P
NEXP = 8
HID = 512
EPS = 1e-5
NC8 = 8
PAIR = D // NC8
TERMS_K = [0, 1, 2, 0, 1, 0]
TERMS_Q = [0, 0, 0, 1, 1, 2]
NT = len(TERMS_K)
ROWS = NT * PAIR
BIG = -1e30
LAMBDA_INIT = float(0.8 - 0.6 * np.exp(-0.3 * 12))
HEADS = [2, 4]
HD = [8, 4]
GROUPS = [4, 8]
AUNITS = [12, 32]
SLOTS = 10
BUFS = 3
C_ID, C_LT, C_MA, C_MC, C_PERM, C_ROT, C_COS, C_SIN, C_HM = 0, 128, 256, 384, 512, 640, 768, 1024, 1280
C_TRI, C_REG, C_CAP, C_IOTA = 1286, 1350, 1358, 1366


def sizes(nb):
    tokens = nb * T
    tiles = 2 * tokens // P + NEXP - 1
    return tokens + P, tiles, tokens // NEXP, C_IOTA + tiles


def constants(nb):
    region, tiles, cap, cols = sizes(nb)
    c = np.zeros((P, cols), np.float32)
    e = np.arange(NEXP)
    c[:, C_TRI:C_TRI + 64] = (e[None, :] < e[:, None]).reshape(1, 64)
    c[:, C_REG:C_REG + NEXP] = e * region
    c[:, C_CAP:C_CAP + NEXP] = e * cap + 1
    c[:, C_IOTA:] = np.arange(tiles)
    i = np.arange(P)
    c[:, C_ID:C_ID + P] = np.eye(P)
    c[:, C_LT:C_LT + P] = i[:, None] < i[None, :]
    c[:, C_MA:C_MA + P] = np.where(i[:, None] < i[None, :], BIG, 0)
    c[:, C_MC:C_MC + P] = np.where(i[:, None] > i[None, :], BIG, 0)
    feat = 16 * (i % 8) + i // 8
    c[feat, C_PERM + i] = 1
    c[feat ^ 1, C_ROT + i] = 1
    half = np.arange(0, 8, 2, dtype=np.float32) / np.float32(8)
    freqs = (np.float32(10000.0) ** (-half)).astype(np.float32)
    ang = np.arange(T, dtype=np.float32)[:, None] * freqs
    which = (feat % 8) // 2
    c[:, C_COS:C_COS + T] = np.cos(ang).astype(np.float32)[:, which].T
    sign = np.where(feat % 2 == 0, -1, 1).astype(np.float32)
    c[:, C_SIN:C_SIN + T] = np.sin(ang).astype(np.float32)[:, which].T * sign[:, None]
    for L in range(2):
        for j in range(HEADS[L]):
            own = (i % PAIR) // HD[L] == j
            aug = (i - ROWS) % HEADS[L] == j
            c[:, C_HM + 2 * L + j] = np.where(i < ROWS, own, (i < ROWS + 2 * HEADS[L]) & aug)
    return c


class Event:

    def __init__(self, sem, nb, n, by):
        self.sem, self.nb, self.n, self.by = sem, nb, n, by

    def at(self, L, b, k=None):
        done = (self.nb * self.n[0] if L else 0) + b * self.n[L] + (self.n[L] if k is None else k)
        return done * self.by


def wait(eng, event, L, b, k=None, own=None):
    value = event.at(L, b, k)
    if not isinstance(value, int) or value > 0:
        eng.wait_ge(event.sem, value)
        if own is not None and not isinstance(value, int):
            eng.sem_inc(own, 1)


def build(nc, NB, ins, out):
    ctx = ExitStack()
    with ctx:
        def sb(name, shape, dt=F32):
            return ctx.enter_context(nc.sbuf_tensor(name, shape, dt))

        def psum(name, cols):
            return ctx.enter_context(nc.psum_tensor(name, [P, cols], F32))

        def sem(name):
            return ctx.enter_context(nc.semaphore(name))

        def event(name, n0=1, n1=None, by=1):
            return Event(sem(name), NB, [n0, n0 if n1 is None else n1], by)

        X = sb("X", [P, NB * QB, D])
        REGION, TILES0, CAP, cols = sizes(NB)
        TPB = NB * QB
        CON = sb("CON", [P, cols])
        IDB = sb("IDB", [P, P], BF16)
        MAB = sb("MAB", [P, 4, P], BF16)
        MCB = sb("MCB", [P, 4, P], BF16)
        LTB = sb("LTB", [P, P], BF16)
        COSS, SINS = sb("COSS", [P, T]), sb("SINS", [P, T])
        WQP = sb("WQP", [P, 2, D])
        WKP = sb("WKP", [P, 2, D])
        WQR, WKR = sb("WQR", [P, D]), sb("WKR", [P, D])
        WVT, WOT = sb("WVT", [P, 2, D]), sb("WOT", [P, 2, D])
        BQK = sb("BQK", [P, 4])
        BVR = sb("BVR", [P, D])
        RWT = sb("RWT", [P, 3, NEXP])
        CA1T, SAT = sb("CA1T", [P, 2, 32]), sb("SAT", [P, 2, 32])
        LAMSEL = sb("LAMSEL", [P, 64])
        WSUB = sb("WSUB", [P, 8])
        NHALF = sb("NHALF", [P, 32])
        ST6, MV = sb("ST6", [P, 2, QB, 6]), sb("MV", [P, 2, QB, 2])
        RSTD, NMR = sb("RSTD", [P, 2, QB]), sb("NMR", [P, 2, QB])
        XN = sb("XN", [P, QB, D])
        HT = sb("HT", [P, T])
        T1, QK, RES = sb("T1", [P, 2, T]), sb("QK", [P, 2 * T]), sb("RES", [P, 2 * T])
        T2 = RES[:, :].rearrange("p (k t) -> p k t", k=2)
        PARTS = sb("PARTS", [P, 3, 2 * T], BF16)
        KU = sb("KU", [P, NC8, T], BF16)
        QS = sb("QS", [P, BUFS, NC8, T], BF16)
        KM = sb("KM", [P, BUFS, 4, NC8, T], BF16)
        VB = sb("VB", [P, BUFS, QB, 16, 32])
        MX = sb("MX", [P, QB * NC8 * 4])
        NM = sb("NM", [P, QB, 64], BF16)
        MTS = sb("MTS", [P, T], BF16)
        PT = sb("PT", [P, 4, 4 * T])
        OT = sb("OT", [P, 8, T])
        TOK = sb("TOK", [P, 8, QB, 4, 9])
        RS, RSL = sb("RS", [P, 64]), sb("RSL", [P, 64])
        TN = sb("TN", [P, 8, QB, 4, 8])
        AOU, SQ, AO = sb("AOU", [P, QB, D]), sb("SQ", [P, QB, D]), sb("AO", [P, QB, D])
        SS, RMS = sb("SS", [P, 32]), sb("RMS", [P, 32])
        AOT = sb("AOT", [P, T])
        MB = sb("MB", [P, 5, D])
        YG = sb("YG", [P, QB, D])
        H2 = sb("H2", [P, QB, D])
        H2T = sb("H2T", [P, T])
        GX = sb("GX", [P, QB, D])
        LG = sb("LG", [P, QB, NEXP])
        ONB = sb("ONB", [P, P], BF16)
        BRR = sb("BRR", [P, NEXP])
        CMP, EQ = sb("CMP", [P, QB, 64]), sb("EQ", [P, QB, 64])
        RK, OHS = sb("RK", [P, QB * NEXP]), sb("OHS", [P, QB, NEXP], BF16)
        OH = sb("OH", [P, TPB, 2, NEXP])
        OH1 = sb("OH1", [P, QB, NEXP])
        M1, L2, W = sb("M1", [P, QB]), sb("L2", [P, QB]), sb("W", [P, QB])
        LE, LX = sb("LE", [P, QB, NEXP]), sb("LX", [P, QB, NEXP])
        WALL = sb("WALL", [P, TPB, 2])
        SALL = sb("SALL", [P, TPB, 2])
        GALL = sb("GALL", [P, TPB])
        RC = sb("RC", [P, 2, NEXP])
        POS = sb("POS", [P, QB, NEXP])
        PO = sb("PO", [P, QB, 2, NEXP])
        PP, EO, KEEP = sb("PP", [P, QB]), sb("EO", [P, QB]), sb("KEEP", [P, QB])
        SIDX = sb("SIDX", [P, QB, 2], I32)
        SF = sb("SF", [P, QB])
        GI0, GI1 = sb("GI0", [P, TPB, 2], I32), sb("GI1", [P, TPB], I32)
        GIS = sb("GIS", [P, QB, 2], I32)
        GY = sb("GY", [P, QB, 2, D])
        GC = sb("GC", [P, QB, D])
        GBR = sb("GBR", [P, 2, D])
        CNT, NTI, NTF = sb("CNT", [P, NEXP]), sb("NTI", [P, NEXP], I32), sb("NTF", [P, NEXP])
        BT, ADJ = sb("BT", [P, NEXP]), sb("ADJ", [P, NEXP])
        BT8 = sb("BT8", [P, 64])
        CNTI = sb("CNTI", [1, NEXP], I32)
        TE, ROW = sb("TE", [1, TILES0], I32), sb("ROW", [1, TILES0], I32)
        LIM = sb("LIM", [1, 1])
        WFC = sb("WFC", [P, NEXP * HID])
        ONE3 = sb("ONE3", [3, P], BF16)
        B1T = RWT[:, 1, :]

        KMF = [KM[:, k, :, :, :].rearrange("p a b c -> p (a b c)").bitcast(F32) for k in range(3)]
        XIN = [KMF[0][:, D * k:D * k + D] for k in range(4)]
        XTT = [KMF[0][:, 512 + D * k:640 + D * k] for k in range(2)]
        HS = [KMF[0][:, 1024 + HID * k:1024 + HID * (k + 1)] for k in range(2)]
        WPR = [KMF[k][:, 2048:4096] for k in range(2)]
        OTF = OT[:, :, :].rearrange("p a t -> p (a t)")
        HTT = [OTF[:, HID * k:HID * (k + 1)] for k in range(2)]
        YO = [OTF[:, 1024 + D * k:1152 + D * k] for k in range(4)]
        BFP = QS[0:3, :, :, :].rearrange("p b c t -> p (b c t)")[:, 0:NEXP * (HID + D)]
        KMW, KMX = KMF[(NB - 3) % 3], KMF[(NB - 2) % 3]
        W1S, W2S, B2R = KMW[:, 0:1024], KMW[:, 1024:2048], KMW[:, 2048:3072]
        CW = min(512, CAP)
        KC = CW // P
        XC = [KMX[:, 512 * k:512 * k + CW] for k in range(4)]
        XCT = [KMX[:, 2048 + 512 * k:2048 + 512 * k + CW] for k in range(2)]
        HC = [KMX[:, 3072 + 512 * k:3072 + 512 * k + CW] for k in range(2)]
        YC = [OTF[:, 512 * k:512 * k + CW] for k in range(2)]
        CHUNKS = NEXP * CAP // CW
        WORK = PT[:, :, :].rearrange("p a t -> p (a t)")
        ZERO, ZFILL = OT[:, 0, 0:D], KMF[2][:, 2048:3072]

        AB = [psum(f"AB{i}", 512) for i in range(3)]
        CS = [psum(f"CS{i}", 512) for i in range(3)]
        OB, MI = psum("OB", 512), psum("MI", 512)
        MIB = MI[:, :].bitcast(BF16)
        TURN = [MI, OB, AB[0], AB[1]]

        parts_dram = nc.dram_tensor("parts_dram", [BUFS, 2, 3, P, T], BF16, kind="Internal").ap()
        max_dram = nc.dram_tensor("max_dram", [BUFS, 64, T], BF16, kind="Internal").ap()
        xs0 = nc.dram_tensor("xs0", [NEXP * REGION, D], F32, kind="Internal").ap()
        ys0 = nc.dram_tensor("ys0", [TILES0 * P, D], F32, kind="Internal").ap()
        xs1 = nc.dram_tensor("xs1", [NEXP * CAP, D], F32, kind="Internal").ap()
        ys1 = nc.dram_tensor("ys1", [NEXP * CAP, D], F32, kind="Internal").ap()
        bias_dram = nc.dram_tensor("bias_dram", [3, NEXP * (HID + D)], BF16, kind="Internal").ap()
        mod_dram = nc.dram_tensor("mod_dram", [2, 32, 5, D], F32, kind="Internal").ap()

        e_stats, e_aggr, e_veps, e_rstd = event("e_stats", 2), event("e_aggr", 2), event("e_veps"), event("e_rstd", 3)
        e_xn, e_xnT, e_hT = event("e_xn", 2), event("e_xnT"), event("e_hT")
        e_qkps, e_cos, e_qkrot, e_sin, e_qk = (event("e_qkps"), event("e_cos", 2, 0), event("e_qkrot", 1, 0),
                                               event("e_sin", 2, 0), event("e_qk"))
        e_split = event("e_split", 4)
        e_pout, e_qs, e_ku = event("e_pout", 3, by=16), event("e_qs", 6, by=16), event("e_ku", 3, by=16)
        e_km = event("e_km", 2, 4)
        e_vps, e_v = event("e_vps"), event("e_v")
        e_amm, e_amax = event("e_amm", *AUNITS), event("e_amax", *AUNITS)
        e_nm, e_nmT, e_mts = event("e_nm", 3), event("e_nmT"), event("e_mts")
        e_mout, e_min = event("e_mout", by=16), event("e_min", by=16)
        e_cmm, e_exp = event("e_cmm", 12, 32), event("e_exp", 12, 32)
        e_pv, e_ot = event("e_pv", *GROUPS), event("e_ot", 2, 4)
        e_otT, e_tok = event("e_otT", 2, 4), event("e_tok", 2, 4)
        e_rs, e_rsl, e_tn, e_aou, e_sq, e_ss = (event("e_rs"), event("e_rsl", 0, 1), event("e_tn", 0, 1),
                                                event("e_aou", 0, 2), event("e_sq", 0, 1), event("e_ss", 0, 1))
        e_ms, e_rms, e_nrm, e_ao = event("e_ms", 0, 1), event("e_rms", 0, 1), event("e_nrm", 0, 1), event("e_ao", 2, 1)
        e_aoT, e_aot, e_y, e_mb, e_yg = (event("e_aoT"), event("e_aot"), event("e_y"), event("e_mb", by=16),
                                         event("e_yg"))
        e_xa, e_x1 = event("e_xa", 1, 0), event("e_x1")
        e_st2, e_ag2, e_ve2, e_rs2 = event("e_st2", 2), event("e_ag2", 2), event("e_ve2"), event("e_rs2", 3)
        e_h1, e_h1c, e_h2 = event("e_h1", 2), event("e_h1c"), event("e_h2")
        e_rank = event("e_rank", 5)
        e_oh, e_ohs, e_wt = event("e_oh", 2, 1), event("e_ohs"), event("e_wt", 4, 1)
        e_wexp, e_gate, e_gate2 = event("e_wexp"), event("e_gate", 3, 2), event("e_gate2", 0, 2)
        e_posps, e_pos, e_slot = event("e_posps"), event("e_pos", 3, 2), event("e_slot", 3, 9)
        e_sc, e_gx = event("e_sc", 4, 2, 16), event("e_gx", 0, 1)
        e_gis, e_gat, e_gbr = event("e_gis", 0, 1), event("e_gat", 0, 4, 16), event("e_gbr", 0, 1, 16)
        e_wy, e_cmb, e_x2 = event("e_wy", 0, 2), event("e_cmb", 0, 3), event("e_x2", 0, 1)
        e_h2T, e_h2t, e_lgps, e_lg = event("e_h2T"), event("e_h2t"), event("e_lgps"), event("e_lg")
        w_pool, w_pe, w_dve, w_sp = sem("w_pool"), sem("w_pe"), sem("w_dve"), sem("w_sp")
        s_ld, s_w, s_ones = sem("s_ld"), sem("s_w"), sem("s_ones")
        s_cb, s_mm, s_ev, s_sv, s_sa = sem("s_cb"), sem("s_mm"), sem("s_ev"), sem("s_sv"), sem("s_sa")
        s_fill, s_wp, s_bfp, s_x0, s_x = sem("s_fill"), sem("s_wp"), sem("s_bfp"), sem("s_x0"), sem("s_x")
        s_rc = sem("s_rc")
        s_tab, s_b3, s_bld, s_tail = sem("s_tab"), sem("s_b3"), sem("s_bld"), sem("s_tail")
        f_x, f_st = [sem(f"f_x{r}") for r in range(4)], [sem(f"f_st{r}") for r in range(4)]
        c_x, c_st = [sem(f"c_x{r}") for r in range(4)], [sem(f"c_st{r}") for r in range(2)]
        o_g, o_gb = [sem(f"o_g{r}") for r in range(2)], [sem(f"o_gb{r}") for r in range(2)]
        f_xT, f_xt, f_h, f_g, f_hT, f_ht, f_y, f_yo = (sem("f_xT"), sem("f_xt"), sem("f_h"),
                                                                  sem("f_g"), sem("f_hT"), sem("f_ht"), sem("f_y"),
                                                                  sem("f_yo"))
        c_w, c_xT, c_xt, c_h, c_r, c_y, c_yo = (sem("c_w"), sem("c_xT"), sem("c_xt"),
                                                           sem("c_h"), sem("c_r"), sem("c_y"), sem("c_yo"))
        o_m, o_a, o_st = sem("o_m"), sem("o_a"), sem("o_st")

        IDF = CON[:, C_ID:C_ID + P]
        PERM, ROT = CON[:, C_PERM:C_PERM + P], CON[:, C_ROT:C_ROT + P]

        WRAW = KM[:, 0, :, :, :].rearrange("p a b c -> p (a b c)").bitcast(F32)
        wraw = [WRAW[:, k * D:(k + 1) * D] for k in range(8)]
        WMOD = [WRAW[:, 1024 + 768 * L:1024 + 768 * (L + 1)] for L in range(2)]
        S = KM[:, 1, :, :, :].rearrange("p a b c -> p (a b c)").bitcast(F32)
        CC = [S[0:32, 128 * L:128 * L + 128] for L in range(2)]
        CE = [S[0:32, 256 + 128 * L:384 + 128 * L] for L in range(2)]
        MODR = [S[0:32, 512 + 768 * L:512 + 768 * (L + 1)] for L in range(2)]
        ROWS_OUT = [S[0:32, 2048 + 640 * L:2048 + 640 * (L + 1)].rearrange("p (k d) -> p k d", d=D) for L in range(2)]
        S2 = KM[:, 2, :, :, :].rearrange("p a b c -> p (a b c)").bitcast(F32)
        SIGN = [S2[0:32, 256 * L:256 * (L + 1)].rearrange("p (k d) -> p k d", d=D) for L in range(2)]
        MAG = [S2[0:32, 512 + 256 * L:512 + 256 * (L + 1)].rearrange("p (k d) -> p k d", d=D) for L in range(2)]
        CT = [S2[:, 1024 + 32 * L:1056 + 32 * L] for L in range(2)]
        BRAW = S2[:, 1100:1102]
        BO32 = S2[0:32, 1152:1280]
        LMB = S2[:, 1300:1316]
        LMP = S2[:, 1320:1328]
        LMS = S2[:, 1330:1332]
        LMX = S2[:, 1334:1337]
        RWS = S2[0:8, 1344:1472]
        SCL = S2[:, 1480:1481]
        B1S = S2[0:8, 1500:1628]
        BW = NEXP * (HID + D) // P
        BIAS, BRES = S2[:, 1700:1700 + BW], S2[:, 1740:1740 + BW]
        BPARTS = S2[:, 1800:1800 + 3 * BW // 2].bitcast(BF16).rearrange("p (k w) -> p k w", k=3)
        SV_SILU, SV_LAM, SV_MOD = 6, 8, 24

        block = ctx.enter_context(nc.Block())
        loop_first, loop_steps = 2, (NB - 4) // 3 * 3
        attn_w = ["Wq", "Wk", "Wv", "Wo"]

        def steps(eng, step):
            for i in range(-2, loop_first):
                step(i, i % 3)
            with eng.Fori(loop_first, loop_first + loop_steps - 2, 3) as i:
                for r in range(3):
                    step(i + r, (loop_first + r) % 3)
            for i in range(loop_first + loop_steps, NB + 2):
                step(i, i % 3)

        def stages(i):
            if not isinstance(i, int):
                return True, True, True, True, True
            return i + 2 < NB, 0 <= i + 1 < NB, 0 <= i < NB, 0 <= i - 1 < NB, 0 <= i - 2 < NB

        def chunk(L, s):
            per = [[0, 2, 4, 6, 8, 9, 10, 11, 12, 12], [0, 4, 8, 12, 16, 20, 24, 27, 30, 32]][L]
            return range(per[s], per[s + 1]) if s < 9 else range(0)

        def group_of(L, s):
            if L == 0:
                return s // 2 if s < 8 and s % 2 == 1 else None
            return s - 1 if 1 <= s < 9 else None

        def heads(L, G):
            return [(G, g) if L else (2 * G + g // 2, g % 2) for g in range(4)]

        def banks(L):
            last = [(1, 0, 2, T), (1, 2, 4, T)] if L else [(1, 0, 4, P)]
            return [(0, 0, 2, T), (0, 2, 4, T)] + last

        loads = []
        TAB_CNT, TAB_ALL = 2, 26

        def tile_loop(eng, behind, ahead):
            for t in range(2):
                ahead(t, t)
            n = (TILES0 - 4) // 4 * 4
            for t in range(2, 4):
                behind(t - 2, t - 2)
                ahead(t, t)
            with eng.Fori(4, 4 + n - 3, 4) as i:
                for r in range(4):
                    behind(i + r - 2, (r + 2) % 4)
                    ahead(i + r, r)
            for t in range(4 + n, TILES0 + 2):
                behind(t - 2, (t - 2) % 4)
                if t < TILES0:
                    ahead(t, t % 4)

        @block.sync
        def _(sp):
            def load(dst, src):
                sp.dma_start(dst, src).then_inc(s_ld, 16)
                loads.append(1)

            load(CON[:, :], ins["const"])
            for L in range(2):
                for k, w in enumerate(attn_w):
                    load(wraw[4 * L + k], ins[f"L{L}_attn_{w}"])
                load(WMOD[L], ins[f"L{L}_wmod"])
                load(CC[L], ins[f"L{L}_c"])
            load(BRAW[:, 0:1], ins["L0_attn_bq"].rearrange("(p a) -> p a", a=1))
            load(BRAW[:, 1:2], ins["L0_attn_bk"].rearrange("(p a) -> p a", a=1))
            load(BVR[:, :], ins["L0_attn_bv"].partition_broadcast(P))
            load(BO32, ins["L0_attn_bo"].partition_broadcast(32))
            load(SCL, ins["L0_attn_scale"].partition_broadcast(P))
            load(RWS, ins["L0_ffn_router_w"])
            load(RWT[:, 2, :], ins["L1_ffn_Wr"])
            for k, n in enumerate(["q1", "k1", "q2", "k2"]):
                load(LMB[:, 4 * k:4 * k + 4], ins[f"L1_attn_lambda_{n}"].partition_broadcast(P))
            load(WSUB[:, :], ins["L1_attn_subln_w"].partition_broadcast(P))
            load(BRR[:, :], ins["L1_ffn_br"].partition_broadcast(P))
            load(B1S, ins["L1_ffn_b1"])
            load(BIAS[:, 0:NEXP * HID // P], ins["L0_ffn_b_fc"].rearrange("e h -> (e h)").rearrange("(p c) -> p c", p=P))
            load(BIAS[:, NEXP * HID // P:], ins["L0_ffn_b_proj"].rearrange("e h -> (e h)").rearrange("(p c) -> p c", p=P))
            xin = ins["L0_attn_x"].rearrange("b (q p) d -> p (b q) d", p=P)
            step_b = 4
            for b in range(0, NB, step_b):
                sp.dma_start(X[:, QB * b:QB * (b + step_b), :], xin[:, QB * b:QB * (b + step_b), :]
                             ).then_inc(s_x if b else s_x0, 16)
            sp.wait_ge(s_b3, 5)
            for k in range(3):
                for lo, hi in ((0, NEXP * HID), (NEXP * HID, NEXP * (HID + D))):
                    sp.dma_start(bias_dram[k, lo:hi].rearrange("(p c) -> p c", p=P),
                                 BPARTS[:, k, lo // P:hi // P]).then_inc(s_bld, 16)
            sp.dma_start(WFC[:, :].rearrange("p (e h) -> p e h", e=NEXP),
                         ins["L0_ffn_w_fc"].rearrange("e c h -> c e h")).then_inc(s_wp, 16)
            sp.wait_ge(s_sv, SV_MOD)
            for L in range(2):
                sp.dma_start(mod_dram[L], ROWS_OUT[L]).then_inc(s_w, 16)
            sp.wait_ge(s_w, 32)
            sp.wait_ge(s_ev, 22)
            for k in range(2):
                for h in range(2):
                    c = NEXP * D * h
                    sp.dma_start(WPR[k][:, c:c + NEXP * D].rearrange("p (e d) -> p e d", e=NEXP),
                                 ins["L0_ffn_w_proj"][:, P * (2 * k + h):P * (2 * k + h + 1), :].rearrange(
                                     "e p d -> p e d")).then_inc(s_wp, 16)
            sp.wait_ge(s_rc, 3)
            rows = NEXP * CAP // P
            for r in range(0, rows, 8):
                sp.dma_start(xs1[r * P:(r + 8) * P, :].rearrange("(p a) d -> p (a d)", a=8), ZFILL
                             ).then_inc(s_fill, 16)

            def layer(L):
                J = HEADS[L]

                def step(i, ph):
                    s1, s2, s3, s4, s5 = stages(i)
                    if s3:
                        n = 2 * J * NC8
                        wait(sp, e_mts, L, i, own=w_sp)
                        wait(sp, e_min, L, i - 3)
                        sp.dma_start(max_dram[ph, 0:n, :], MTS[0:n, :]).then_inc(e_mout.sem, 16)
                        wait(sp, e_mout, L, i, own=w_sp)
                        wait(sp, e_cmm, L, i - 3, own=w_sp)
                        sp.dma_start(QS[ROWS:ROWS + 2 * J, ph, :, :].rearrange("p c t -> p (c t)"),
                                     max_dram[ph, 0:n, :].rearrange("(r c) t -> r (c t)", c=NC8)
                                     ).then_inc(e_min.sem, 16)
                    if s4:
                        b = i - 1
                        wait(sp, e_h2, L, b - 1, own=w_sp)
                        sp.dma_start(MB[:, :, :].rearrange("p k d -> p (k d)"),
                                     bcast_rows(mod_dram, L, b)).then_inc(e_mb.sem, 16)
                    if L and isinstance(i, int) and i == NB:
                        wait(sp, e_cmm, L, NB - 3)
                        wait(sp, e_amm, L, NB - 3)
                        for dst, w in ((W1S, "W1"), (W2S, "W2")):
                            sp.dma_start(dst.rearrange("p (e f) -> p e f", e=NEXP),
                                         ins[f"L1_ffn_{w}"].rearrange("e c f -> c e f")).then_inc(c_w, 16)
                        sp.dma_start(B2R, ins["L1_ffn_b2"].rearrange("e f -> (e f)").partition_broadcast(P)
                                     ).then_inc(c_w, 16)
                    if s1 and L:
                        load_gb(i + 3)
                    if s1:
                        b, o = i + 2, (ph + 2) % 3
                        wait(sp, e_split, L, b)
                        wait(sp, e_qs, L, b - 3)
                        wait(sp, e_ku, L, b - 3, own=w_sp)
                        for part in range(3):
                            sp.dma_start(parts_dram[o, :, part].rearrange("q p t -> p q t"),
                                         PARTS[:, part, :].rearrange("p (q t) -> p q t", q=2)
                                         ).then_inc(e_pout.sem, 16)
                        wait(sp, e_pout, L, b, own=w_sp)
                        wait(sp, e_km, L, b - 1, own=w_sp)
                        for t0, n in ((0, 3), (3, 2), (5, 1)):
                            src = parts_dram[o, 1, TERMS_K[t0]:TERMS_K[t0] + n]
                            sp.dma_start(KU[PAIR * t0:PAIR * (t0 + n), :, :].rearrange("p c t -> p (c t)"),
                                         src.rearrange("a (r c) t -> (a r) (c t)", c=NC8)).then_inc(e_ku.sem, 16)
                        wait(sp, e_cmm, L, b - 3)
                        wait(sp, e_amm, L, b - 3, own=w_sp)
                        for t in range(NT):
                            sp.dma_start(QS[PAIR * t:PAIR * (t + 1), o, :, :].rearrange("p c t -> p (c t)"),
                                         parts_dram[o, 0, TERMS_Q[t]].rearrange("(r c) t -> r (c t)", c=NC8)
                                         ).then_inc(e_qs.sem, 16)

                def load_gb(b):
                    if isinstance(b, int) and b >= NB:
                        return
                    wait(sp, e_x2, L, b - 1, own=w_sp)
                    sp.dma_start(GBR[:, 0, :], bcast_rows(mod_dram, 0, b, 4)).then_inc(e_gbr.sem, 16)

                if L:
                    load_gb(0)
                steps(sp, step)

            def bcast_rows(dram, L, b, k=None):
                row = dram[L, bass.ds(b, 1)] if not isinstance(b, int) else dram[L, b:b + 1]
                if k is not None:
                    row = row[:, k:k + 1, :]
                return row.rearrange("b k d -> b (k d)").to_broadcast([P, (5 if k is None else 1) * D])

            layer(0)
            sp.wait_ge(e_cmm.sem, e_cmm.at(0, NB - 1))
            sp.wait_ge(s_bld, 96)
            sp.dma_start(BFP, bias_dram[:, :]).then_inc(s_bfp, 16)
            sp.wait_ge(s_tab, TAB_CNT)
            for e in range(NEXP):
                n = sp.value_load(CNTI[0:1, e:e + 1], min_val=0, max_val=NB * T)
                sp.dma_start(xs0[bass.ds(n + e * REGION, P), :], ZERO).then_inc(s_tail, 16)
            sp.wait_ge(s_tab, TAB_ALL)
            sp.wait_ge(s_tail, 16 * NEXP)
            sp.wait_ge(e_sc.sem, e_sc.at(0, NB - 1))

            def tile_load(t, r):
                if not isinstance(t, int) or t >= 4:
                    sp.wait_ge(f_xT, t - 3)
                row = sp.value_load(ROW[0:1, bass.ds(t, 1)], min_val=0, max_val=(NEXP - 1) * REGION + NB * T)
                sp.dma_start(XIN[r], xs0[bass.ds(row, P), :]).then_inc(f_x[r], 16)

            def tile_store(t, r):
                sp.wait_ge(f_yo, t + 1)
                sp.dma_start(ys0[bass.ds(t * P, P), :], YO[r]).then_inc(f_st[r], 16)

            for t in range(4):
                tile_load(t, t)
            n = (TILES0 - 4) // 4 * 4
            with sp.Fori(4, 4 + n - 3, 4) as i:
                for r in range(4):
                    tile_load(i + r, r)
                    tile_store(i + r - 4, r)
            for t in range(4 + n, TILES0 + 4):
                if t < TILES0:
                    tile_load(t, t % 4)
                tile_store(t - 4, t % 4)
            layer(1)
            sp.wait_ge(e_sc.sem, e_sc.at(1, NB - 1))
            sp.wait_ge(e_cmm.sem, e_cmm.at(1, NB - 1))
            for k in range(CHUNKS + 4):
                if k >= 4:
                    sp.wait_ge(c_yo, k - 3)
                    sp.dma_start(ys1[(k - 4) * CW:(k - 3) * CW, :].rearrange("(a p) d -> p a d", p=P),
                                 YC[k % 2].rearrange("p (a d) -> p a d", d=D)).then_inc(c_st[k % 2], 16)
                if k < CHUNKS:
                    if k >= 4:
                        sp.wait_ge(c_xT, k - 3)
                    sp.dma_start(XC[k % 4].rearrange("p (a d) -> p a d", d=D),
                                 xs1[k * CW:(k + 1) * CW, :].rearrange("(a p) d -> p a d", p=P)
                                 ).then_inc(c_x[k % 4], 16)
            for b in range(NB + 1):
                if b < NB:
                    if b >= 2:
                        sp.wait_ge(o_m, 2 * (b - 1))
                    sp.dma_start(GBR[:, b % 2, :], bcast_rows(mod_dram, 1, b, 4)).then_inc(o_gb[b % 2], 16)
                if b >= 1:
                    sp.wait_ge(o_a, b)
                    sp.dma_start(out[b - 1].rearrange("(q p) d -> p q d", p=P),
                                 X[:, QB * (b - 1):QB * b, :]).then_inc(o_st, 16)
            sp.wait_ge(o_st, 16 * NB)

        N_LD = 16 * len(loads)

        @block.scalar
        def _(act):
            act.wait_ge(s_ld, N_LD)
            for L in range(2):
                nc.scalar.activation(CE[L], CC[L], ACT.Exp, scale=-1.0).then_inc(s_sa, 1)
            n = 0
            outs = [(WQP[:, 0, :], D), (WKP[:, 0, :], D), (WVT[:, 0, :], D), (WOT[:, 0, :], D),
                    (WQP[:, 1, :], D), (WKP[:, 1, :], D), (WVT[:, 1, :], D), (WOT[:, 1, :], D),
                    (WQR[:, :], D), (WKR[:, :], D), (BQK[:, :], 4), (RWT[:, 0:2, :].rearrange("p a e -> p (a e)"), 2 * NEXP)]
            for k, (dst, w) in enumerate(outs):
                act.wait_ge(s_mm, k + 1)
                if k == 4:
                    nc.scalar.activation(dst, TURN[k % 4][:, 0:w], ACT.Copy, scale=float(HD[1]) ** -0.5).then_inc(s_ev, 1)
                else:
                    nc.scalar.activation(dst, TURN[k % 4][:, 0:w], ACT.Copy).then_inc(s_ev, 1)
            for L in range(2):
                act.wait_ge(s_mm, 13 + 3 * L)
                nc.scalar.activation(CT[L], TURN[(12 + 3 * L) % 4][:, 0:32], ACT.Copy).then_inc(s_ev, 1)
                for h in range(2):
                    act.wait_ge(s_mm, 14 + 3 * L + h)
                    nc.scalar.activation(MODR[L][:, 384 * h:384 * h + 384], TURN[(13 + 3 * L + h) % 4][0:32, 0:384], ACT.Copy
                                         ).then_inc(s_ev, 1)
            for k in range(4):
                act.wait_ge(s_mm, 19 + k)
                dst = (SAT if k % 2 == 0 else CA1T)[:, k // 2, :]
                nc.scalar.activation(dst, TURN[(18 + k) % 4][:, 0:32], ACT.Copy).then_inc(s_ev, 1)
            act.wait_ge(s_sv, SV_LAM)
            nc.scalar.activation(LMX[:, 0:2], LMS, ACT.Exp).then_inc(s_sa, 1)

            def layer(L):
                def step(i, ph):
                    s1, s2, s3, s4, s5 = stages(i)
                    for s in range(SLOTS):
                        if s == 0 and L == 1 and isinstance(i, int) and i == -2:
                            weigh(i + 2)
                        if s4 and s < GROUPS[L] // 4:
                            tok(i - 1, 2 * s)
                            if s == 0:
                                tok(i - 1, 1)
                        G = group_of(L, s) if s3 else None
                        if L == 0:
                            chores(i, ph, s)
                        if G is not None:
                            numerators(i, G, 0)
                        if s4 and s == 1 and L == 1:
                            tok(i - 1, 3)
                        if L == 1:
                            chores(i, ph, s)
                        if G is not None:
                            numerators(i, G, 1)
                            if G >= 2 and G % 2 == 0:
                                evac(i, G // 2 - 1)
                    if s3:
                        evac(i, GROUPS[L] // 2 - 1)
                def chores(i, ph, s):
                    s1, s2, s3, s4, s5 = stages(i)
                    if s1 and s == 1 + L:
                        b = i + 2
                        wait(act, e_rstd, L, b)
                        wait(act, e_xnT, L, b - 1)
                        for q in range(QB):
                            normed(XN[:, q, :], b, q, 0).then_inc(e_xn.sem, 1)
                    if s5 and s == 3:
                        b = i - 2
                        wait(act, e_rs2, L, b)
                        wait(act, e_h2T, L, b - 1)
                        wait(act, e_gx if L else e_sc, L, b - 1)
                        for q in range(QB):
                            normed(H2[:, q, :], b, q, 1).then_inc(e_h1.sem, 1)
                    if s1 and s == 1 + L:
                        b = i + 2
                        col = bass.ds(b, 1)
                        wait(act, e_xnT, L, b)
                        wait(act, e_vps, L, b - 1)
                        nc.scalar.activation(HT[:, :], MI[:, 0:T], ACT.Identity, scale=CA1T[:, L, col],
                                             bias=SAT[:, L, col]).then_inc(e_hT.sem, 1)
                    if s1 and s == 3 and L == 1:
                        wait(act, e_qkps, L, i + 2)
                        wait(act, e_split, L, i + 1)
                        nc.scalar.activation(QK[:, :], MI[:, :], ACT.Copy).then_inc(e_qk.sem, 1)
                    if s4 and s == 7:
                        wait(act, e_aoT, L, i - 1)
                        wait(act, e_y, L, i - 2)
                        nc.scalar.activation(AOT[:, :], MI[:, 0:T], ACT.Copy).then_inc(e_aot.sem, 1)
                    if s1 and s == 5 and L == 1:
                        b = i + 2
                        wait(act, e_vps, L, b)
                        wait(act, e_pv, L, b - 3)
                        nc.scalar.activation(VB[:, (ph + 2) % 3, :, :, 0:8],
                                             MI[:, 0:T].rearrange("p (q h d) -> p q h d", q=QB, d=8),
                                             ACT.Copy).then_inc(e_v.sem, 1)
                    if s5 and s == 4:
                        wait(act, e_h2T, L, i - 2)
                        wait(act, e_lgps, L, i - 3)
                        nc.scalar.activation(H2T[:, :], MI[:, 0:T], ACT.Copy).then_inc(e_h2t.sem, 1)
                    if s1 and s == 4 - L:
                        wait(act, e_qk, L, i + 2)
                        wait(act, e_pout, L, i + 1)
                        nc.scalar.activation(PARTS[:, 0, :], QK[:, :], ACT.Copy).then_inc(e_split.sem, 1)
                    if s == 9 and L == 1 and (not isinstance(i, int) or i + 3 < NB):
                        weigh(i + 3)
                    if s5 and s == 8:
                        b = i - 2
                        wait(act, e_wt, L, b)
                        wait(act, e_gate, L, b - 1)
                        src, dst = (L2[:, :], W[:, :]) if L == 0 else (LE[:, :, :], LX[:, :, :])
                        nc.scalar.activation(dst, src, ACT.Exp).then_inc(e_wexp.sem, 1)
                    if s1 and s == 5 - L:
                        wait(act, e_split, L, i + 2, 2)
                        nc.scalar.activation(PARTS[:, 1, :], RES[:, :], ACT.Copy).then_inc(e_split.sem, 1)
                    if s2 and s == 9:
                        wait(act, e_nmT, L, i + 1)
                        wait(act, e_mout, L, i)
                        n = 2 * HEADS[L] * NC8
                        nc.scalar.activation(MTS[0:n, :], MIB[0:n, 0:T], ACT.Copy).then_inc(e_mts.sem, 1)

                def numerators(i, G, part):
                    for m, (kb, g0, g1, w) in enumerate(banks(L)):
                        if m // 2 != part:
                            continue
                        n = len(banks(L)) * G + m
                        wait(act, e_cmm, L, i, n + 1)
                        if G < 2:
                            wait(act, e_pv, L, i - 1, GROUPS[L] - 1 + G)
                        else:
                            wait(act, e_pv, L, i, G - 1)
                        nc.scalar.activation(PT[:, (2 * G + kb) % 4, g0 * w:g1 * w], CS[n % 3][:, :], ACT.Exp
                                             ).then_inc(e_exp.sem, 1)

                def tok(b, r):
                    wait(act, e_otT, L, b, r + 1)
                    wait(act, e_tn if L else e_ao, L, b - 1)
                    nc.scalar.activation(TOK[:, 2 * r:2 * r + 2, :, :, :].rearrange("p a q g d -> p (a q g) d"),
                                         MI[:, :].rearrange("p (x d) -> p x d", d=32)[:, :, 0:9], ACT.Copy
                                         ).then_inc(e_tok.sem, 1)

                def weigh(b):
                    wait(act, e_gat, L, b)
                    wait(act, e_x2, L, b - 1)
                    for q in range(QB):
                        nc.scalar.activation(GC[:, q, :], GY[:, q, 0, :], ACT.Copy,
                                             scale=WALL[:, bass.ds(b * QB + q, 1), 0]).then_inc(e_wy.sem, 1)

                def normed(dst, b, q, which):
                    return nc.scalar.activation(dst, X[:, bass.ds(b * QB + q, 1), :].rearrange("p a d -> p (a d)"),
                                                ACT.Identity, scale=RSTD[:, which, q:q + 1],
                                                bias=NMR[:, which, q:q + 1])

                def evac(i, r):
                    wait(act, e_pv, L, i, 2 * r + 2)
                    wait(act, e_otT, L, i - 1)
                    nc.scalar.activation(OT[:, 2 * r:2 * r + 2, :].rearrange("p g t -> p (g t)"), OB[:, :], ACT.Copy
                                         ).then_inc(e_ot.sem, 1)
                steps(act, step)

            layer(0)

            def gelu(t, r):
                act.wait_ge(f_h, t + 1)
                if not isinstance(t, int) or t >= 2:
                    act.wait_ge(f_hT, t - 1)
                nc.scalar.activation(HS[r % 2], AB[r % 2][:, :], ACT.Gelu_apprx_tanh).then_inc(f_g, 1)

            tile_loop(act, gelu, lambda t, r: None)
            layer(1)
            for k in range(CHUNKS + 1):
                if k < CHUNKS:
                    act.wait_ge(c_xT, k + 1)
                    if k >= 2:
                        act.wait_ge(c_h, k - 1)
                    nc.scalar.activation(XCT[k % 2], AB[k % 2][:, 0:CW], ACT.Copy).then_inc(c_xt, 1)
                if k >= 1:
                    n = k - 1
                    e = n * CW // CAP
                    act.wait_ge(c_h, n + 1)
                    if n >= 2:
                        act.wait_ge(c_y, n - 1)
                    nc.scalar.activation(HC[n % 2], CS[n % 2][:, 0:CW], ACT.Relu, bias=B1T[:, e:e + 1]
                                         ).then_inc(c_r, 1)

        @block.tensor
        def _(pe):
            mm = nc.tensor.matmul
            pe.wait_ge(s_ld, N_LD)
            n = [0]

            def turn(rows, lo, hi, lhsT, rhs):
                if n[0] >= 4:
                    pe.wait_ge(s_ev, n[0] - 3)
                n[0] += 1
                return mm(TURN[(n[0] - 1) % 4][0:rows, lo:hi], lhsT, rhs, start=True, stop=True)

            for k, m in enumerate([PERM, PERM, IDF, IDF, PERM, PERM, IDF, IDF]):
                turn(P, 0, D, wraw[k], m).then_inc(s_mm, 1)
            turn(P, 0, D, wraw[0], ROT).then_inc(s_mm, 1)
            turn(P, 0, D, wraw[1], ROT).then_inc(s_mm, 1)
            turn(P, 0, 2, PERM, BRAW)
            mm(TURN[(n[0] - 1) % 4][:, 2:4], ROT, BRAW, start=True, stop=True).then_inc(s_mm, 1)
            turn(P, 0, NEXP, RWS, CON[0:8, 0:8])
            mm(TURN[(n[0] - 1) % 4][:, NEXP:2 * NEXP], B1S, CON[0:8, 0:8], start=True, stop=True).then_inc(s_mm, 1)
            pe.wait_ge(s_sv, SV_SILU)
            for L in range(2):
                turn(P, 0, 32, CE[L], CON[0:32, 0:32]).then_inc(s_mm, 1)
                pe.wait_ge(s_ev, 13 + 3 * L)
                for h in range(2):
                    turn(32, 0, 384, CT[L], WMOD[L][:, 384 * h:384 * h + 384]).then_inc(s_mm, 1)
            pe.wait_ge(s_sv, SV_MOD)
            for L in range(2):
                for k in range(2):
                    turn(P, 0, 32, MODR[L][:, D * k:D * k + D], CON[0:32, 0:32]).then_inc(s_mm, 1)
            pe.wait_ge(s_ev, 22)
            pe.wait_ge(s_cb, 8)
            pe.wait_ge(s_ones, 4)

            def layer(L):
                J = HEADS[L]

                def max_unit(b, o, u):
                    bank = AB[u % 3]
                    wait(pe, e_amax, L, b, max(u - 2, 0))
                    if L == 1:
                        q, c, j = u // 16, u // 2 % 8, 2 * (u % 2)
                        mm(bank[:, :].rearrange("p (j t) -> p j t", j=2), QS[0:ROWS, o, c, q * P:q * P + P],
                           KM[0:ROWS, o, j:j + 2, c, :], start=True, stop=True).then_inc(e_amm.sem, 1)
                    elif u < 4:
                        for h in range(2):
                            mm(bank[:, 256 * h:256 * h + 256].rearrange("p (j t) -> p j t", j=2),
                               QS[0:ROWS, o, 2 * u + h, 0:P], KM[0:ROWS, o, 0:2, 2 * u + h, 0:P],
                               start=(h == 0), stop=False, skip_group_check=True)
                        mm(bank[:, :].rearrange("p (j t) -> p j t", j=4), IDB[:, :], MAB[:, :, :],
                           start=False, stop=True, skip_group_check=True).then_inc(e_amm.sem, 1)
                    else:
                        v = bank[:, :].rearrange("p (j t) -> p j t", j=2)
                        mm(v, QS[0:ROWS, o, u - 4, P:T], KM[0:ROWS, o, 0:2, u - 4, :],
                           start=True, stop=False, skip_group_check=True)
                        mm(v[:, :, P:T], IDB[:, :], MAB[:, 0:2, :],
                           start=False, stop=True, skip_group_check=True).then_inc(e_amm.sem, 1)

                def scores(b, o, G, m):
                    kb, g0, g1, w = banks(L)[m]
                    n = len(banks(L)) * G + m
                    wait(pe, e_exp, L, b, max(n - 2, 0))
                    for g, (c, j) in enumerate(heads(L, G)[g0:g1]):
                        x = mm(CS[n % 3][:, g * w:g * w + w], KM[:, o, j, c, kb * P:kb * P + P],
                               QS[:, o, c, T - w:T], start=(g == 0), stop=bool(L), skip_group_check=True)
                    if L == 0:
                        v = CS[n % 3][:, :].rearrange("p (g t) -> p g t", t=w)
                        x = mm(v[:, :, 0:P], IDB[:, :], MCB[:, 0:g1 - g0, :],
                               start=False, stop=True, skip_group_check=True)
                    x.then_inc(e_cmm.sem, 1)

                def values(b, o, G, kb):
                    n = len(banks(L))
                    wait(pe, e_exp, L, b, n * G + 2 if kb == 0 else n * (G + 1))
                    if G % 2 == 0 and kb == 0:
                        wait(pe, e_ot, L, b, G // 2)
                    w = T if L or kb == 0 else P
                    for g, (c, j) in enumerate(heads(L, G)):
                        head = 2 * c + (j // 2 if L else j)
                        m = mm(OB[32 * g:32 * g + 32, (G % 2) * T + T - w:(G % 2) * T + T],
                               VB[:, o, kb, head, :], PT[:, (2 * G + kb) % 4, g * w:g * w + w],
                               start=(kb == 0), stop=(kb == 1), skip_group_check=True)
                    if kb == 1:
                        m.then_inc(e_pv.sem, 1)

                def step(i, ph):
                    s1, s2, s3, s4, s5 = stages(i)
                    free = [(e_mts, i, None) if not isinstance(i, int) or 0 <= i < NB else
                            (e_yg, i - 2, None) if i >= NB else (e_v, i + 1, None) if i > -2 else None]

                    def bank_free():
                        if free[0]:
                            wait(pe, free[0][0], L, free[0][1], free[0][2])

                    def uses(event, b, k=None):
                        free[0] = (event, b, k)

                    def turn_out(r):
                        bank_free()
                        wait(pe, e_ot, L, i - 1, r + 1)
                        for x in range(4):
                            m = nc.tensor.transpose(MI[:, P * x:P * x + P],
                                                    OT[:, 2 * r + x // 2, P * (x % 2):P * (x % 2) + P], IDF)
                        m.then_inc(e_otT.sem, 1)
                        uses(e_tok, i - 1, r + 1)

                    pending = None
                    for s in range(SLOTS):
                        if s4 and s < GROUPS[L] // 4:
                            turn_out(2 * s)
                        G = group_of(L, s) if s3 else None
                        units = list(chunk(L, s)) if s2 else []
                        if s == 0 and s2:
                            wait(pe, e_qs, L, i + 1)
                            wait(pe, e_km, L, i + 1)
                        if G == 0:
                            wait(pe, e_min, L, i)
                            wait(pe, e_v, L, i)
                        if units:
                            max_unit(i + 1, (ph + 1) % 3, units.pop(0))
                        if G is not None:
                            scores(i, ph, G, 0)
                        for u in units[0:1]:
                            max_unit(i + 1, (ph + 1) % 3, u)
                        if G is not None:
                            scores(i, ph, G, 1)
                        if s4 and s < GROUPS[L] // 4:
                            turn_out(2 * s + 1)
                        if s1 and s == 1 + L:
                            bank_free()
                            wait(pe, e_xn, L, i + 2)
                            for q in range(QB):
                                m = nc.tensor.transpose(MI[:, P * q:P * q + P], XN[:, q, :], IDF)
                            m.then_inc(e_xnT.sem, 1)
                            uses(e_hT, i + 2)
                        if s1 and s == 2 + L:
                            bank_free()
                            for k, w in enumerate((WQP, WKP)):
                                m = mm(MI[:, T * k:T * k + T], w[:, L, :], HT[:, :], start=True, stop=True)
                            m.then_inc(e_qkps.sem, 1)
                            uses(e_qk if L else e_cos, i + 2)
                        if s1 and s == 3 and L == 0:
                            bank_free()
                            for k, w in enumerate((WQR, WKR)):
                                m = mm(MI[:, T * k:T * k + T], w[:, :], HT[:, :], start=True, stop=True)
                            m.then_inc(e_qkrot.sem, 1)
                            uses(e_sin, i + 2)
                        if s5 and s == 4:
                            bank_free()
                            wait(pe, e_h2, L, i - 2)
                            for q in range(QB):
                                m = nc.tensor.transpose(MI[:, P * q:P * q + P], H2[:, q, :], IDF)
                            m.then_inc(e_h2T.sem, 1)
                            uses(e_h2t, i - 2)
                        if s1 and s == 4 + L:
                            bank_free()
                            for q in range(QB):
                                m = mm(MI[:, P * q:P * q + P], HT[:, P * q:P * q + P], WVT[:, L, :],
                                       start=True, stop=True)
                            m.then_inc(e_vps.sem, 1)
                            uses(e_v, i + 2)
                        if s5 and s == 5:
                            bank_free()
                            for q in range(QB):
                                m = mm(MI[:, NEXP * q:NEXP * q + NEXP], H2T[:, P * q:P * q + P], RWT[:, 2 * L, :],
                                       start=True, stop=True)
                            m.then_inc(e_lgps.sem, 1)
                            uses(e_lg, i - 2)
                        if s4 and s == 7:
                            bank_free()
                            wait(pe, e_ao, L, i - 1)
                            for q in range(QB):
                                m = nc.tensor.transpose(MI[:, P * q:P * q + P], AO[:, q, :], IDF)
                            m.then_inc(e_aoT.sem, 1)
                            uses(e_aot, i - 1)
                        if s5 and s == 7:
                            bank_free()
                            wait(pe, e_ohs, L, i - 2)
                            acc = [(0, LTB, 0), (1, LTB, 1), (1, ONB, 0), (2, ONB, 0), (2, ONB, 1)]
                            for k, (col, lhsT, q) in enumerate(acc):
                                m = mm(MI[:, NEXP * col:NEXP * (col + 1)], lhsT[:, :], OHS[:, q, :],
                                       start=k in (0, 1, 3), stop=k in (0, 2, 4), skip_group_check=True)
                            m.then_inc(e_posps.sem, 1)
                            uses(e_pos, i - 2, 2)
                        if s4 and s == 8:
                            bank_free()
                            wait(pe, e_aot, L, i - 1)
                            for q in range(QB):
                                m = mm(MI[:, P * q:P * q + P], AOT[:, P * q:P * q + P], WOT[:, L, :],
                                       start=True, stop=True)
                            m.then_inc(e_y.sem, 1)
                            uses(e_yg, i - 1)
                        if s2 and s == 9:
                            bank_free()
                            wait(pe, e_nm, L, i + 1, own=w_pe)
                            n = 2 * J * NC8
                            for q in range(QB):
                                m = nc.tensor.transpose(MIB[0:n, P * q:P * q + P], NM[:, q, 0:n], IDB[:, :])
                            m.then_inc(e_nmT.sem, 1)
                            uses(e_mts, i + 1)
                        if G is not None:
                            scores(i, ph, G, 2)
                        for u in units[1:2]:
                            max_unit(i + 1, (ph + 1) % 3, u)
                        drain = pending is not None and (G is not None or s == SLOTS - 1)
                        if drain:
                            values(i, ph, pending, 0)
                        if G is not None and L:
                            scores(i, ph, G, 3)
                        for u in units[2:]:
                            max_unit(i + 1, (ph + 1) % 3, u)
                        if drain:
                            values(i, ph, pending, 1)
                            pending = None
                        if G is not None:
                            pending = G
                steps(pe, step)

            layer(0)
            pe.wait_ge(s_bfp, 16)
            pe.wait_ge(s_wp, 80)

            def ahead(t, r):
                pe.wait_ge(f_x[r], 4 * (t - r) + 16)
                if not isinstance(t, int) or t >= 1:
                    pe.wait_ge(f_xt, t)
                nc.tensor.transpose(MI[:, 0:P], XIN[r], IDF).then_inc(f_xT, 1)

            def hidden(t, r, e):
                pe.wait_ge(f_xt, t + 1)
                if not isinstance(t, int) or t >= 2:
                    pe.wait_ge(f_g, t - 1)
                mm(AB[r % 2][:, :], XTT[r % 2], WFC[:, bass.ds(e * HID, HID)], start=True, stop=False)
                mm(AB[r % 2][:, :], ONE3[:, :], BFP[:, bass.ds(e * HID, HID)], start=False, stop=True
                   ).then_inc(f_h, 1)

            def turned(t, r):
                pe.wait_ge(f_g, t + 1)
                if not isinstance(t, int) or t >= 1:
                    pe.wait_ge(f_ht, t)
                for k in range(4):
                    m = nc.tensor.transpose(CS[0][:, P * k:P * k + P], HS[r % 2][:, P * k:P * k + P], IDF)
                m.then_inc(f_hT, 1)

            def project(t, r, e):
                pe.wait_ge(f_ht, t + 1)
                if not isinstance(t, int) or t >= 1:
                    pe.wait_ge(f_yo, t)
                for k in range(4):
                    mm(OB[:, 0:D], HTT[r % 2][:, P * k:P * k + P], WPR[k // 2][:, bass.ds((e + k % 2 * NEXP) * D, D)],
                       start=(k == 0), stop=False)
                mm(OB[:, 0:D], ONE3[:, :], BFP[:, bass.ds(e * D + NEXP * HID, D)], start=False, stop=True
                   ).then_inc(f_y, 1)

            def expert(t):
                return pe.value_load(TE[0:1, bass.ds(t, 1)], min_val=0, max_val=NEXP - 1)

            ahead(0, 0)
            hidden(0, 0, expert(0))
            ahead(1, 1)

            def tile(t, r, before):
                turned(t - 1, (r + 3) % 4)
                own = expert(t)
                hidden(t, r, own)
                project(t - 1, (r + 3) % 4, expert(t - 1) if before is None else before)
                ahead(t + 1, (r + 1) % 4)
                return own

            loops = (TILES0 - 2) // 8
            with pe.Fori(1, 1 + 8 * loops - 7, 8) as i:
                before = None
                for r in range(8):
                    before = tile(i + r, (1 + r) % 4, before)
            before = None
            for t in range(1 + 8 * loops, TILES0 - 1):
                before = tile(t, t % 4, before)
            t = TILES0 - 1
            turned(t - 1, (t - 1) % 4)
            hidden(t, t % 4, expert(t))
            project(t - 1, (t - 1) % 4, expert(t - 1))
            turned(t, t % 4)
            project(t, t % 4, expert(t))

            layer(1)
            pe.wait_ge(c_w, 48)
            for k in range(CHUNKS + 2):
                if k < CHUNKS:
                    pe.wait_ge(c_x[k % 4], 16 * (k // 4 + 1))
                    if k >= 2:
                        pe.wait_ge(c_xt, k - 1)
                    for a in range(KC):
                        m = nc.tensor.transpose(AB[k % 2][:, P * a:P * a + P], XC[k % 4][:, P * a:P * a + P], IDF)
                    m.then_inc(c_xT, 1)
                if 1 <= k <= CHUNKS:
                    n = k - 1
                    e = n * CW // CAP
                    pe.wait_ge(c_xt, n + 1)
                    if n >= 2:
                        pe.wait_ge(c_r, n - 1)
                    mm(CS[n % 2][:, 0:CW], W1S[:, D * e:D * e + D], XCT[n % 2], start=True, stop=True
                       ).then_inc(c_h, 1)
                if k >= 2:
                    n = k - 2
                    e = n * CW // CAP
                    pe.wait_ge(c_r, n + 1)
                    if n >= 2:
                        pe.wait_ge(c_yo, n - 1)
                    for a in range(KC):
                        m = mm((OB, MI)[n % 2][:, P * a:P * a + P], HC[n % 2][:, P * a:P * a + P],
                               W2S[:, D * e:D * e + D], start=True, stop=True)
                    m.then_inc(c_y, 1)

        @block.vector
        def _(dve):
            v = nc.vector
            dve.wait_ge(s_ld, N_LD)
            v.tensor_copy(IDB[:, :], IDF).then_inc(s_cb, 1)
            v.memset(KU[ROWS:P, :, :], 1.0).then_inc(s_cb, 1)
            v.memset(QS[ROWS:P, :, :, :], 0.0).then_inc(s_cb, 1)
            v.tensor_copy(LTB[:, :], CON[:, C_LT:C_LT + P]).then_inc(s_cb, 1)
            for dst, c in ((MAB, C_MA), (MCB, C_MC)):
                v.tensor_copy(dst[:, :, :], CON[:, c:c + P].unsqueeze(1).to_broadcast([P, 4, P])).then_inc(s_cb, 1)
            v.tensor_scalar(COSS[:, :], CON[:, C_COS:C_COS + T], SCL, None, ALU.mult).then_inc(s_cb, 1)
            v.tensor_scalar(SINS[:, :], CON[:, C_SIN:C_SIN + T], SCL, None, ALU.mult).then_inc(s_cb, 1)
            c = [0]

            def link(ins):
                ins.then_inc(s_sv, 1)
                c[0] += 1
                dve.wait_ge(s_sv, c[0])

            for k in range(3):
                v.tensor_copy(BPARTS[:, k, :], BRES if k else BIAS).then_inc(s_b3, 1)
                dve.wait_ge(s_b3, 2 * k + 1)
                if k < 2:
                    v.tensor_tensor(BRES, BRES if k else BIAS, BPARTS[:, k, :], ALU.subtract).then_inc(s_b3, 1)
                    dve.wait_ge(s_b3, 2 * k + 2)
            dve.wait_ge(s_sa, 2)
            for L in range(2):
                link(v.tensor_scalar(CE[L], CE[L], 1.0, None, ALU.add))
                link(v.reciprocal(CE[L], CE[L]))
                link(v.tensor_tensor(CE[L], CE[L], CC[L], ALU.mult))
            link(v.tensor_tensor(LMP.rearrange("p (a d) -> p a d", a=2),
                                 LMB.rearrange("p (a k d) -> p a k d", a=2, k=2)[:, :, 0, :],
                                 LMB.rearrange("p (a k d) -> p a k d", a=2, k=2)[:, :, 1, :], ALU.mult))
            link(v.tensor_reduce(LMS, LMP.rearrange("p (a d) -> p a d", a=2), AX.X, ALU.add))
            for L in range(2):
                dve.wait_ge(s_ev, 15 + 3 * L)
                m = MODR[L].rearrange("p (k d) -> p k d", d=D)
                link(v.tensor_scalar(SIGN[L], m[:, 2:6:3, :], 0.0, 2.0, ALU.is_ge, ALU.mult))
                link(v.scalar_tensor_tensor(MAG[L], m[:, 2:6:3, :], -1.0, m[:, 2:6:3, :], ALU.mult, ALU.max))
                link(v.tensor_scalar(MAG[L], MAG[L], 0.25, None, ALU.max))
                R = ROWS_OUT[L]
                link(v.scalar_tensor_tensor(R[:, 0:5:4, :], SIGN[L], -1.0, MAG[L], ALU.add, ALU.mult))
                if L == 0:
                    link(v.tensor_tensor(R[:, 1, :], R[:, 0, :], BO32, ALU.mult))
                else:
                    link(v.memset(R[:, 1, :], 0.0))
                link(v.tensor_scalar(R[:, 2, :], m[:, 4, :], 1.0, None, ALU.add))
                link(v.tensor_copy(R[:, 3, :], m[:, 3, :]))
            for L in range(2):
                link(v.tensor_scalar(MODR[L][:, D:2 * D], MODR[L][:, D:2 * D], 1.0, None, ALU.add))
            dve.wait_ge(s_sa, 3)
            link(v.tensor_tensor(LMX[:, 2:3], LMX[:, 1:2], LMX[:, 0:1], ALU.subtract))
            dve.wait_ge(s_ones, 4)
            link(v.tensor_scalar(LAMSEL[:, :].rearrange("p (a b) -> p a b", b=2)[:, :, 1],
                                 NHALF[:, :], 0.5, LMX[:, 2:3], ALU.add, ALU.add))
            link(v.tensor_scalar(LAMSEL[:, :].rearrange("p (a b) -> p a b", b=2)[:, :, 1],
                                 LAMSEL[:, :].rearrange("p (a b) -> p a b", b=2)[:, :, 1],
                                 -LAMBDA_INIT, None, ALU.add))
            link(v.tensor_scalar(WSUB[:, :], WSUB[:, :], 1.0 - LAMBDA_INIT, None, ALU.mult))
            dve.wait_ge(s_ev, 22)
            dve.wait_ge(s_cb, 8)

            v.memset(RC[:, :, :], 0.0).then_inc(s_rc, 1)
            v.memset(ONB[:, :], 1.0).then_inc(s_rc, 1)
            v.memset(ZFILL, 0.0).then_inc(s_rc, 1)
            v.memset(ONE3[:, :], 1.0).then_inc(s_rc, 1)
            dve.wait_ge(s_rc, 4)
            dve.wait_ge(s_x0, 16)

            def tables():
                n = [0]

                def table(ins):
                    ins.then_inc(s_tab, 1)
                    n[0] += 1
                    dve.wait_ge(s_tab, n[0])

                wait(dve, e_pos, 0, NB - 1)
                table(v.memset(ZERO, 0.0))
                table(v.tensor_copy(CNTI[:, :], RC[0:1, 0, :]))
                table(v.tensor_scalar(CNT[:, :], RC[:, 0, :], float(P - 1), None, ALU.add))
                table(v.tensor_copy(NTI[:, :], CNT[:, :]))
                table(v.tensor_single_scalar(NTI[:, :], NTI[:, :], 7, op=ALU.arith_shift_right))
                table(v.tensor_copy(NTF[:, :], NTI[:, :]))
                table(v.tensor_tensor(BT8[:, :].rearrange("p (e j) -> p e j", e=NEXP),
                                      CON[:, C_TRI:C_TRI + 64].rearrange("p (e j) -> p e j", e=NEXP),
                                      NTF[:, :].unsqueeze(1).to_broadcast([P, NEXP, NEXP]), ALU.mult))
                table(v.tensor_reduce(BT[:, :], BT8[:, :].rearrange("p (e j) -> p e j", e=NEXP), AX.X, ALU.add))
                table(v.scalar_tensor_tensor(ADJ[:, :], BT[:, :], float(P), CON[:, C_REG:C_REG + NEXP],
                                             ALU.mult, ALU.subtract))
                A = KMF[0][0:1, 0:TILES0 * NEXP].rearrange("p (t e) -> p t e", e=NEXP)
                A2 = KMF[1][0:1, 0:TILES0 * NEXP].rearrange("p (t e) -> p t e", e=NEXP)
                io = CON[0:1, C_IOTA:C_IOTA + TILES0]
                bt = BT[0:1, :].unsqueeze(1).to_broadcast([1, TILES0, NEXP])
                table(v.tensor_tensor(A, io.unsqueeze(2).to_broadcast([1, TILES0, NEXP]), bt, ALU.is_ge))
                table(v.tensor_tensor(A2, A, bt, ALU.mult))
                TEF, TBF = OT[0:1, 4, 0:TILES0], OT[0:1, 5, 0:TILES0]
                table(v.tensor_reduce(TEF, A, AX.X, ALU.add))
                table(v.tensor_reduce(TBF, A2, AX.X, ALU.max))
                table(v.tensor_scalar(TEF, TEF, -1.0, None, ALU.add))
                table(v.tensor_copy(TE[:, :], TEF))
                table(v.tensor_tensor(TBF, io, TBF, ALU.subtract))
                table(v.tensor_scalar(LIM[:, :], NTF[0:1, NEXP - 1:NEXP], -1.0, 0.0, ALU.add, ALU.max))
                table(v.tensor_scalar(LIM[:, :], LIM[:, :], float(P), float((NEXP - 1) * REGION), ALU.mult, ALU.add))
                table(v.tensor_scalar(TBF, TBF, float(P), None, ALU.mult))
                table(v.scalar_tensor_tensor(TBF, TEF, float(REGION), TBF, ALU.mult, ALU.add))
                table(v.tensor_scalar(TBF, TBF, LIM[:, :], None, ALU.min))
                table(v.tensor_copy(ROW[:, :], TBF))
                OHT = WORK[:, 0:TPB * 2 * NEXP].rearrange("p (t e) -> p t e", e=NEXP)
                table(v.tensor_tensor(OHT, OH[:, :, :, :].rearrange("p t k e -> p (t k) e"),
                                      ADJ[:, :].unsqueeze(1).to_broadcast([P, TPB * 2, NEXP]), ALU.mult))
                SH = WORK[:, TPB * 16:TPB * 18]
                table(v.tensor_reduce(SH, OHT, AX.X, ALU.add))
                table(v.tensor_tensor(SH, SH, SALL[:, :, :].rearrange("p t k -> p (t k)"), ALU.add))
                table(v.tensor_copy(GI0[:, :, :].rearrange("p t k -> p (t k)"), SH))
                assert n[0] == TAB_ALL, n[0]

            def layer(L):
                J = HEADS[L]
                MXv = MX[:, 0:QB * NC8 * J].rearrange("p (q c j) -> p q c j", q=QB, c=NC8)

                def stats(b, which, e_in, e_a, e_b, free, part):
                    if part == 0:
                        if e_in is not None:
                            wait(dve, e_in, L, b)
                        wait(dve, free, L, b - 1, own=w_dve)
                        for q in range(QB):
                            v.bn_stats(ST6[:, which, q, :], X[:, bass.ds(b * QB + q, 1), :].rearrange(
                                "p a d -> p (a d)")).then_inc(e_a.sem, 1)
                        return
                    wait(dve, e_a, L, b, own=w_dve)
                    for q in range(QB):
                        v.bn_aggr(MV[:, which, q, :], ST6[:, which, q, :]).then_inc(e_b.sem, 1)

                def step(i, ph):
                    s1, s2, s3, s4, s5 = stages(i)
                    if L == 0 and isinstance(i, int) and i == 1:
                        dve.wait_ge(s_x, 16 * (NB // 4 - 1))
                    for s in range(SLOTS):
                        units = list(chunk(L, s)) if s2 else []
                        for k in range(4):
                            for u in units[k:k + 1]:
                                maxima(i + 1, u)
                            between(i, ph, s, k)
                        if s2 and s == 8:
                            b = i + 1
                            wait(dve, e_amax, L, b)
                            wait(dve, e_nmT, L, b - 1)
                            NMv = NM[:, :, 0:2 * J * NC8].rearrange("p q (a j c) -> p q a j c", a=2, j=J)
                            v.tensor_scalar(NMv[:, :, 0].rearrange("p q j c -> p q c j"), MXv, -1.0, None, ALU.mult
                                            ).then_inc(e_nm.sem, 1)
                            wait(dve, e_nm, L, b, 1)
                            for q in range(QB):
                                v.scalar_tensor_tensor(NMv[:, q, 1].rearrange("p j c -> p c j"), MXv[:, q], -1.0,
                                                       NMv[:, q, 0].rearrange("p j c -> p c j"), ALU.mult,
                                                       ALU.subtract).then_inc(e_nm.sem, 1)

                def between(i, ph, s, k):
                    s1, s2, s3, s4, s5 = stages(i)
                    if s1 and L and s == 0:
                        combine(i + 2, k)
                    if s1 and s == L and k < 2:
                        stats(i + 2, 0, e_x2 if L else None, e_stats, e_aggr, e_xn, k)
                    if s5 and (s, k) in ((0, 3), (1, 2)):
                        stats(i - 2, 1, e_x1, e_st2, e_ag2, e_h2, s)
                    if s4 and (s, k) == (1, 3):
                        wait(dve, e_tok, L, i - 1)
                        wait(dve, e_rsl if L else e_ao, L, i - 2)
                        n = GROUPS[L] * QB * 4
                        v.reciprocal(RS[:, 0:n], TOK[:, 0:GROUPS[L], :, :, :].rearrange(
                            "p a q g d -> p (a q g) d")[:, :, 8]).then_inc(e_rs.sem, 1)
                    if s4 and L == 1 and (s, k) == (3, 2):
                        b = i - 1
                        wait(dve, e_sq, L, b)
                        wait(dve, e_ms, L, b - 1)
                        v.tensor_reduce(SS[:, :], SQ[:, :, :].rearrange("p q (h d) -> p (q h) d", d=8), AX.X,
                                        ALU.add).then_inc(e_ss.sem, 1)
                    if s1 and L == 0 and s in (2, 3) and k == 1:
                        b = i + 2
                        wait(dve, e_qkps if s == 2 else e_qkrot, L, b)
                        wait(dve, e_qk, L, b - 1)
                        if s == 3:
                            wait(dve, e_split, L, b - 1)
                        dst = T1 if s == 2 else T2
                        tab = (COSS[:, :], CON[:, C_COS:C_COS + T]) if s == 2 else (SINS[:, :],
                                                                                   CON[:, C_SIN:C_SIN + T])
                        for k in range(2):
                            v.scalar_tensor_tensor(dst[:, k, :], MI[:, T * k:T * k + T],
                                                   BQK[:, 2 * (s - 2) + k:2 * (s - 2) + k + 1], tab[k],
                                                   ALU.add, ALU.mult).then_inc((e_cos if s == 2 else e_sin).sem, 1)
                    if s1 and L == 0 and (s, k) == (4, 1):
                        b = i + 2
                        wait(dve, e_vps, L, b)
                        wait(dve, e_pv, L, b - 3)
                        v.tensor_tensor(VB[:, (ph + 2) % 3, :, :, 0:8],
                                        MI[:, 0:T].rearrange("p (q h d) -> p q h d", q=QB, d=8),
                                        BVR[:, :].rearrange("p (h d) -> p h d", d=8).unsqueeze(1).to_broadcast(
                                            [P, QB, 16, 8]), ALU.add).then_inc(e_v.sem, 1)
                    if s1 and (s, k) == (5, 0 if L else 3):
                        wait(dve, e_split, L, i + 2, 3)
                        v.tensor_tensor(PARTS[:, 2, :], RES[:, :], PARTS[:, 1, :], ALU.subtract
                                        ).then_inc(e_split.sem, 1)
                    if s5 and (5, 2) <= (s, k) <= (8, 0):
                        route(i - 2, s, k)
                    if s5 and (s, k) == (8, 0):
                        place(i - 2, 0)
                    if s4 and (s, k) == (8, 2):
                        b = i - 1
                        wait(dve, e_y, L, b)
                        wait(dve, e_mb, L, b)
                        wait(dve, e_x1, L, b - 1)
                        v.tensor_tensor(YG[:, :, :], MI[:, 0:T].rearrange("p (q d) -> p q d", q=QB),
                                        MB[:, 0, :].unsqueeze(1).to_broadcast([P, QB, D]), ALU.mult
                                        ).then_inc(e_yg.sem, 1)
                    if s5 and (s, k) == (9, 1):
                        place(i - 2, 1)
                    if s1 and (s, k) in (((9, 2), (9, 3)) if L == 0 else ((7, 3), (8, 1), (8, 3), (9, 0))):
                        b, o = i + 2, (ph + 2) % 3
                        j = [(7, 3), (8, 1), (8, 3), (9, 0)].index((s, k)) if L else k - 2
                        if j == 0:
                            wait(dve, e_ku, L, b)
                            wait(dve, e_cmm, L, b - 3)
                            wait(dve, e_amm, L, b - 3)
                        v.tensor_scalar(KM[:, o, j, :, :], KU[:, :, :],
                                        CON[:, C_HM + 2 * L + j:C_HM + 2 * L + j + 1], None, ALU.mult
                                        ).then_inc(e_km.sem, 1)

                def maxima(b, u):
                    wait(dve, e_amm, L, b, u + 1)
                    if u == 0:
                        wait(dve, e_nm, L, b - 1)
                    if L:
                        dst = MXv[:, u // 16, u // 2 % 8, 2 * (u % 2):2 * (u % 2) + 2]
                        src = AB[u % 3][:, :].rearrange("p (j t) -> p j t", j=2)
                    elif u < 4:
                        dst = MXv[:, 0, 2 * u:2 * u + 2, :].rearrange("p c j -> p (c j)")
                        src = AB[u % 3][:, :].rearrange("p (j t) -> p j t", j=4)
                    else:
                        dst = MXv[:, 1, u - 4, :]
                        src = AB[u % 3][:, :].rearrange("p (j t) -> p j t", j=2)
                    v.tensor_reduce(dst, src, AX.X, ALU.max).then_inc(e_amax.sem, 1)

                def route(b, s, k):
                    tiles = bass.ds(b * QB, QB)
                    cmp = CMP[:, :, :].rearrange("p q (e j) -> p q e j", e=NEXP)
                    eq = EQ[:, :, :].rearrange("p q (e j) -> p q e j", e=NEXP)
                    rk = RK[:, :].rearrange("p (q e) -> p q e", q=QB)
                    if (s, k) == (5, 2):
                        wait(dve, e_lgps, L, b)
                        wait(dve, e_wexp, L, b - 1)
                        lg = MI[:, 0:QB * NEXP].rearrange("p (q e) -> p q e", q=QB)
                        if L:
                            v.tensor_tensor(LG[:, :, :], lg, BRR[:, :].unsqueeze(1).to_broadcast([P, QB, NEXP]),
                                            ALU.add).then_inc(e_lg.sem, 1)
                        else:
                            v.tensor_copy(LG[:, :, :], lg).then_inc(e_lg.sem, 1)
                    if (s, k) == (5, 3):
                        wait(dve, e_lg, L, b)
                        lj = LG[:, :, :].unsqueeze(2).to_broadcast([P, QB, NEXP, NEXP])
                        le = LG[:, :, :].unsqueeze(3).to_broadcast([P, QB, NEXP, NEXP])
                        v.tensor_tensor(cmp, lj, le, ALU.is_gt).then_inc(e_rank.sem, 1)
                        v.tensor_tensor(eq, lj, le, ALU.is_equal).then_inc(e_rank.sem, 1)
                    if (s, k) == (6, 0):
                        wait(dve, e_rank, L, b, 2)
                        v.tensor_tensor(EQ[:, :, :], EQ[:, :, :], CON[:, C_TRI:C_TRI + 64].unsqueeze(1).to_broadcast(
                            [P, QB, 64]), ALU.mult).then_inc(e_rank.sem, 1)
                    if (s, k) == (6, 1):
                        wait(dve, e_rank, L, b, 3)
                        v.tensor_tensor(CMP[:, :, :], CMP[:, :, :], EQ[:, :, :], ALU.add).then_inc(e_rank.sem, 1)
                    if (s, k) == (6, 2):
                        wait(dve, e_rank, L, b, 4)
                        v.tensor_reduce(RK[:, :], CMP[:, :, :].rearrange("p q (e j) -> p (q e) j", e=NEXP), AX.X,
                                        ALU.add).then_inc(e_rank.sem, 1)
                    if (s, k) == (6, 3):
                        wait(dve, e_rank, L, b, 5)
                        wait(dve, e_posps, L, b - 1)
                        v.tensor_scalar(OHS[:, :, :], rk, 1.0 if L == 0 else 0.0, None, ALU.is_le
                                        ).then_inc(e_ohs.sem, 1)
                        if L == 0:
                            for n in range(2):
                                v.tensor_scalar(OH[:, tiles, n, :], rk, float(n), None, ALU.is_equal
                                                ).then_inc(e_oh.sem, 1)
                            v.tensor_reduce(M1[:, :], LG[:, :, :], AX.X, ALU.max).then_inc(e_wt.sem, 1)
                        else:
                            v.tensor_scalar(OH1[:, :, :], rk, 0.0, None, ALU.is_equal).then_inc(e_oh.sem, 1)
                            v.tensor_reduce(M1[:, :], LG[:, :, :], AX.X, ALU.max).then_inc(e_gate.sem, 1)
                    if (s, k) == (7, 0):
                        if L == 0:
                            wait(dve, e_oh, L, b)
                            v.tensor_tensor(LE[:, :, :], LG[:, :, :], OH[:, tiles, 1, :], ALU.mult
                                            ).then_inc(e_wt.sem, 1)
                        else:
                            wait(dve, e_gate, L, b, 1)
                            v.tensor_tensor(LE[:, :, :], LG[:, :, :], M1[:, :].unsqueeze(2).to_broadcast(
                                [P, QB, NEXP]), ALU.subtract).then_inc(e_wt.sem, 1)
                    if L == 0 and (s, k) == (7, 2):
                        wait(dve, e_wt, L, b, 2)
                        v.tensor_reduce(L2[:, :], LE[:, :, :], AX.X, ALU.add).then_inc(e_wt.sem, 1)
                    if L == 0 and (s, k) == (8, 0):
                        wait(dve, e_wt, L, b, 3)
                        v.tensor_tensor(L2[:, :], L2[:, :], M1[:, :], ALU.subtract).then_inc(e_wt.sem, 1)

                def place(b, part):
                    tiles = bass.ds(b * QB, QB)
                    if part:
                        place_rows(b, tiles)
                        return
                    wait(dve, e_posps, L, b)
                    wait(dve, e_pos, L, b - 1)
                    v.tensor_tensor(POS[:, :, :], MI[:, 0:QB * NEXP].rearrange("p (q e) -> p q e", q=QB),
                                    RC[:, L, :].unsqueeze(1).to_broadcast([P, QB, NEXP]), ALU.add
                                    ).then_inc(e_pos.sem, 1)
                    wait(dve, e_pos, L, b, 1)
                    v.tensor_tensor(RC[:, L, :], RC[:, L, :], MI[:, QB * NEXP:(QB + 1) * NEXP], ALU.add
                                    ).then_inc(e_pos.sem, 1)

                def place_rows(b, tiles):
                    wait(dve, e_sc, L, b - 1)
                    if L == 0:
                        v.tensor_tensor(POS[:, :, :], POS[:, :, :], CON[:, C_REG:C_REG + NEXP].unsqueeze(1
                                        ).to_broadcast([P, QB, NEXP]), ALU.add).then_inc(e_pos.sem, 1)
                        wait(dve, e_pos, L, b)
                        v.tensor_tensor(PO[:, :, :, :], OH[:, tiles, :, :],
                                        POS[:, :, :].unsqueeze(2).to_broadcast([P, QB, 2, NEXP]), ALU.mult
                                        ).then_inc(e_slot.sem, 1)
                        wait(dve, e_slot, L, b, 1)
                        v.tensor_reduce(SALL[:, tiles, :].rearrange("p q k -> p (q k)"),
                                        PO[:, :, :, :].rearrange("p q k e -> p (q k) e"), AX.X, ALU.add
                                        ).then_inc(e_slot.sem, 1)
                        wait(dve, e_slot, L, b, 2, own=w_dve)
                        v.tensor_copy(SIDX[:, :, :], SALL[:, tiles, :]).then_inc(e_slot.sem, 1)
                        wait(dve, e_wexp, L, b)
                        v.tensor_scalar(M1[:, :], W[:, :], 1.0, None, ALU.add).then_inc(e_gate.sem, 1)
                        wait(dve, e_gate, L, b, 1)
                        v.reciprocal(WALL[:, tiles, 0], M1[:, :]).then_inc(e_gate.sem, 1)
                        wait(dve, e_gate, L, b, 2)
                        v.tensor_tensor(WALL[:, tiles, 1], WALL[:, tiles, 0], W[:, :], ALU.mult
                                        ).then_inc(e_gate.sem, 1)
                        return
                    v.tensor_tensor(PO[:, :, 0, :], OH1[:, :, :], POS[:, :, :], ALU.mult).then_inc(e_slot.sem, 1)
                    v.tensor_tensor(PO[:, :, 1, :], OH1[:, :, :], CON[:, C_CAP:C_CAP + NEXP].unsqueeze(1
                                    ).to_broadcast([P, QB, NEXP]), ALU.mult).then_inc(e_slot.sem, 1)
                    wait(dve, e_wexp, L, b)
                    v.tensor_reduce(SF[:, :], LX[:, :, :], AX.X, ALU.add).then_inc(e_gate.sem, 1)
                    wait(dve, e_slot, L, b, 2)
                    v.tensor_reduce(PP[:, :], PO[:, :, 0, :], AX.X, ALU.add).then_inc(e_slot.sem, 1)
                    v.tensor_reduce(EO[:, :], PO[:, :, 1, :], AX.X, ALU.add).then_inc(e_slot.sem, 1)
                    wait(dve, e_slot, L, b, 4)
                    v.tensor_scalar(KEEP[:, :], PP[:, :], float(CAP - 1), None, ALU.is_lt).then_inc(e_slot.sem, 1)
                    v.tensor_tensor(EO[:, :], PP[:, :], EO[:, :], ALU.add).then_inc(e_slot.sem, 1)
                    wait(dve, e_slot, L, b, 6)
                    wait(dve, e_gate, L, b)
                    v.tensor_tensor(GI1[:, tiles], EO[:, :], KEEP[:, :], ALU.mult).then_inc(e_slot.sem, 1)
                    v.scalar_tensor_tensor(PP[:, :], EO[:, :], float(-NEXP * CAP), KEEP[:, :], ALU.add, ALU.mult
                                           ).then_inc(e_slot.sem, 1)
                    v.reciprocal(M1[:, :], SF[:, :]).then_inc(e_gate2.sem, 1)
                    wait(dve, e_slot, L, b, 8)
                    wait(dve, e_gate2, L, b, 1)
                    v.tensor_scalar(SIDX[:, :, 0], PP[:, :], float(NEXP * CAP), None, ALU.add).then_inc(e_slot.sem, 1)
                    wait(dve, e_gx, L, b - 1)
                    v.tensor_tensor(GALL[:, tiles], M1[:, :], KEEP[:, :], ALU.mult).then_inc(e_gate2.sem, 1)

                def combine(b, part):
                    if part == 1:
                        for q in range(QB):
                            wait(dve, e_wy, L, b, q + 1)
                            v.scalar_tensor_tensor(GC[:, q, :], GY[:, q, 1, :], WALL[:, bass.ds(b * QB + q, 1), 1],
                                                   GC[:, q, :], ALU.mult, ALU.add).then_inc(e_cmb.sem, 1)
                    elif part == 2:
                        wait(dve, e_gbr, L, b)
                        wait(dve, e_cmb, L, b, 2)
                        v.tensor_tensor(GC[:, :, :], GC[:, :, :], GBR[:, 0, :].unsqueeze(1).to_broadcast([P, QB, D]),
                                        ALU.mult).then_inc(e_cmb.sem, 1)
                    elif part == 3:
                        wait(dve, e_cmb, L, b)
                        v.tensor_tensor(X[:, bass.ds(b * QB, QB), :], X[:, bass.ds(b * QB, QB), :], GC[:, :, :],
                                        ALU.add).then_inc(e_x2.sem, 1)

                steps(dve, step)

            layer(0)
            tables()
            dve.wait_ge(s_tail, 16 * NEXP)

            def tile_out(t, r):
                dve.wait_ge(f_hT, t + 1)
                if not isinstance(t, int) or t >= 2:
                    dve.wait_ge(f_y, t - 1)
                v.tensor_copy(HTT[r % 2], CS[0][:, 0:HID]).then_inc(f_ht, 1)
                dve.wait_ge(f_y, t + 1)
                if not isinstance(t, int) or t >= 4:
                    dve.wait_ge(f_st[r], 4 * (t - r))
                v.tensor_copy(YO[r], OB[:, 0:D]).then_inc(f_yo, 1)

            def tile_in(t, r):
                dve.wait_ge(f_xT, t + 1)
                if not isinstance(t, int) or t >= 2:
                    dve.wait_ge(f_h, t - 1)
                v.tensor_copy(XTT[r % 2], MI[:, 0:P]).then_inc(f_xt, 1)

            tile_loop(dve, tile_out, tile_in)
            dve.wait_ge(s_fill, 16 * (NEXP * CAP // P // 8))
            layer(1)
            for k in range(CHUNKS):
                e = k * CW // CAP
                dve.wait_ge(c_y, k + 1)
                if k >= 2:
                    dve.wait_ge(c_st[k % 2], 16 * (k // 2))
                v.tensor_tensor(YC[k % 2].rearrange("p (a d) -> p a d", d=D),
                                (OB, MI)[k % 2][:, 0:CW].rearrange("p (a d) -> p a d", d=D),
                                B2R[:, D * e:D * e + D].unsqueeze(1).to_broadcast([P, KC, D]), ALU.add
                                ).then_inc(c_yo, 1)
            for b in range(NB):
                dve.wait_ge(o_g[b % 2], 32 * (b // 2 + 1))
                dve.wait_ge(o_gb[b % 2], 16 * (b // 2 + 1))
                for q in range(QB):
                    v.scalar_tensor_tensor(GC[:, q, :] if b % 2 else YG[:, q, :], GY[:, q, b % 2, :],
                                           GALL[:, QB * b + q:QB * b + q + 1], GBR[:, b % 2, :], ALU.mult, ALU.mult
                                           ).then_inc(o_m, 1)
                dve.wait_ge(o_m, 2 * (b + 1))
                v.tensor_tensor(X[:, QB * b:QB * b + QB, :], X[:, QB * b:QB * b + QB, :],
                                GC[:, :, :] if b % 2 else YG[:, :, :], ALU.add).then_inc(o_a, 1)

        @block.gpsimd
        def _(pool):
            g = nc.gpsimd
            g.memset(VB[:, :, :, :, :], 0.0).then_inc(s_ones, 1)
            g.memset(LAMSEL[:, :], 1.0).then_inc(s_ones, 1)
            g.memset(NHALF[:, :], -0.5).then_inc(s_ones, 1)
            pool.wait_ge(s_ones, 3)
            g.memset(VB[:, :, :, :, 8:9], 1.0).then_inc(s_ones, 1)
            pool.wait_ge(s_ones, 4)
            pool.wait_ge(s_ev, 22)
            pool.wait_ge(s_w, 32)
            pool.wait_ge(s_cb, 8)

            def layer(L):
                J, NG = HEADS[L], GROUPS[L]

                def rstd(b, which, e_ag, e_a, e_b):
                    wait(pool, e_ag, L, b, own=w_pool)
                    g.tensor_scalar(RSTD[:, which, :], MV[:, which, :, 1], EPS, None, ALU.add).then_inc(e_a.sem, 1)
                    wait(pool, e_a, L, b, own=w_pool)
                    g.tensor_tensor(RSTD[:, which, :], RSTD[:, which, :], NHALF[:, 0:QB], ALU.pow
                                    ).then_inc(e_b.sem, 1)
                    wait(pool, e_b, L, b, 1, own=w_pool)
                    g.tensor_tensor(NMR[:, which, :], MV[:, which, :, 0], RSTD[:, which, :], ALU.mult
                                    ).then_inc(e_b.sem, 1)
                    wait(pool, e_b, L, b, 2, own=w_pool)
                    g.tensor_scalar(NMR[:, which, :], NMR[:, which, :], -1.0, None, ALU.mult).then_inc(e_b.sem, 1)

                def step(i, ph):
                    s1, s2, s3, s4, s5 = stages(i)
                    if s1:
                        b = i + 2
                        wait(pool, e_xn, L, b - 1, own=w_pool)
                        rstd(b, 0, e_aggr, e_veps, e_rstd)
                    if s5:
                        b = i - 2
                        wait(pool, e_h1, L, b - 1, own=w_pool)
                        rstd(b, 1, e_ag2, e_ve2, e_rs2)
                    if s4 and L == 0:
                        b = i - 1
                        wait(pool, e_rs, L, b, own=w_pool)
                        wait(pool, e_aoT, L, b - 1, own=w_pool)
                        for q in range(QB):
                            g.tensor_tensor(AO[:, q, :].rearrange("p (a g d) -> p a g d", a=NG, d=8),
                                            TOK[:, 0:NG, q, :, 0:8],
                                            RS[:, 0:32].rearrange("p (a q g) -> p a q g", a=NG, q=QB)[
                                                :, :, q, :].unsqueeze(3).to_broadcast([P, NG, 4, 8]),
                                            ALU.mult).then_inc(e_ao.sem, 1)
                    if s4 and L == 1:
                        b = i - 1
                        wait(pool, e_rs, L, b, own=w_pool)
                        wait(pool, e_tn, L, b - 1, own=w_pool)
                        g.tensor_tensor(RSL[:, :], RS[:, :], LAMSEL[:, :], ALU.mult).then_inc(e_rsl.sem, 1)
                        wait(pool, e_rsl, L, b, own=w_pool)
                        wait(pool, e_aou, L, b - 1, own=w_pool)
                        g.tensor_tensor(TN[:, :, :, :, :].rearrange("p a q g d -> p (a q g) d"),
                                        TOK[:, :, :, :, :].rearrange("p a q g d -> p (a q g) d")[:, :, 0:8],
                                        RSL[:, :].unsqueeze(2).to_broadcast([P, 64, 8]), ALU.mult
                                        ).then_inc(e_tn.sem, 1)
                        wait(pool, e_tn, L, b, own=w_pool)
                        wait(pool, e_nrm, L, b - 1, own=w_pool)
                        for q in range(QB):
                            g.tensor_tensor(AOU[:, q, :].rearrange("p (a g d) -> p a g d", a=8, d=8),
                                            TN[:, :, q, 0:4:2, :], TN[:, :, q, 1:4:2, :], ALU.add
                                            ).then_inc(e_aou.sem, 1)
                        wait(pool, e_aou, L, b, own=w_pool)
                        wait(pool, e_ss, L, b - 1, own=w_pool)
                        g.tensor_tensor(SQ[:, :, :], AOU[:, :, :], AOU[:, :, :], ALU.mult).then_inc(e_sq.sem, 1)
                    if s5:
                        b = i - 2
                        wait(pool, e_h1, L, b, own=w_pool)
                        wait(pool, e_mb, L, b, own=w_pool)
                        g.tensor_tensor(H2[:, :, :], H2[:, :, :],
                                        MB[:, 2, :].unsqueeze(1).to_broadcast([P, QB, D]), ALU.mult
                                        ).then_inc(e_h1c.sem, 1)
                        wait(pool, e_h1c, L, b, own=w_pool)
                        g.tensor_tensor(H2[:, :, :], H2[:, :, :],
                                        MB[:, 3, :].unsqueeze(1).to_broadcast([P, QB, D]), ALU.add
                                        ).then_inc(e_h2.sem, 1)
                    if s1:
                        b = i + 2
                        if L == 0:
                            wait(pool, e_cos, L, b, own=w_pool)
                            wait(pool, e_sin, L, b, own=w_pool)
                            wait(pool, e_split, L, b - 1, own=w_pool)
                            g.tensor_tensor(QK[:, :], T1[:, :, :].rearrange("p k t -> p (k t)"),
                                            RES[:, :], ALU.add).then_inc(e_qk.sem, 1)
                        wait(pool, e_split, L, b, 1, own=w_pool)
                        g.tensor_tensor(RES[:, :], QK[:, :], PARTS[:, 0, :], ALU.subtract).then_inc(e_split.sem, 1)
                    if s4 and L == 1:
                        b = i - 1
                        wait(pool, e_ss, L, b, own=w_pool)
                        wait(pool, e_nrm, L, b - 1, own=w_pool)
                        g.tensor_scalar(RMS[:, :], SS[:, :], 1.0 / 8, EPS, ALU.mult, ALU.add).then_inc(e_ms.sem, 1)
                        wait(pool, e_ms, L, b, own=w_pool)
                        g.tensor_tensor(RMS[:, :], RMS[:, :], NHALF[:, :], ALU.pow).then_inc(e_rms.sem, 1)
                        wait(pool, e_rms, L, b, own=w_pool)
                        g.tensor_tensor(AOU[:, :, :].rearrange("p q (h d) -> p (q h) d", d=8),
                                        AOU[:, :, :].rearrange("p q (h d) -> p (q h) d", d=8),
                                        RMS[:, :].unsqueeze(2).to_broadcast([P, 32, 8]), ALU.mult
                                        ).then_inc(e_nrm.sem, 1)
                        wait(pool, e_nrm, L, b, own=w_pool)
                        wait(pool, e_aoT, L, b - 1, own=w_pool)
                        g.tensor_tensor(AO[:, :, :].rearrange("p q (h d) -> p (q h) d", d=8),
                                        AOU[:, :, :].rearrange("p q (h d) -> p (q h) d", d=8),
                                        WSUB[:, :].unsqueeze(1).to_broadcast([P, 32, 8]), ALU.mult
                                        ).then_inc(e_ao.sem, 1)
                    if s1 and L:
                        gather(i + 3)
                    if s4:
                        b = i - 1
                        xb = X[:, bass.ds(b * QB, QB), :]
                        wait(pool, e_yg, L, b, own=w_pool)
                        g.tensor_tensor(xb, xb, YG[:, :, :], ALU.add).then_inc(e_xa.sem if L == 0 else e_x1.sem, 1)
                        if L == 0:
                            wait(pool, e_xa, L, b, own=w_pool)
                            g.tensor_tensor(xb, xb, MB[:, 1, :].unsqueeze(1).to_broadcast([P, QB, D]), ALU.add
                                            ).then_inc(e_x1.sem, 1)
                    if s5:
                        b = i - 2
                        if L:
                            wait(pool, e_gate2, L, b, own=w_pool)
                            wait(pool, e_sc, L, b - 1, own=w_pool)
                            g.tensor_tensor(GX[:, :, :], H2[:, :, :], GALL[:, bass.ds(b * QB, QB)].unsqueeze(2
                                            ).to_broadcast([P, QB, D]), ALU.mult).then_inc(e_gx.sem, 1)
                            wait(pool, e_gx, L, b, own=w_pool)
                        wait(pool, e_slot, L, b, own=w_pool)
                        for q in range(QB):
                            for k in range(1 if L else 2):
                                dst = xs1 if L else xs0
                                g.indirect_dma_start(dst[:, :], bass.IndirectOffsetOnAxis(SIDX[:, q, k:k + 1], 0),
                                                     GX[:, q, :] if L else H2[:, q, :], None,
                                                     bounds_check=(NEXP * (CAP if L else REGION)) - 1,
                                                     oob_is_err=False).then_inc(e_sc.sem, 16)

                def gather(b):
                    if isinstance(b, int) and b >= NB:
                        return
                    wait(pool, e_x2, L, b - 1, own=w_pool)
                    g.tensor_copy(GIS[:, :, :], GI0[:, bass.ds(b * QB, QB), :]).then_inc(e_gis.sem, 1)
                    wait(pool, e_gis, L, b, own=w_pool)
                    for q in range(QB):
                        for k in range(2):
                            g.indirect_dma_start(GY[:, q, k, :], None, ys0[:, :],
                                                 bass.IndirectOffsetOnAxis(GIS[:, q, k:k + 1], 0),
                                                 bounds_check=TILES0 * P - 1, oob_is_err=False
                                                 ).then_inc(e_gat.sem, 16)

                if L:
                    gather(0)
                steps(pool, step)

            layer(0)
            pool.wait_ge(s_tab, TAB_ALL)
            for r in range(4):
                pool.wait_ge(f_st[r], 16 * len(range(r, TILES0, 4)))
            layer(1)
            for r in range(2):
                pool.wait_ge(c_st[r], 16 * len(range(r, CHUNKS, 2)))
            for b in range(NB):
                if b >= 2:
                    pool.wait_ge(o_m, 2 * (b - 1))
                for q in range(QB):
                    g.indirect_dma_start(GY[:, q, b % 2, :], None, ys1[:, :],
                                         bass.IndirectOffsetOnAxis(GI1[:, QB * b + q:QB * b + q + 1], 0),
                                         bounds_check=NEXP * CAP - 1, oob_is_err=False).then_inc(o_g[b % 2], 16)


_INS = (["L0_attn_x", "L0_c", "L0_wmod", "L1_c", "L1_wmod", "L0_attn_scale", "L1_attn_subln_w"]
        + ["L0_attn_" + n for n in ("Wq", "bq", "Wk", "bk", "Wv", "bv", "Wo", "bo")]
        + ["L0_ffn_" + n for n in ("router_w", "w_fc", "b_fc", "w_proj", "b_proj")]
        + ["L1_attn_" + n for n in ("Wq", "Wk", "Wv", "Wo", "lambda_q1", "lambda_k1", "lambda_q2", "lambda_k2")]
        + ["L1_ffn_" + n for n in ("Wr", "br", "W1", "b1", "W2", "b2")])


def kernel(**inputs):
    import numpy as _np
    import concourse.bacc as _bacc
    from concourse import mybir as _mybir
    from concourse.bass_utils import run_bass_kernel_spmd as _run

    nc = _bacc.Bacc("TRN2", target_bir_lowering=False, num_devices=1)
    nb = inputs["L0_attn_x"].shape[0]
    arrays, ins = {}, {}
    for name in _INS + ["const"]:
        a = constants(nb) if name == "const" else _np.ascontiguousarray(inputs[name])
        arrays[f"in_{name}"] = a
        ins[name] = nc.dram_tensor(f"in_{name}", a.shape, _mybir.dt.from_np(a.dtype), kind="ExternalInput").ap()
    out = nc.dram_tensor("out_x", (nb, T, D), F32, kind="ExternalOutput").ap()
    build(nc, nb, ins, out)
    r = _run(nc, [arrays], core_ids=[0])
    return r.results[0]["out_x"]
```
